# Optimizing a Trainium2 kernel written in Bass

```python
import numpy as np
import jax
import jax.numpy as jnp

def _softmax(x, axis=-1):
    return jax.nn.softmax(x, axis=axis)

def _gelu(x):
    return jax.nn.gelu(x, approximate=True)

def _silu(x):
    return jax.nn.silu(x)

def _sigmoid(x):
    return jax.nn.sigmoid(x)

def _layernorm(x, axis=-1, eps=1e-05):
    m = jnp.mean(x, axis=axis, keepdims=True)
    v = jnp.var(x, axis=axis, keepdims=True)
    return (x - m) / jnp.sqrt(v + eps)

def _scatter_add(tgt, idx, src, axis=0):
    return tgt.at[idx].add(src)

def _segment_sum(src, seg, n):
    return jax.ops.segment_sum(src, seg, n)
kernel_name = 'mk_decoder_postln_d2_seqx_r4_977c6f'

def setup_inputs(seed: int=0):
    np.random.seed(seed)
    _w = jnp.asarray

    def _rec_inputs():
        import jax
        import jax.numpy as jnp
        _rk = jax.random.key(seed)
        x = -0.0003929 + 0.9999 * jax.random.normal(jax.random.fold_in(_rk, 1), (8, 256, 512), jnp.float32)
        _lenS = 256 - jax.random.randint(jax.random.fold_in(_rk, 7), (8,), 0, max(1, 256 // 4) + 1, jnp.int32)
        _lenS2 = 256 - jax.random.randint(jax.random.fold_in(_rk, 8), (8,), 0, max(1, 256 // 4) + 1, jnp.int32)
        _ctx_1024P = jax.random.normal(jax.random.fold_in(_rk, 11), (8, 16, 256), jnp.float32)
        _ctx_1024c = jax.random.dirichlet(jax.random.fold_in(_rk, 511), 0.3 * jnp.ones((16,), jnp.float32), (8, 256))
        _ctx_1024t = jnp.einsum('bsk,bkd->bsd', _ctx_1024c, _ctx_1024P)
        _ctx_1024t = _ctx_1024t * jax.lax.rsqrt(jnp.mean(jnp.square(_ctx_1024t)) + 1e-12) * 0.953939
        ctx_1024 = -0.000494167 + 1.00018 * (_ctx_1024t + 0.3 * jax.random.normal(jax.random.fold_in(_rk, 611), (8, 256, 256), jnp.float32))
        fside_BxSx2_0 = jax.random.uniform(jax.random.fold_in(_rk, 13), (8, 256, 2), jnp.float32, 0.0, 0.999707)
        _validS = jnp.arange(256)[None, :] < _lenS[:, None]
        _validS2 = jnp.arange(256)[None, :] < _lenS2[:, None]
        _causal = jnp.tril(jnp.ones((256, 256), dtype=bool))
        mask_BxS2_bf1 = jnp.ones((8, 256), dtype=bool)
        return (x, ctx_1024, fside_BxSx2_0, mask_BxS2_bf1)
    x, ctx_1024, fside_BxSx2_0, mask_BxS2_bf1 = _rec_inputs()

    def _L0_attn_setup():
        import jax, jax.numpy as jnp
        import numpy as np
        HQ, HKV, HD, WIN = (16, 4, 128, 128)

        def _sliding_window_attention(q, k, v, win):
            B, H, S, hd = q.shape
            W = win
            nb = S // W
            qb = q.reshape(B, H, nb, W, hd)
            kpad = jnp.pad(k, ((0, 0), (0, 0), (W, 0), (0, 0)))
            vpad = jnp.pad(v, ((0, 0), (0, 0), (W, 0), (0, 0)))
            kb = jnp.concatenate([kpad[:, :, :S].reshape(B, H, nb, W, hd), k.reshape(B, H, nb, W, hd)], axis=3)
            vb = jnp.concatenate([vpad[:, :, :S].reshape(B, H, nb, W, hd), v.reshape(B, H, nb, W, hd)], axis=3)
            scores = jnp.einsum('bhnqd,bhnkd->bhnqk', qb, kb) / jnp.asarray(hd, qb.dtype)
            qi = jnp.arange(W)[:, None]
            ki = jnp.arange(2 * W)[None, :]
            band = (ki >= qi + 1) & (ki <= qi + W)
            blk = jnp.arange(nb)[:, None, None]
            valid = band[None] & ((blk > 0) | (ki[None] >= W))
            neg = jnp.finfo(scores.dtype).min
            scores = jnp.where(valid[None, None], scores, neg)
            probs = jax.nn.softmax(scores, axis=-1)
            out = jnp.einsum('bhnqk,bhnkd->bhnqd', probs, vb)
            return out.reshape(B, H, S, hd)
        key = jax.random.key(seed)
        k0, k1, k2, k3, k4 = jax.random.split(key, 5)
        B, S, D = (1, 2048, 512)
        std = 0.02
        hidden_states = jax.random.normal(k0, (B, S, D), jnp.float32)
        Wq = jax.random.normal(k1, (D, HQ * HD), jnp.float32) * std
        Wk = jax.random.normal(k2, (D, HKV * HD), jnp.float32) * std
        Wv = jax.random.normal(k3, (D, HKV * HD), jnp.float32) * std
        Wo = jax.random.normal(k4, (HQ * HD, D), jnp.float32) * std
        return {'hidden_states': hidden_states, 'Wq': Wq, 'Wk': Wk, 'Wv': Wv, 'Wo': Wo}
    _L0_attn_all = _L0_attn_setup()
    _L0_attn_in = {k: v for k, v in _L0_attn_all.items() if k in ('Wq', 'Wk', 'Wv', 'Wo')}
    del _L0_attn_all

    def _L0_xattn_setup():
        import jax, jax.numpy as jnp
        import numpy as np
        N_HEADS = 16
        N_KV_HEADS = 8
        HEAD_DIM = 128
        D_TEXT = 512
        D_VISION = 256
        GROUPS = N_HEADS // N_KV_HEADS
        key = jax.random.key(seed)
        ks = jax.random.split(key, 6)
        B, T_text, T_vis = (4, 512, 144)
        text_hidden = jax.random.normal(ks[0], (B, T_text, D_TEXT), dtype=jnp.float32)
        vision_tokens = jax.random.normal(ks[1], (B, T_vis, D_VISION), dtype=jnp.float32)
        vision_mask = jnp.ones((B, T_vis), dtype=bool)
        s = 0.02
        Wq = jax.random.normal(ks[2], (D_TEXT, N_HEADS * HEAD_DIM), dtype=jnp.float32) * s
        Wk = jax.random.normal(ks[3], (D_VISION, N_KV_HEADS * HEAD_DIM), dtype=jnp.float32) * s
        Wv = jax.random.normal(ks[4], (D_VISION, N_KV_HEADS * HEAD_DIM), dtype=jnp.float32) * s
        Wo = jax.random.normal(ks[5], (N_HEADS * HEAD_DIM, D_TEXT), dtype=jnp.float32) * s
        return {'text_hidden': text_hidden, 'vision_tokens': vision_tokens, 'vision_mask': vision_mask, 'Wq': Wq, 'Wk': Wk, 'Wv': Wv, 'Wo': Wo}
    _L0_xattn_all = _L0_xattn_setup()
    _L0_xattn_in = {k: v for k, v in _L0_xattn_all.items() if k in ('Wq', 'Wk', 'Wv', 'Wo')}
    del _L0_xattn_all

    def _L0_ffn_setup():
        import jax, jax.numpy as jnp
        import numpy as np
        TOP_K = 2
        key = jax.random.key(seed)
        ks = jax.random.split(key, 7)
        B, S, H = (2, 512, 512)
        E, A, NS = (8, 64, 4096)
        x = jax.random.normal(ks[0], (B, S, H), jnp.float32)
        gate_w = jax.random.normal(ks[1], (E, H), jnp.float32) * 0.01
        W = jax.random.normal(ks[2], (H, H), jnp.float32) * 0.02
        atoms = jax.random.normal(ks[3], (A, NS), jnp.float32) * 0.02
        expert_atom_weights = jax.random.normal(ks[4], (E, A), jnp.float32) * 0.1
        importance = jax.random.normal(ks[5], (E, NS), jnp.float32) * 0.1
        mask_idx = jax.random.randint(ks[6], (NS,), 0, H * H, jnp.int32)
        return dict(x=x, gate_w=gate_w, W=W, atoms=atoms, expert_atom_weights=expert_atom_weights, importance=importance, mask_idx=mask_idx)
    _L0_ffn_all = _L0_ffn_setup()
    _L0_ffn_in = {k: v for k, v in _L0_ffn_all.items() if k in ('gate_w', 'W', 'atoms', 'expert_atom_weights', 'importance', 'mask_idx')}
    del _L0_ffn_all

    def _L1_attn_setup():
        import jax, jax.numpy as jnp
        import numpy as np
        B, T, D = (2, 512, 512)
        H, G = (32, 8)
        HD = D // H
        GROUP = H // G
        ROPE_BASE = 10000.0

        def _apply_rope(x):
            t = x.shape[2]
            half = HD // 2
            inv_freq = 1.0 / ROPE_BASE ** (jnp.arange(half, dtype=jnp.float32) * 2.0 / HD)
            ang = jnp.arange(t, dtype=jnp.float32)[:, None] * inv_freq[None, :]
            cos, sin = (jnp.cos(ang), jnp.sin(ang))
            x1, x2 = (x[..., :half], x[..., half:])
            out = jnp.concatenate([x1 * cos - x2 * sin, x2 * cos + x1 * sin], axis=-1)
            return out.astype(x.dtype)
        key = jax.random.key(seed)
        kx, kq, kk, kv, ko = jax.random.split(key, 5)
        scale = 0.02
        x = jax.random.normal(kx, (B, T, D), dtype=jnp.float32)
        Wq = jax.random.normal(kq, (D, D), dtype=jnp.float32) * scale
        Wk = jax.random.normal(kk, (D, G * HD), dtype=jnp.float32) * scale
        Wv = jax.random.normal(kv, (D, G * HD), dtype=jnp.float32) * scale
        Wo = jax.random.normal(ko, (D, D), dtype=jnp.float32) * scale
        return {'x': x, 'Wq': Wq, 'Wk': Wk, 'Wv': Wv, 'Wo': Wo}
    _L1_attn_all = _L1_attn_setup()
    _L1_attn_in = {k: v for k, v in _L1_attn_all.items() if k in ('Wq', 'Wk', 'Wv', 'Wo')}
    del _L1_attn_all

    def _L1_xattn_setup():
        import jax, jax.numpy as jnp
        import numpy as np
        DIM = 512
        CTX_DIM = 256
        N_HEADS = 32
        HEAD_DIM = DIM // N_HEADS
        POS_DIM = 2
        B, N, CTXN = (2, 512, 512)
        ROPE_BASE = 10000.0

        def apply_axial_rope(x, pos):
            b, n, h, d = x.shape
            p = pos.shape[-1]
            dpa = d // p
            half = dpa // 2
            freqs = ROPE_BASE ** (-jnp.arange(half, dtype=x.dtype) / half)
            ang = pos[..., :, None] * freqs
            cos = jnp.cos(ang)[:, :, None, :, :]
            sin = jnp.sin(ang)[:, :, None, :, :]
            xr = x.reshape(b, n, h, p, half, 2)
            x1, x2 = (xr[..., 0], xr[..., 1])
            out = jnp.stack([x1 * cos - x2 * sin, x1 * sin + x2 * cos], axis=-1)
            return out.reshape(b, n, h, d)
        key = jax.random.key(seed)
        ks = jax.random.split(key, 8)
        x = jax.random.normal(ks[0], (B, N, DIM), jnp.float32)
        ctx = jax.random.normal(ks[1], (B, CTXN, CTX_DIM), jnp.float32)
        pos_map = jax.random.uniform(ks[2], (B, N, POS_DIM), jnp.float32)
        ctx_pos_map = jax.random.uniform(ks[3], (B, CTXN, POS_DIM), jnp.float32)
        Wq = jax.random.normal(ks[4], (DIM, DIM), jnp.float32) / np.sqrt(DIM)
        Wkv = jax.random.normal(ks[5], (CTX_DIM, 2 * DIM), jnp.float32) / np.sqrt(CTX_DIM)
        Wout = jax.random.normal(ks[6], (DIM, DIM), jnp.float32) / np.sqrt(DIM)
        bout = jnp.zeros((DIM,), jnp.float32)
        return {'x': x, 'ctx': ctx, 'pos_map': pos_map, 'ctx_pos_map': ctx_pos_map, 'Wq': Wq, 'Wkv': Wkv, 'Wout': Wout, 'bout': bout}
    _L1_xattn_all = _L1_xattn_setup()
    _L1_xattn_in = {k: v for k, v in _L1_xattn_all.items() if k in ('Wq', 'Wkv', 'Wout', 'bout')}
    del _L1_xattn_all

    def _L1_ffn_setup():
        import jax, jax.numpy as jnp
        import numpy as np
        HIDDEN = 512
        INTER = 2048
        SCALE = 64.0

        def fwht(x):
            orig_shape = x.shape
            n = orig_shape[-1]
            x = x.reshape(-1, n)
            h = 1
            while h < n:
                x = x.reshape(-1, n // (2 * h), 2, h)
                a, b = (x[:, :, 0, :], x[:, :, 1, :])
                x = jnp.stack([a + b, a - b], axis=2).reshape(-1, n)
                h *= 2
            return (x / jnp.sqrt(jnp.asarray(n, x.dtype))).reshape(orig_shape)
        key = jax.random.key(seed)
        ks = jax.random.split(key, 8)
        inp = jax.random.normal(ks[0], (4, 512, HIDDEN), dtype=jnp.float32)
        SU_ug = jnp.where(jax.random.bernoulli(ks[1], 0.5, (HIDDEN,)), 1.0, -1.0).astype(jnp.float32)
        SU_dp = jnp.where(jax.random.bernoulli(ks[2], 0.5, (INTER,)), 1.0, -1.0).astype(jnp.float32)
        Wscale_ug = jax.random.uniform(ks[3], (2 * INTER,), jnp.float32, 0.5, 1.5)
        Wscale_dp = jax.random.uniform(ks[4], (HIDDEN,), jnp.float32, 0.5, 1.5)
        W_up = jax.random.normal(ks[5], (INTER, HIDDEN), dtype=jnp.float32) * 0.02
        W_gate = jax.random.normal(ks[6], (INTER, HIDDEN), dtype=jnp.float32) * 0.02
        W_down = jax.random.normal(ks[7], (HIDDEN, INTER), dtype=jnp.float32) * 0.02
        return {'input': inp, 'SU_ug': SU_ug, 'SU_dp': SU_dp, 'Wscale_ug': Wscale_ug, 'Wscale_dp': Wscale_dp, 'W_up': W_up, 'W_gate': W_gate, 'W_down': W_down}
    _L1_ffn_all = _L1_ffn_setup()
    _L1_ffn_in = {k: v for k, v in _L1_ffn_all.items() if k in ('SU_ug', 'SU_dp', 'Wscale_ug', 'Wscale_dp', 'W_up', 'W_gate', 'W_down')}
    del _L1_ffn_all
    return {'x': x, 'ctx_1024': ctx_1024, 'fside_BxSx2_0': fside_BxSx2_0, 'mask_BxS2_bf1': mask_BxS2_bf1, 'L0_attn_Wq': _L0_attn_in['Wq'], 'L0_attn_Wk': _L0_attn_in['Wk'], 'L0_attn_Wv': _L0_attn_in['Wv'], 'L0_attn_Wo': _L0_attn_in['Wo'], 'L0_xattn_Wq': _L0_xattn_in['Wq'], 'L0_xattn_Wk': _L0_xattn_in['Wk'], 'L0_xattn_Wv': _L0_xattn_in['Wv'], 'L0_xattn_Wo': _L0_xattn_in['Wo'], 'L0_ffn_gate_w': _L0_ffn_in['gate_w'], 'L0_ffn_W': _L0_ffn_in['W'], 'L0_ffn_atoms': _L0_ffn_in['atoms'], 'L0_ffn_expert_atom_weights': _L0_ffn_in['expert_atom_weights'], 'L0_ffn_importance': _L0_ffn_in['importance'], 'L0_ffn_mask_idx': _L0_ffn_in['mask_idx'], 'L1_attn_Wq': _L1_attn_in['Wq'], 'L1_attn_Wk': _L1_attn_in['Wk'], 'L1_attn_Wv': _L1_attn_in['Wv'], 'L1_attn_Wo': _L1_attn_in['Wo'], 'L1_xattn_Wq': _L1_xattn_in['Wq'], 'L1_xattn_Wkv': _L1_xattn_in['Wkv'], 'L1_xattn_Wout': _L1_xattn_in['Wout'], 'L1_xattn_bout': _L1_xattn_in['bout'], 'L1_ffn_SU_ug': _L1_ffn_in['SU_ug'], 'L1_ffn_SU_dp': _L1_ffn_in['SU_dp'], 'L1_ffn_Wscale_ug': _L1_ffn_in['Wscale_ug'], 'L1_ffn_Wscale_dp': _L1_ffn_in['Wscale_dp'], 'L1_ffn_W_up': _L1_ffn_in['W_up'], 'L1_ffn_W_gate': _L1_ffn_in['W_gate'], 'L1_ffn_W_down': _L1_ffn_in['W_down']}

def reference(x, ctx_1024, fside_BxSx2_0, mask_BxS2_bf1, L0_attn_Wq, L0_attn_Wk, L0_attn_Wv, L0_attn_Wo, L0_xattn_Wq, L0_xattn_Wk, L0_xattn_Wv, L0_xattn_Wo, L0_ffn_gate_w, L0_ffn_W, L0_ffn_atoms, L0_ffn_expert_atom_weights, L0_ffn_importance, L0_ffn_mask_idx, L1_attn_Wq, L1_attn_Wk, L1_attn_Wv, L1_attn_Wo, L1_xattn_Wq, L1_xattn_Wkv, L1_xattn_Wout, L1_xattn_bout, L1_ffn_SU_ug, L1_ffn_SU_dp, L1_ffn_Wscale_ug, L1_ffn_Wscale_dp, L1_ffn_W_up, L1_ffn_W_gate, L1_ffn_W_down):
    import jax
    import jax.numpy as jnp

    def _L0_attn_ref(hidden_states, Wq, Wk, Wv, Wo):
        import jax, jax.numpy as jnp
        import numpy as np
        HQ, HKV, HD, WIN = (16, 4, 128, 128)

        def _sliding_window_attention(q, k, v, win):
            B, H, S, hd = q.shape
            W = win
            nb = S // W
            qb = q.reshape(B, H, nb, W, hd)
            kpad = jnp.pad(k, ((0, 0), (0, 0), (W, 0), (0, 0)))
            vpad = jnp.pad(v, ((0, 0), (0, 0), (W, 0), (0, 0)))
            kb = jnp.concatenate([kpad[:, :, :S].reshape(B, H, nb, W, hd), k.reshape(B, H, nb, W, hd)], axis=3)
            vb = jnp.concatenate([vpad[:, :, :S].reshape(B, H, nb, W, hd), v.reshape(B, H, nb, W, hd)], axis=3)
            scores = jnp.einsum('bhnqd,bhnkd->bhnqk', qb, kb) / jnp.asarray(hd, qb.dtype)
            qi = jnp.arange(W)[:, None]
            ki = jnp.arange(2 * W)[None, :]
            band = (ki >= qi + 1) & (ki <= qi + W)
            blk = jnp.arange(nb)[:, None, None]
            valid = band[None] & ((blk > 0) | (ki[None] >= W))
            neg = jnp.finfo(scores.dtype).min
            scores = jnp.where(valid[None, None], scores, neg)
            probs = jax.nn.softmax(scores, axis=-1)
            out = jnp.einsum('bhnqk,bhnkd->bhnqd', probs, vb)
            return out.reshape(B, H, S, hd)
        B, S, D = hidden_states.shape
        q = (hidden_states @ Wq).reshape(B, S, HQ, HD).transpose(0, 2, 1, 3)
        k = (hidden_states @ Wk).reshape(B, S, HKV, HD).transpose(0, 2, 1, 3)
        v = (hidden_states @ Wv).reshape(B, S, HKV, HD).transpose(0, 2, 1, 3)
        rep = HQ // HKV
        k = jnp.repeat(k, rep, axis=1)
        v = jnp.repeat(v, rep, axis=1)
        attn = _sliding_window_attention(q, k, v, WIN)
        attn = attn.transpose(0, 2, 1, 3).reshape(B, S, HQ * HD)
        return attn @ Wo

    def _L0_xattn_ref(text_hidden, vision_tokens, vision_mask, Wq, Wk, Wv, Wo):
        import jax, jax.numpy as jnp
        import numpy as np
        N_HEADS = 16
        N_KV_HEADS = 8
        HEAD_DIM = 128
        D_TEXT = 512
        D_VISION = 256
        GROUPS = N_HEADS // N_KV_HEADS
        B, T_text, _ = text_hidden.shape
        T_vis = vision_tokens.shape[1]
        scale = jnp.float32(np.sqrt(HEAD_DIM))
        q = (text_hidden @ Wq).reshape(B, T_text, N_HEADS, HEAD_DIM).transpose(0, 2, 1, 3)
        k = (vision_tokens @ Wk).reshape(B, T_vis, N_KV_HEADS, HEAD_DIM).transpose(0, 2, 1, 3)
        v = (vision_tokens @ Wv).reshape(B, T_vis, N_KV_HEADS, HEAD_DIM).transpose(0, 2, 1, 3)
        k = jnp.repeat(k, GROUPS, axis=1)
        v = jnp.repeat(v, GROUPS, axis=1)
        scores = jnp.einsum('bhtd,bhsd->bhts', q, k) / scale
        mask = vision_mask[:, None, None, :]
        scores = jnp.where(mask, scores, -jnp.inf)
        attn = jax.nn.softmax(scores, axis=-1)
        attn = jnp.nan_to_num(attn, nan=0.0)
        out = jnp.einsum('bhts,bhsd->bhtd', attn, v)
        out = out.transpose(0, 2, 1, 3).reshape(B, T_text, N_HEADS * HEAD_DIM)
        return out @ Wo

    def _L0_ffn_ref(x, gate_w, W, atoms, expert_atom_weights, importance, mask_idx):
        import jax, jax.numpy as jnp
        import numpy as np
        TOP_K = 2
        B, S, H = x.shape
        xt = x.reshape(-1, H)
        logits = jnp.clip(xt @ gate_w.T, -50.0, 50.0)
        top_w, top_idx = jax.lax.top_k(logits, TOP_K)
        rw = jax.nn.softmax(top_w, axis=-1)
        deltas = jax.nn.softmax(expert_atom_weights, axis=-1) @ atoms
        weighted = deltas * jax.nn.sigmoid(importance)
        rows = mask_idx // H
        cols = mask_idx % H
        vals = jnp.einsum('tk,tks->ts', rw, weighted[top_idx])
        xg = xt[:, cols]
        contrib = jax.ops.segment_sum((xg * vals).T, rows, num_segments=H)
        out = xt @ W.T + contrib.T
        return out.reshape(B, S, H)

    def _L1_attn_ref(x, Wq, Wk, Wv, Wo):
        import jax, jax.numpy as jnp
        import numpy as np
        B, T, D = (2, 512, 512)
        H, G = (32, 8)
        HD = D // H
        GROUP = H // G
        ROPE_BASE = 10000.0

        def _apply_rope(x):
            t = x.shape[2]
            half = HD // 2
            inv_freq = 1.0 / ROPE_BASE ** (jnp.arange(half, dtype=jnp.float32) * 2.0 / HD)
            ang = jnp.arange(t, dtype=jnp.float32)[:, None] * inv_freq[None, :]
            cos, sin = (jnp.cos(ang), jnp.sin(ang))
            x1, x2 = (x[..., :half], x[..., half:])
            out = jnp.concatenate([x1 * cos - x2 * sin, x2 * cos + x1 * sin], axis=-1)
            return out.astype(x.dtype)
        b, t, _ = x.shape
        q = (x @ Wq).reshape(b, t, H, HD).transpose(0, 2, 1, 3)
        k = (x @ Wk).reshape(b, t, G, HD).transpose(0, 2, 1, 3)
        v = (x @ Wv).reshape(b, t, G, HD).transpose(0, 2, 1, 3)
        q = _apply_rope(q)
        k = _apply_rope(k)
        k = jnp.repeat(k, GROUP, axis=1)
        v = jnp.repeat(v, GROUP, axis=1)
        scores = jnp.einsum('bhqd,bhkd->bhqk', q, k)
        causal = jnp.triu(jnp.ones((t, t), dtype=bool), k=1)
        scores = jnp.where(causal, -jnp.inf, scores)
        attn = jax.nn.softmax(scores / jnp.sqrt(jnp.float32(HD)), axis=-1)
        ctx = jnp.einsum('bhqk,bhkd->bhqd', attn, v)
        ctx = jnp.swapaxes(ctx, -2, -1).reshape(b, t, D)
        return ctx @ Wo

    def _L1_xattn_ref(x, ctx, pos_map, ctx_pos_map, Wq, Wkv, Wout, bout):
        import jax, jax.numpy as jnp
        import numpy as np
        DIM = 512
        CTX_DIM = 256
        N_HEADS = 32
        HEAD_DIM = DIM // N_HEADS
        POS_DIM = 2
        B, N, CTXN = (2, 512, 512)
        ROPE_BASE = 10000.0

        def apply_axial_rope(x, pos):
            b, n, h, d = x.shape
            p = pos.shape[-1]
            dpa = d // p
            half = dpa // 2
            freqs = ROPE_BASE ** (-jnp.arange(half, dtype=x.dtype) / half)
            ang = pos[..., :, None] * freqs
            cos = jnp.cos(ang)[:, :, None, :, :]
            sin = jnp.sin(ang)[:, :, None, :, :]
            xr = x.reshape(b, n, h, p, half, 2)
            x1, x2 = (xr[..., 0], xr[..., 1])
            out = jnp.stack([x1 * cos - x2 * sin, x1 * sin + x2 * cos], axis=-1)
            return out.reshape(b, n, h, d)
        b, n, _ = x.shape
        ctx_n = ctx.shape[1]
        q = (x @ Wq).reshape(b, n, N_HEADS, HEAD_DIM)
        k, v = jnp.split(ctx @ Wkv, 2, axis=-1)
        k = k.reshape(b, ctx_n, N_HEADS, HEAD_DIM)
        v = v.reshape(b, ctx_n, N_HEADS, HEAD_DIM)
        q = apply_axial_rope(q, pos_map)
        k = apply_axial_rope(k, ctx_pos_map)
        scale = 1.0 / np.sqrt(HEAD_DIM).astype(np.float32)
        logits = jnp.einsum('bqhd,bkhd->bhqk', q, k) * scale
        w = jax.nn.softmax(logits, axis=-1)
        attn = jnp.einsum('bhqk,bkhd->bqhd', w, v)
        attn = attn.reshape(b, n, N_HEADS * HEAD_DIM)
        return attn @ Wout + bout

    def _L1_ffn_ref(input, SU_ug, SU_dp, Wscale_ug, Wscale_dp, W_up, W_gate, W_down):
        import jax, jax.numpy as jnp
        import numpy as np
        HIDDEN = 512
        INTER = 2048
        SCALE = 64.0

        def fwht(x):
            orig_shape = x.shape
            n = orig_shape[-1]
            x = x.reshape(-1, n)
            h = 1
            while h < n:
                x = x.reshape(-1, n // (2 * h), 2, h)
                a, b = (x[:, :, 0, :], x[:, :, 1, :])
                x = jnp.stack([a + b, a - b], axis=2).reshape(-1, n)
                h *= 2
            return (x / jnp.sqrt(jnp.asarray(n, x.dtype))).reshape(orig_shape)
        n = SU_ug.shape[0]
        x = input.reshape(-1, n)
        x = fwht(x * SU_ug) / SCALE
        x_up = x @ W_up.T * (Wscale_ug[:INTER] * SCALE)
        x_gate = x @ W_gate.T * (Wscale_ug[INTER:] * SCALE)
        x = jax.nn.silu(x_gate) * x_up
        x = fwht(x * SU_dp) / SCALE
        x = x @ W_down.T * (Wscale_dp * SCALE)
        return x.reshape(input.shape)
    x = _layernorm(x + _L0_attn_ref(x, L0_attn_Wq, L0_attn_Wk, L0_attn_Wv, L0_attn_Wo), axis=-1)
    x = _layernorm(x + _L0_xattn_ref(x, ctx_1024, mask_BxS2_bf1, L0_xattn_Wq, L0_xattn_Wk, L0_xattn_Wv, L0_xattn_Wo), axis=-1)
    x = _layernorm(x + _L0_ffn_ref(x, L0_ffn_gate_w, L0_ffn_W, L0_ffn_atoms, L0_ffn_expert_atom_weights, L0_ffn_importance, L0_ffn_mask_idx), axis=-1)
    x = _layernorm(x + _L1_attn_ref(x, L1_attn_Wq, L1_attn_Wk, L1_attn_Wv, L1_attn_Wo), axis=-1)
    x = _layernorm(x + _L1_xattn_ref(x, ctx_1024, fside_BxSx2_0, fside_BxSx2_0, L1_xattn_Wq, L1_xattn_Wkv, L1_xattn_Wout, L1_xattn_bout), axis=-1)
    x = _layernorm(x + _L1_ffn_ref(x, L1_ffn_SU_ug, L1_ffn_SU_dp, L1_ffn_Wscale_ug, L1_ffn_Wscale_dp, L1_ffn_W_up, L1_ffn_W_gate, L1_ffn_W_down), axis=-1)
    return x

_drawn_inputs = setup_inputs


def setup_inputs(seed=0):
    import zlib

    import numpy as np

    out = dict(_drawn_inputs(seed))
    spreads = {'L1_xattn_bout': (0.0, 0.1)}
    factors = {'L0_attn_Wq': 8.0,
     'L0_attn_Wk': 8.0,
     'L0_xattn_Wq': 8.0,
     'L0_xattn_Wk': 8.0,
     'L0_ffn_gate_w': 8.0,
     'L0_ffn_atoms': 8.0,
     'L0_ffn_expert_atom_weights': 8.0,
     'L0_ffn_importance': 36.61,
     'L1_attn_Wq': 8.0,
     'L1_attn_Wk': 8.0}
    for name, (base, spread) in spreads.items():
        noise = np.random.default_rng([zlib.crc32(name.encode()), seed]).standard_normal(out[name].shape)
        drawn = base * np.exp(spread * noise) if base else spread * noise
        out[name] = jnp.asarray(drawn.astype(out[name].dtype))
    for name, factor in factors.items():
        out[name] = (out[name] * factor).astype(out[name].dtype)
    return out
```

```python
import numpy as np
import concourse.bass as bass
from concourse import mybir
from contextlib import ExitStack

FP32 = mybir.dt.float32
INT32 = mybir.dt.int32
BF16 = mybir.dt.bfloat16
ALU = mybir.AluOpType
ACT = mybir.ActivationFunctionType
AX = mybir.AxisListType

P = 128
BATCH, SEQ, DIM = 8, 256, 512
TILES = SEQ // P
NTILE = BATCH * TILES
DC = DIM // P
CTX_DIM = 256
CC = CTX_DIM // P
EXPERTS, ATOMS, NSPARSE = 8, 64, 4096
LOW = -1e30
FLOOR = -3e38
EPS = 1e-5

C_ID, C_OWN, C_BAND, C_CAUSAL, C_HAD, C_NHAD, C_COS, C_SIN, C_FREQ, C_RANK, C_BEFORE, C_SPARE, C_OWN_T = (
    0, 128, 256, 512, 768, 896, 1024, 1056, 1088, 1096, 1112, 1240, 1241)
C_COLS = 1369


def constants():
    c = np.zeros((P, C_COLS), np.float32)
    i = np.arange(P)
    c[:, C_ID:C_ID + P] = np.eye(P)
    own = np.where(i[None, :] <= i[:, None], 0.0, LOW)
    prev = np.where(i[None, :] > i[:, None], 0.0, LOW)
    c[:, C_OWN:C_OWN + P] = own
    c[:, C_BAND:C_BAND + P] = prev
    c[:, C_BAND + P:C_BAND + 2 * P] = own
    c[:, C_CAUSAL + P:C_CAUSAL + 2 * P] = own
    h = np.ones((1, 1), np.float32)
    while h.shape[0] < P:
        h = np.block([[h, h], [h, -h]])
    c[:, C_HAD:C_HAD + P] = h
    c[:, C_NHAD:C_NHAD + P] = -h
    half = 8
    inv = (np.float32(1.0) / np.float32(10000.0) ** (np.arange(half, dtype=np.float32) * np.float32(2.0) / np.float32(16))).astype(np.float32)
    pos = np.arange(SEQ, dtype=np.float32).reshape(TILES, P)
    ang = (pos[:, :, None] * inv).astype(np.float32)
    cos, sin = np.cos(ang), np.sin(ang)
    for t in range(TILES):
        c[:, C_COS + 16 * t:C_COS + 16 * t + 16] = np.concatenate([cos[t], cos[t]], 1)
        c[:, C_SIN + 16 * t:C_SIN + 16 * t + 16] = np.concatenate([-sin[t], sin[t]], 1)
    c[:, C_FREQ:C_FREQ + 4] = (np.float32(10000.0) ** (-np.arange(4, dtype=np.float32) / np.float32(4))).astype(np.float32)
    c[:, C_RANK:C_RANK + TILES * EXPERTS] = np.tile(EXPERTS - np.arange(EXPERTS), TILES)
    c[:, C_BEFORE:C_BEFORE + P] = i[None, :] < i[:, None]
    c[:, C_OWN_T:C_OWN_T + P] = own.T
    c[:, C_SPARE] = DIM * DIM + i
    return c


class Chip:

    def __init__(self, nc, ctx):
        sb = lambda name, shape, dt=FP32: ctx.enter_context(nc.sbuf_tensor(name, shape, dt))
        self.nc = nc
        self.x = sb("x_all", [P, NTILE + TILES, DIM])
        self.const = sb("const", [P, C_COLS])
        self.ident = self.const[:, C_ID:C_ID + P]
        self.bank = [ctx.enter_context(nc.psum_tensor(f"bank{i}", [P, 512], FP32)) for i in range(8)]

    def sequence_buffers(self, ctx, tag):
        sb = lambda name, shape: ctx.enter_context(self.nc.sbuf_tensor(f"{name}_{tag}", shape, FP32))
        self.xs = sb("x_static", [P, TILES, DIM])
        self.xT = sb("xT", [P, DC, SEQ])
        self.res = sb("residual", [P, TILES, DIM])
        self.stat = sb("ln_stats", [P, TILES, 8])
        self.var, self.rstd, self.newton = (sb(n, [P, TILES]) for n in ("ln_var", "ln_rstd", "ln_newton"))


class Carve:

    def __init__(self, buf, size):
        self.buf, self.size, self.at = buf, size, 0

    def __call__(self, *shape):
        n = int(np.prod(shape))
        flat = self.buf[:, self.at:self.at + n]
        self.at += n
        assert self.at <= self.size, self.at
        names = "abcd"[:len(shape)]
        if len(shape) == 1:
            return flat
        return flat.rearrange(f"p ({' '.join(names)}) -> p {' '.join(names)}",
                              **{n_: s for n_, s in zip(names, shape)})


def clear_semaphores(nc, semaphores):
    with nc.Block() as block:
        @block.sync
        def _(sp):
            for sem in semaphores:
                sp.sem_clear(sem)


def setup(nc, chip, x_dram, const_dram):
    with ExitStack() as c:
        loaded = c.enter_context(nc.semaphore("x_loaded"))
        c.callback(clear_semaphores, nc, [loaded])
        block = c.enter_context(nc.Block())

        @block.sync
        def _(sp):
            sp.dma_start(chip.const[:, :], const_dram).then_inc(loaded, 16)
            x = x_dram.rearrange("b (t p) d -> p (b t) d", p=P)
            sp.dma_start(chip.x[:, 0:NTILE, :], x).then_inc(loaded, 16)
            sp.wait_ge(loaded, 32)

        @block.vector
        def _(dve):
            dve.memset(chip.x[:, NTILE:, :], 0.0)


def ln_vector(dve, chip, out_banks, batch, s, it):
    for t in range(TILES):
        last = dve.tensor_tensor(chip.res[:, t, :], out_banks[t][:, :],
                                 chip.x[:, bass.ds(batch * TILES + t, 1), :], ALU.add)
    last.then_inc(s["out_read"], 1)
    dve.drain()
    ln_rows(dve, chip, batch, s)


def rsqrt(dve, out, variance, var, newton):
    dve.tensor_scalar(var, variance, EPS, None, ALU.add)
    dve.drain()
    dve.tensor_scalar(out.bitcast(INT32), var.bitcast(INT32), -0.5, float(0x5F3759DF), ALU.mult, ALU.add)
    dve.drain()
    for _ in range(3):
        dve.tensor_tensor(newton, out, out, ALU.mult)
        dve.drain()
        dve.scalar_tensor_tensor(newton, newton, -0.5, var, ALU.mult, ALU.mult)
        dve.drain()
        dve.scalar_tensor_tensor(out, newton, 1.5, out, ALU.add, ALU.mult)
        dve.drain()


def ln_rows(dve, chip, batch, s):
    for t in range(TILES):
        dve.bn_stats(chip.stat[:, t, 0:6], chip.res[:, t, :])
    dve.drain()
    for t in range(TILES):
        dve.bn_aggr(chip.stat[:, t, 6:8], chip.stat[:, t, 0:6])
    dve.drain()
    rsqrt(dve, chip.rstd[:, :], chip.stat[:, :, 7], chip.var[:, :], chip.newton[:, :])
    for t in range(TILES):
        last = dve.tensor_scalar(chip.x[:, bass.ds(batch * TILES + t, 1), :], chip.res[:, t, :],
                                 chip.stat[:, t, 6:7], chip.rstd[:, t:t + 1], ALU.subtract, ALU.mult)
    last.then_inc(s["x_ready"], 1)



def attention_wide(nc, chip, wq_dram, wk_dram, wv_dram, wo_dram, groups, scale,
                   ctx_dram=None, mask_dram=None):
    H, HD = 16, 128
    cross = ctx_dram is not None
    KC = CC if cross else DC
    KVW = groups * HD
    PAIRS = H // 2
    NK, NV = groups // 2, TILES * KVW // 512
    NJ = NK + NV + PAIRS + 2 + (2 if cross else 0)
    assert NJ % 2 == 0
    SLOTS = 4
    tag = "x" if cross else "s"

    c = ExitStack()
    chip.sequence_buffers(c, tag)
    weights = c.enter_context(nc.sbuf_tensor(f"weights_{tag}", [P, 2 * KC * KVW + (DC * HD + DIM) * H], FP32))
    at = 0

    def region(chunks, width):
        nonlocal at
        r = weights[:, at:at + chunks * width].rearrange("p (c n) -> p c n", c=chunks)
        at += chunks * width
        return r

    wk, wv = region(KC, KVW), region(KC, KVW)
    wq, wo = region(DC, H * HD), region(H, DIM)
    carve = Carve(c.enter_context(nc.sbuf_tensor(f"work_{tag}", [P, 14848], FP32)), 14848)
    qT = carve(2, 512)
    kT = carve(groups, SEQ)
    v = carve(TILES, KVW)
    probs = carve(SLOTS, 2 * SEQ)
    probsT = carve(2, 2 * SEQ)
    oT = carve(H, SEQ)
    mx, neg, den, inv = carve(SLOTS, 2), carve(SLOTS, 2), carve(SLOTS, 2), carve(SLOTS, 2)
    tick = carve(1)
    if cross:
        ctx_sb, ctxT = carve(TILES, CTX_DIM), carve(CC, SEQ)
        mask8 = carve(BATCH * SEQ // 4).bitcast(mybir.dt.uint8)
        bias, maskcol8 = carve(SEQ), carve(BATCH * TILES // 4).bitcast(mybir.dt.uint8)
        maskcol = carve(BATCH * TILES)
        mc = carve(TILES)
    kv_src = ctxT if cross else chip.xT

    KEYS = [(0, 2), (0, 2)] if cross else [(0, 1), (0, 2)]
    COL = [0, 256]
    proj = chip.bank[0:2]
    score = chip.bank[2:4]
    trans = chip.bank[4]
    obank = chip.bank[5]
    out = chip.bank[6:8]

    with c:
        s = {n: c.enter_context(nc.semaphore(f"{n}_{tag}")) for n in (
            "wk_loaded", "wv_loaded", "wq_loaded", "wo_loaded", "xs_ready", "proj_ready", "proj_copied",
            "scores_ready", "masked", "exp_ready", "inv_ready", "probs_ready", "probsT_ready",
            "probsT_copied", "heads_ready", "heads_copied", "out_ready", "x_ready", "out_read", "ctx_loaded", "ctx_used", "mask_loaded", "bias_ready")}
        c.callback(clear_semaphores, nc, list(s.values()))
        block = c.enter_context(nc.Block())

        @block.sync
        def _(sp):
            if cross:
                sp.dma_start(mask8, mask_dram.rearrange("b s -> (b s)").partition_broadcast(P)).then_inc(s["mask_loaded"], 16)
                with nc.allow_non_contiguous_dma(reason="2048 mask bytes onto the partitions"):
                    sp.dma_start(maskcol8, mask_dram.rearrange("b (t p) -> p (b t)", p=P)).then_inc(s["mask_loaded"], 16)
            sp.dma_start(wk, wk_dram.rearrange("(c p) n -> p c n", p=P)).then_inc(s["wk_loaded"], 16)
            sp.dma_start(wv, wv_dram.rearrange("(c p) n -> p c n", p=P)).then_inc(s["wv_loaded"], 16)
            sp.dma_start(wq, wq_dram.rearrange("(c p) n -> p c n", p=P)).then_inc(s["wq_loaded"], 16)
            sp.dma_start(wo, wo_dram.rearrange("(c p) n -> p c n", p=P)).then_inc(s["wo_loaded"], 16)
            if cross:
                sp.dma_start(ctx_sb, ctx_dram[0, :, :].rearrange("(t p) d -> p t d", p=P)).then_inc(s["ctx_loaded"], 16)
                with sp.Fori(1, BATCH) as it:
                    sp.wait_ge(s["ctx_used"], it)
                    sp.dma_start(ctx_sb, ctx_dram[bass.ds(it, 1), :, :].rearrange("b (t p) d -> p (b t) d", p=P))\
                      .then_inc(s["ctx_loaded"], 16)
            sp.wait_ge(s["x_ready"], BATCH)

        @block.tensor
        def _(pe):
            def transpose_x():
                for j in range(2):
                    for i in range(4):
                        cc, t = 2 * j + i // 2, i % 2
                        last = pe.transpose(proj[j][:, 128 * i:128 * i + 128],
                                            chip.xs[:, t, cc * P:(cc + 1) * P], chip.ident)
                    last.then_inc(s["proj_ready"], 1)

            pe.wait_ge(s["xs_ready"], 1)
            transpose_x()
            for w in ("wk", "wv", "wq"):
                pe.wait_ge(s[f"{w}_loaded"], 16)
            with pe.Fori(0, BATCH) as it:
                j = 0

                def bank():
                    nonlocal j
                    pe.wait_ge(s["proj_copied"], it * NJ + j + 1)
                    j += 1
                    return proj[(j - 1) % 2]

                if cross:
                    pe.wait_ge(s["ctx_loaded"], it * 16 + 16)
                    for cc in range(CC):
                        b = bank()
                        for t in range(TILES):
                            last = pe.transpose(b[:, P * t:P * t + P], ctx_sb[:, t, cc * P:(cc + 1) * P], chip.ident)
                        last.then_inc(s["proj_ready"], 1)
                    pe.drain().then_inc(s["ctx_used"], 1)
                for n in range(NK):
                    b = bank()
                    if n == 0:
                        pe.wait_ge(s["proj_copied"], it * NJ + j + 1)
                    for i in range(2):
                        g = 2 * n + i
                        for cc in range(KC):
                            last = pe.matmul(b[:, i * SEQ:(i + 1) * SEQ], wk[:, cc, g * HD:(g + 1) * HD],
                                             kv_src[:, cc, :], start=(cc == 0), stop=(cc == KC - 1))
                    last.then_inc(s["proj_ready"], 1)
                for n in range(NV):
                    b = bank()
                    t, col = n % TILES, n // TILES * 512
                    for cc in range(KC):
                        last = pe.matmul(b[:, :], kv_src[:, cc, t * P:(t + 1) * P], wv[:, cc, col:col + 512],
                                         start=(cc == 0), stop=(cc == KC - 1))
                    last.then_inc(s["proj_ready"], 1)

                def query(pair):
                    b = bank()
                    for i in range(2):
                        h = 2 * pair + i
                        for cc in range(DC):
                            last = pe.matmul(b[:, i * SEQ:(i + 1) * SEQ], wq[:, cc, h * HD:(h + 1) * HD],
                                             chip.xT[:, cc, :], start=(cc == 0), stop=(cc == DC - 1))
                    last.then_inc(s["proj_ready"], 1)

                def scores(h):
                    pe.wait_ge(s["proj_copied"], it * NJ + (NJ - 2 - PAIRS) + h // 2 + 3)
                    if h >= 2:
                        pe.wait_ge(s["masked"], it * H + h - 1)
                    g = h * groups // H
                    for t, (k0, nk) in enumerate(KEYS):
                        q = qT[:, h // 2 % 2, (h % 2) * SEQ + t * P:(h % 2) * SEQ + (t + 1) * P]
                        last = pe.matmul(score[h % 2][:, COL[t]:COL[t] + nk * P], q, kT[:, g, k0 * P:(k0 + nk) * P],
                                         start=True, stop=True)
                    last.then_inc(s["scores_ready"], 1)

                def turn(h):
                    pe.wait_ge(s["probs_ready"], it * H + h + 1)
                    if h >= 1:
                        pe.wait_ge(s["probsT_copied"], it * H + h)
                    for t, (k0, nk) in enumerate(KEYS):
                        for k in range(nk):
                            last = pe.transpose(trans[:, k * SEQ + t * P:k * SEQ + (t + 1) * P],
                                                probs[:, h % SLOTS, COL[t] + k * P:COL[t] + (k + 1) * P], chip.ident)
                    last.then_inc(s["probsT_ready"], 1)

                def values(h):
                    pe.wait_ge(s["probsT_copied"], it * H + h + 1)
                    if h >= 1:
                        pe.wait_ge(s["heads_copied"], it * H + h)
                    g = h * groups // H
                    for k in range(TILES):
                        q0 = 0 if cross else k * P
                        last = pe.matmul(obank[:, (h % 2) * SEQ + q0:(h % 2 + 1) * SEQ], v[:, k, g * HD:(g + 1) * HD],
                                         probsT[:, h % 2, k * SEQ + q0:(k + 1) * SEQ],
                                         start=(k == 0), stop=(k == TILES - 1), skip_group_check=True)
                    last.then_inc(s["heads_ready"], 1)

                def output(h0, h1):
                    if h0 == 0:
                        pe.wait_ge(s["wo_loaded"], 16)
                    pe.wait_ge(s["heads_copied"], it * H + h1)
                    for t in range(TILES):
                        for h in range(h0, h1):
                            last = pe.matmul(out[t][:, :], oT[:, h, t * P:(t + 1) * P], wo[:, h, :],
                                             start=(h == 0), stop=(h == H - 1), skip_group_check=True)
                    if h1 == H:
                        last.then_inc(s["out_ready"], 1)

                for step in range(H + 4):
                    if step < H and step % 2 == 0:
                        query(step // 2)
                    if 1 <= step <= H:
                        scores(step - 1)
                    if step == H:
                        pe.wait_ge(s["xs_ready"], it + 2)
                        pe.wait_ge(s["proj_copied"], it * NJ + NJ)
                        transpose_x()
                        j += 2
                        output(0, 6)
                    if 3 <= step < H + 3:
                        turn(step - 3)
                    if step >= 4:
                        values(step - 4)
                    if step == H + 1:
                        output(6, 12)
                output(12, H)
                assert j == NJ

        @block.scalar
        def _(act):
            copy = lambda dst, src: act.activation(dst, src, ACT.Copy)
            xt_half = lambda i: chip.xT[:, 2 * i:2 * i + 2, :].rearrange("p c q -> p (c q)")
            copy(chip.xs[:, :, :], chip.x[:, 0:TILES, :]).then_inc(s["xs_ready"], 1)
            for i in range(2):
                act.wait_ge(s["proj_ready"], i + 1)
                copy(xt_half(i), proj[i][:, :]).then_inc(s["proj_copied"], 1)
            with act.Fori(0, BATCH) as it:
                j = 0

                def evacuate(dst, cols=512):
                    nonlocal j
                    act.wait_ge(s["proj_ready"], it * NJ + j + 3)
                    copy(dst, proj[j % 2][:, 0:cols]).then_inc(s["proj_copied"], 1)
                    j += 1

                if cross:
                    for cc in range(CC):
                        evacuate(ctxT[:, cc, :], SEQ)
                for n in range(NK):
                    evacuate(kT[:, 2 * n:2 * n + 2, :].rearrange("p g q -> p (g q)"))
                for n in range(NV):
                    t, col = n % TILES, n // TILES * 512
                    if cross:
                        if n == 0:
                            act.wait_ge(s["bias_ready"], it + 1)
                        act.wait_ge(s["proj_ready"], it * NJ + j + 3)
                        act.activation(v[:, t, col:col + 512], proj[j % 2][:, :], ACT.Copy, scale=mc[:, t:t + 1])\
                           .then_inc(s["proj_copied"], 1)
                        j += 1
                    else:
                        evacuate(v[:, t, col:col + 512])
                for step in range(H + 4):
                    if step < H and step % 2 == 0:
                        evacuate(qT[:, step // 2 % 2, :])
                    if 1 <= step <= H:
                        h = step - 1
                        act.wait_ge(s["masked"], it * H + h + 1)
                        for t, (k0, nk) in enumerate(KEYS):
                            pr = probs[:, h % SLOTS, COL[t]:COL[t] + nk * P]
                            last = act.activation(pr, pr, ACT.Exp, bias=neg[:, h % SLOTS, t:t + 1],
                                                  accum_out=den[:, h % SLOTS, t:t + 1])
                        last.then_inc(s["exp_ready"], 1)
                    if step == H // 2:
                        copy(chip.xs[:, :, :], chip.x[:, bass.ds(it * TILES + TILES, TILES), :]).then_inc(s["xs_ready"], 1)
                    if step == H:
                        for i in range(2):
                            evacuate(xt_half(i))
                    if step >= 4:
                        h = step - 4
                        act.wait_ge(s["heads_ready"], it * H + h + 1)
                        copy(oT[:, h, :], obank[:, (h % 2) * SEQ:(h % 2 + 1) * SEQ]).then_inc(s["heads_copied"], 1)

        @block.vector
        def _(dve):
            if cross:
                dve.wait_ge(s["mask_loaded"], 32)
                dve.tensor_copy(maskcol, maskcol8)
                dve.drain()
            with dve.Fori(0, BATCH) as it:
                if cross:
                    dve.tensor_copy(mc, maskcol[:, bass.ds(it * TILES, TILES)])
                    dve.tensor_copy(bias, mask8[:, bass.ds(it * SEQ, SEQ)])
                    dve.drain()
                    dve.tensor_scalar(bias, bias, 1.0, -LOW, ALU.subtract, ALU.mult).then_inc(s["bias_ready"], 1)
                    dve.drain()
                for step in range(H + 3):
                    if step < H:
                        h = step
                        dve.wait_ge(s["scores_ready"], it * H + h + 1)
                        dve.memset(tick, 0.0)
                        for t, (k0, nk) in enumerate(KEYS):
                            if cross:
                                hide = bias
                            else:
                                at_ = C_OWN if t == 0 else C_BAND
                                hide = chip.const[:, at_:at_ + nk * P]
                            dve.tensor_tensor_reduce(
                                out=probs[:, h % SLOTS, COL[t]:COL[t] + nk * P],
                                in0=score[h % 2][:, COL[t]:COL[t] + nk * P], in1=hide, scale=scale,
                                scalar=FLOOR, op0=ALU.add, op1=ALU.max, accum_out=mx[:, h % SLOTS, t:t + 1])
                        dve.drain()
                        dve.tensor_scalar(neg[:, h % SLOTS, :], mx[:, h % SLOTS, :], -1.0, None, ALU.mult)\
                           .then_inc(s["masked"], 1)
                    if 1 <= step <= H:
                        h = step - 1
                        dve.wait_ge(s["exp_ready"], it * H + h + 1)
                        dve.reciprocal(inv[:, h % SLOTS, :], den[:, h % SLOTS, :]).then_inc(s["inv_ready"], 1)
                    if step >= 3:
                        h = step - 3
                        dve.wait_ge(s["probsT_ready"], it * H + h + 1)
                        if cross:
                            dve.tensor_copy(probsT[:, h % 2, :], trans[:, :]).then_inc(s["probsT_copied"], 1)
                        else:
                            dve.tensor_copy(probsT[:, h % 2, 0:SEQ], trans[:, 0:SEQ])
                            dve.tensor_copy(probsT[:, h % 2, SEQ + P:], trans[:, SEQ + P:])\
                               .then_inc(s["probsT_copied"], 1)
                dve.wait_ge(s["out_ready"], it + 1)
                ln_vector(dve, chip, out, it, s, it)

        @block.gpsimd
        def _(pool):
            with pool.Fori(0, BATCH) as it:
                for h in range(H):
                    pool.wait_ge(s["inv_ready"], it * H + h + 1)
                    for t, (k0, nk) in enumerate(KEYS):
                        pr = probs[:, h % SLOTS, COL[t]:COL[t] + nk * P]
                        last = pool.tensor_tensor(pr, pr, inv[:, h % SLOTS, t:t + 1].to_broadcast([P, nk * P]), ALU.mult)
                    last.then_inc(s["probs_ready"], 1)

def expert_table(nc, chip, table, atoms_dram, mix_dram, importance_dram, index_dram):
    SETS = NSPARSE // P
    c = ExitStack()
    big = c.enter_context(nc.sbuf_tensor("expert_big", [P, 20480], FP32))
    carve = Carve(c.enter_context(nc.sbuf_tensor("expert_work", [P, 4096], FP32)), 4096)
    zero = big[:, 0:4096]
    atoms = big[0:ATOMS, 4096:4096 + NSPARSE]
    importance = big[0:EXPERTS, 8192:8192 + NSPARSE]
    same = big[:, 12288:12288 + SETS * P].rearrange("p (i s) -> p i s", i=SETS)
    mix = carve(ATOMS)[0:EXPERTS]
    mixT = carve(EXPERTS)[0:ATOMS]
    mstat = carve(4)[0:EXPERTS]
    index, col, row = carve(SETS).bitcast(INT32), carve(SETS).bitcast(INT32), carve(SETS).bitcast(INT32)
    indexf, colf, rowf, dest = carve(SETS), carve(SETS), carve(SETS), carve(SETS)
    dest_int = carve(SETS).bitcast(INT32)
    before = carve(SETS)
    earlier = big[:, 16384:16384 + SETS * P].rearrange("p (i s) -> p i s", i=SETS)
    weighted, summed = carve(SETS, EXPERTS), carve(SETS, EXPERTS)
    gate = carve(SETS, EXPERTS)
    ROWS = DIM * DIM + P
    flat = lambda a: a.rearrange("p a b -> p (a b)")

    with c:
        s = {n: c.enter_context(nc.semaphore(f"{n}_e")) for n in (
            "zeros_ready", "table_clear", "mix_loaded", "atoms_loaded", "importance_loaded", "index_loaded",
            "mix_max", "mix_exp", "mix_ready", "mixT_ready", "mixT_copied", "deltas_ready", "imp_ready",
            "imp_exp", "weighted_ready", "index_ready", "row_ready", "same_ready", "sums_ready",
            "summed_ready", "set_added")}
        block = c.enter_context(nc.Block())

        @block.sync
        def _(sp):
            sp.dma_start(mix, mix_dram).then_inc(s["mix_loaded"], 16)
            sp.dma_start(index, index_dram.rearrange("(p i) -> p i", i=SETS)).then_inc(s["index_loaded"], 16)
            sp.dma_start(importance, importance_dram).then_inc(s["importance_loaded"], 16)
            sp.dma_start(atoms, atoms_dram).then_inc(s["atoms_loaded"], 16)
            sp.wait_ge(s["zeros_ready"], 1)
            part = DIM * DIM // 4
            for i in range(4):
                sp.dma_start(table[i * part:(i + 1) * part, :].rearrange("(p n) e -> p (n e)", p=P), zero)\
                  .then_inc(s["table_clear"], 16)
            sp.dma_start(table[4 * part:ROWS, :], zero[:, 0:EXPERTS]).then_inc(s["table_clear"], 16)
            sp.wait_ge(s["table_clear"], 80)

        @block.tensor
        def _(pe):
            ident8 = chip.const[0:EXPERTS, C_ID:C_ID + EXPERTS]
            pe.wait_ge(s["mix_ready"], 1)
            pe.transpose(chip.bank[0][0:ATOMS, 0:EXPERTS], mix, ident8).then_inc(s["mixT_ready"], 1)
            pe.wait_ge(s["importance_loaded"], 16)
            for i in range(SETS):
                last = pe.transpose(chip.bank[1][:, EXPERTS * i:EXPERTS * (i + 1)],
                                    importance[:, i::SETS], ident8)
            last.then_inc(s["imp_ready"], 1)
            pe.wait_ge(s["mixT_copied"], 1)
            pe.wait_ge(s["atoms_loaded"], 16)
            for i in range(SETS):
                last = pe.matmul(chip.bank[2][:, EXPERTS * i:EXPERTS * (i + 1)], atoms[:, i::SETS], mixT,
                                 start=True, stop=True)
            last.then_inc(s["deltas_ready"], 1)
            pe.wait_ge(s["index_ready"], 1)
            for n in range(SETS // 4):
                if n >= 2:
                    pe.wait_ge(s["same_ready"], 4 * (n - 1))
                for i in range(4 * n, 4 * n + 4):
                    last = pe.matmul(chip.bank[3 + n % 2][:, P * (i % 4):P * (i % 4 + 1)],
                                     indexf[:, i:i + 1].to_broadcast([P, P]), chip.ident, start=True, stop=True)
                last.then_inc(s["row_ready"], 1)
            pe.wait_ge(s["same_ready"], SETS)
            pe.wait_ge(s["weighted_ready"], 1)
            for i in range(SETS):
                last = pe.matmul(chip.bank[5][:, EXPERTS * i:EXPERTS * (i + 1)], same[:, i, :], weighted[:, i, :],
                                 start=True, stop=True)
            last.then_inc(s["sums_ready"], 1)

        @block.scalar
        def _(act):
            act.wait_ge(s["mix_max"], 1)
            act.activation(mix, mix, ACT.Exp, bias=mstat[:, 1:2], accum_out=mstat[:, 2:3]).then_inc(s["mix_exp"], 1)
            act.wait_ge(s["imp_ready"], 1)
            act.activation(flat(gate), chip.bank[1][:, 0:SETS * EXPERTS], ACT.Exp, scale=-1.0)\
               .then_inc(s["imp_exp"], 1)

        @block.vector
        def _(dve):
            dve.memset(zero, 0.0).then_inc(s["zeros_ready"], 1)
            dve.wait_ge(s["mix_loaded"], 16)
            dve.tensor_reduce(mstat[:, 0:1], mix, AX.X, ALU.max)
            dve.drain()
            dve.tensor_scalar(mstat[:, 1:2], mstat[:, 0:1], -1.0, None, ALU.mult).then_inc(s["mix_max"], 1)
            dve.wait_ge(s["mix_exp"], 1)
            dve.reciprocal(mstat[:, 3:4], mstat[:, 2:3])
            dve.drain()
            dve.tensor_scalar(mix, mix, mstat[:, 3:4], None, ALU.mult).then_inc(s["mix_ready"], 1)
            dve.wait_ge(s["index_loaded"], 16)
            dve.tensor_copy(indexf, index)
            dve.tensor_scalar(col, index, DIM - 1, None, ALU.bitwise_and)
            dve.tensor_scalar(row, index, DIM.bit_length() - 1, None, ALU.logical_shift_right)
            dve.drain().then_inc(s["index_ready"], 1)
            dve.tensor_copy(colf, col)
            dve.tensor_copy(rowf, row)
            dve.drain()
            dve.scalar_tensor_tensor(dest, colf, float(DIM), rowf, ALU.mult, ALU.add)
            dve.wait_ge(s["mixT_ready"], 1)
            dve.tensor_copy(mixT, chip.bank[0][0:ATOMS, 0:EXPERTS]).then_inc(s["mixT_copied"], 1)
            dve.wait_ge(s["imp_exp"], 1)
            dve.tensor_scalar(flat(gate), flat(gate), 1.0, None, ALU.add)
            dve.drain()
            dve.reciprocal(flat(gate), flat(gate))
            dve.drain()
            dve.wait_ge(s["deltas_ready"], 1)
            dve.tensor_tensor(flat(weighted), chip.bank[2][:, 0:SETS * EXPERTS], flat(gate), ALU.mult)\
               .then_inc(s["weighted_ready"], 1)
            for i in range(SETS):
                if i % 4 == 0:
                    dve.wait_ge(s["row_ready"], i // 4 + 1)
                dve.tensor_scalar(same[:, i, :], chip.bank[3 + i // 4 % 2][:, P * (i % 4):P * (i % 4 + 1)],
                                  indexf[:, i:i + 1], None, ALU.is_equal).then_inc(s["same_ready"], 1)
            dve.drain()
            dve.tensor_tensor(earlier, same, chip.const[:, C_BEFORE:C_BEFORE + P].unsqueeze(1)
                              .to_broadcast([P, SETS, P]), ALU.mult)
            dve.drain()
            dve.tensor_reduce(before, earlier, AX.X, ALU.add)
            dve.drain()
            dve.tensor_scalar(before, before, 0.0, None, ALU.is_gt)
            dve.tensor_scalar(colf, dest, -1.0, chip.const[:, C_SPARE:C_SPARE + 1], ALU.mult, ALU.add)
            dve.drain()
            dve.tensor_tensor(colf, colf, before, ALU.mult)
            dve.drain()
            dve.tensor_tensor(dest, dest, colf, ALU.add)
            dve.drain()
            dve.tensor_copy(dest_int, dest)
            dve.wait_ge(s["sums_ready"], 1)
            dve.tensor_copy(flat(summed), chip.bank[5][:, 0:SETS * EXPERTS])
            dve.drain().then_inc(s["summed_ready"], 1)

        @block.gpsimd
        def _(pool):
            pool.wait_ge(s["table_clear"], 80)
            pool.wait_ge(s["summed_ready"], 1)
            for i in range(SETS):
                pool.indirect_dma_start(
                    out=table, out_offset=bass.IndirectOffsetOnAxis(ap=dest_int[:, i:i + 1].bitcast(mybir.dt.uint32), axis=0),
                    in_=summed[:, i, :], in_offset=None, compute_op=ALU.add).then_inc(s["set_added"], 16)
                pool.wait_ge(s["set_added"], 16 * (i + 1))


def experts(nc, chip, table, gate_dram, w_dram):
    c = ExitStack()
    chip.sequence_buffers(c, "m")
    weights = c.enter_context(nc.sbuf_tensor("weights_m", [P, 24576], FP32))
    WT = weights[:, 0:DC * DIM].rearrange("p (c r) -> p c r", c=DC)
    at = DC * DIM
    M = weights[:, at:at + DC * EXPERTS * DIM].rearrange("p (c e r) -> p c e r", c=DC, e=EXPERTS)
    at += DC * EXPERTS * DIM
    stage = weights[:, at:at + EXPERTS * DIM]
    carve = Carve(c.enter_context(nc.sbuf_tensor("work_m", [P, 5120], FP32)), 5120)
    w_rows = carve(DC, DIM)
    gate_rows = carve(DIM)[0:EXPERTS]
    gateT = carve(DC, EXPERTS)
    xg = carve(2, DC, SEQ)
    logit, low, key, one, two, g = (carve(TILES, EXPERTS) for _ in range(6))
    m1, m2, k1, k2, d, r, dr = (carve(TILES) for _ in range(7))
    rank = chip.const[:, C_RANK:C_RANK + TILES * EXPERTS].rearrange("p (t e) -> p t e", t=TILES)
    logits_bank, gates_bank, turn_bank, out = chip.bank[0], chip.bank[1:3], chip.bank[4:6], chip.bank[6:8]
    wide = lambda a: a.unsqueeze(2).to_broadcast([P, TILES, EXPERTS])

    with c:
        s = {n: c.enter_context(nc.semaphore(f"{n}_m")) for n in (
            "w_loaded", "gate_loaded", "chunk_loaded", "chunk_used", "chunk_used2", "wT_ready", "wT_copied", "xs_ready",
            "xT_ready", "xT_copied", "logits_ready", "margin_ready", "exp_ready", "gates_ready",
            "spread_ready", "scaled", "expert_done", "out_ready", "x_ready", "out_read")}
        block = c.enter_context(nc.Block())

        @block.sync
        def _(sp):
            sp.dma_start(w_rows, w_dram.rearrange("(c p) n -> p c n", p=P)).then_inc(s["w_loaded"], 16)
            sp.dma_start(gate_rows, gate_dram).then_inc(s["gate_loaded"], 16)
            for cc in range(DC):
                if cc >= 1:
                    sp.wait_ge(s["chunk_used"], cc)
                    sp.wait_ge(s["chunk_used2"], cc)
                sp.dma_start(stage, table[cc * P * DIM:(cc + 1) * P * DIM, :].rearrange("(p r) e -> p (r e)", p=P))\
                  .then_inc(s["chunk_loaded"], 16)
            sp.wait_ge(s["x_ready"], BATCH)

        @block.tensor
        def _(pe):
            def transpose_x():
                for j in range(2):
                    for i in range(4):
                        cc, t = 2 * j + i // 2, i % 2
                        last = pe.transpose(turn_bank[j][:, P * i:P * i + P],
                                            chip.xs[:, t, cc * P:(cc + 1) * P], chip.ident)
                    last.then_inc(s["xT_ready"], 1)

            pe.wait_ge(s["w_loaded"], 16)
            for cc in range(DC):
                if cc >= 2:
                    pe.wait_ge(s["wT_copied"], cc - 1)
                for ro in range(DC):
                    last = pe.transpose(turn_bank[cc % 2][:, P * ro:P * (ro + 1)],
                                        w_rows[:, ro, cc * P:(cc + 1) * P], chip.ident)
                last.then_inc(s["wT_ready"], 1)
            pe.wait_ge(s["gate_loaded"], 16)
            for cc in range(DC):
                last = pe.transpose(logits_bank[:, EXPERTS * cc:EXPERTS * (cc + 1)], gate_rows[:, cc * P:(cc + 1) * P],
                                    chip.const[0:EXPERTS, C_ID:C_ID + EXPERTS])
            last.then_inc(s["wT_ready"], 1)
            pe.wait_ge(s["xs_ready"], 1)
            pe.wait_ge(s["wT_copied"], DC + 1)
            transpose_x()
            pe.wait_ge(s["chunk_used"], DC)
            pe.wait_ge(s["chunk_used2"], DC)
            with pe.Fori(0, BATCH) as it:
                pe.wait_ge(s["xT_copied"], 2 * it + 2)
                for t in range(TILES):
                    for cc in range(DC):
                        last = pe.matmul(logits_bank[:, EXPERTS * t:EXPERTS * (t + 1)], chip.xT[:, cc, t * P:(t + 1) * P],
                                         gateT[:, cc, :], start=(cc == 0), stop=(cc == DC - 1))
                last.then_inc(s["logits_ready"], 1)
                pe.wait_ge(s["out_read"], it + 1)
                for t in range(TILES):
                    for cc in range(DC):
                        pe.matmul(out[t][:, :], chip.xT[:, cc, t * P:(t + 1) * P], WT[:, cc, :],
                                  start=(cc == 0), stop=False, skip_group_check=True)

                def spread(e):
                    if e >= 2:
                        pe.wait_ge(s["scaled"], it * EXPERTS + e - 1)
                    for t in range(TILES):
                        last = pe.matmul(gates_bank[e % 2][:, P * t:P * (t + 1)],
                                         g[:, t, e:e + 1].to_broadcast([P, P]), chip.ident, start=True, stop=True)
                    last.then_inc(s["spread_ready"], 1)

                pe.wait_ge(s["gates_ready"], it + 1)
                spread(0)
                spread(1)
                for e in range(EXPERTS):
                    pe.wait_ge(s["scaled"], it * EXPERTS + e + 1)
                    for t in range(TILES):
                        for cc in range(DC):
                            last = pe.matmul(out[t][:, :], xg[:, e % 2, cc, t * P:(t + 1) * P], M[:, cc, e, :],
                                             start=False, stop=(e == EXPERTS - 1 and cc == DC - 1),
                                             skip_group_check=True)
                    last.then_inc(s["expert_done"], 1)
                    if e + 2 < EXPERTS:
                        spread(e + 2)
                    if e == EXPERTS - 3:
                        pe.wait_ge(s["xs_ready"], it + 2)
                        transpose_x()

        @block.scalar
        def _(act):
            copy = lambda dst, src: act.activation(dst, src, ACT.Copy)
            copy(chip.xs[:, :, :], chip.x[:, 0:TILES, :]).then_inc(s["xs_ready"], 1)
            for cc in range(DC):
                act.wait_ge(s["wT_ready"], cc + 1)
                copy(WT[:, cc, :], turn_bank[cc % 2][:, :]).then_inc(s["wT_copied"], 1)
            act.wait_ge(s["wT_ready"], DC + 1)
            copy(gateT.rearrange("p c e -> p (c e)"), logits_bank[:, 0:DC * EXPERTS]).then_inc(s["wT_copied"], 1)
            for cc in range(DC):
                act.wait_ge(s["chunk_loaded"], 16 * (cc + 1))
                copy(M[:, cc, :, DIM // 2:], stage.rearrange("p (r e) -> p e r", e=EXPERTS)[:, :, DIM // 2:])\
                    .then_inc(s["chunk_used"], 1)
            for j in range(2):
                act.wait_ge(s["xT_ready"], j + 1)
                copy(chip.xT[:, 2 * j:2 * j + 2, :].rearrange("p c q -> p (c q)"), turn_bank[j][:, :])\
                    .then_inc(s["xT_copied"], 1)
            with act.Fori(0, BATCH) as it:
                act.wait_ge(s["margin_ready"], it + 1)
                act.activation(d, d, ACT.Exp).then_inc(s["exp_ready"], 1)
                copy(chip.xs[:, :, :], chip.x[:, bass.ds(it * TILES + TILES, TILES), :]).then_inc(s["xs_ready"], 1)
                act.wait_ge(s["scaled"], it * EXPERTS + EXPERTS)
                for j in range(2):
                    act.wait_ge(s["xT_ready"], it * 2 + j + 3)
                    copy(chip.xT[:, 2 * j:2 * j + 2, :].rearrange("p c q -> p (c q)"), turn_bank[j][:, :])\
                        .then_inc(s["xT_copied"], 1)

        @block.vector
        def _(dve):
            dve.drain().then_inc(s["out_read"], 1)
            with dve.Fori(0, BATCH) as it:
                dve.wait_ge(s["logits_ready"], it + 1)
                dve.tensor_scalar(logit, logits_bank[:, 0:TILES * EXPERTS].rearrange("p (t e) -> p t e", t=TILES),
                                  -50.0, 50.0, ALU.max, ALU.min)
                dve.drain()

                def pick(values, top, rank_top, chosen):
                    dve.tensor_reduce(top, values, AX.X, ALU.max)
                    dve.drain()
                    dve.tensor_tensor(key, values, wide(top), ALU.is_equal)
                    dve.drain()
                    dve.tensor_tensor(key, key, rank, ALU.mult)
                    dve.drain()
                    dve.tensor_reduce(rank_top, key, AX.X, ALU.max)
                    dve.drain()
                    dve.tensor_tensor(chosen, rank, wide(rank_top), ALU.is_equal)
                    dve.drain()

                pick(logit, m1, k1, one)
                dve.scalar_tensor_tensor(low, one, -1000.0, logit, ALU.mult, ALU.add)
                dve.drain()
                pick(low, m2, k2, two)
                dve.tensor_tensor(d, m2, m1, ALU.subtract).then_inc(s["margin_ready"], 1)
                dve.wait_ge(s["exp_ready"], it + 1)
                dve.tensor_scalar(r, d, 1.0, None, ALU.add)
                dve.drain()
                dve.reciprocal(r, r)
                dve.drain()
                dve.tensor_tensor(dr, d, r, ALU.mult)
                dve.tensor_tensor(one, one, wide(r), ALU.mult)
                dve.drain()
                dve.tensor_tensor(two, two, wide(dr), ALU.mult)
                dve.drain()
                dve.tensor_tensor(g, one, two, ALU.add).then_inc(s["gates_ready"], 1)
                for e in range(EXPERTS):
                    dve.wait_ge(s["spread_ready"], it * EXPERTS + e + 1)
                    if e >= 2:
                        dve.wait_ge(s["expert_done"], it * EXPERTS + e - 1)
                    dve.tensor_tensor(xg[:, e % 2, :, :], chip.xT[:, :, :],
                                      gates_bank[e % 2][:, 0:SEQ].unsqueeze(1).to_broadcast([P, DC, SEQ]), ALU.mult)\
                       .then_inc(s["scaled"], 1)
                dve.wait_ge(s["expert_done"], it * EXPERTS + EXPERTS)
                ln_vector(dve, chip, out, it, s, it)

        @block.gpsimd
        def _(pool):
            for cc in range(DC):
                pool.wait_ge(s["chunk_loaded"], 16 * (cc + 1))
                pool.tensor_copy(M[:, cc, :, 0:DIM // 2], stage.rearrange("p (r e) -> p e r", e=EXPERTS)[:, :, 0:DIM // 2])\
                    .then_inc(s["chunk_used2"], 1)

FP32R = mybir.dt.float32r
NH, HW, VW = 32, 16, 32


class Uses:

    def __init__(self, first, each):
        assert len(first) % 2 == 0 and len(each) % 2 == 0
        self.first, self.each = first, each
        self.name = {n: j for j, (n, _) in enumerate(each)}
        self.name_first = {n: j for j, (n, _) in enumerate(first)}

    def count(self, uses, engine):
        return sum(e == engine for _, e in uses)

    def place(self, name, batch):
        if batch is None:
            j = self.name_first[name]
            e = self.first[j][1]
            return j % 2, j + 1, e, self.count(self.first[:j + 1], e)
        j = self.name[name]
        e = self.each[j][1]
        return (j % 2, len(self.first) + batch * len(self.each) + j + 1, e,
                self.count(self.first, e) + batch * self.count(self.each, e) + self.count(self.each[:j + 1], e))

    def before(self, name, batch):
        if batch is None:
            j = self.name_first[name]
            return None if j < 2 else (self.first[j - 2][1], self.count(self.first[:j - 1], self.first[j - 2][1]))
        j = self.name[name]
        if j >= 2:
            e = self.each[j - 2][1]
            return e, (self.count(self.first, e) + batch * self.count(self.each, e)
                       + self.count(self.each[:j - 1], e))
        e = self.each[j - 2][1]
        later = self.count(self.each[len(self.each) + j - 1:], e)
        return e, self.count(self.first, e) + batch * self.count(self.each, e) - later


def rotary_tables(nc, chip, keep, fside_dram):
    NT = NTILE + TILES
    chip.rot_sin, chip.rot_cos = (keep.enter_context(nc.sbuf_tensor(n, [P, NT, HW], FP32)) for n in ("rot_sin", "rot_cos"))
    with ExitStack() as c:
        sb = lambda name, shape: c.enter_context(nc.sbuf_tensor(name, shape, FP32))
        pos = sb("pos", [P, NT, 2])
        ang, turns, red = sb("ang", [P, NT, 8]), sb("turns", [P, NT, 8]), sb("red", [P, NT, 8])
        loaded, reduced, taken = (c.enter_context(nc.semaphore(n)) for n in ("pos_loaded", "ang_reduced", "sin_taken"))
        block = c.enter_context(nc.Block())
        PI, TWO_PI_HI = float(np.float32(np.pi)), 6.28125
        TWO_PI_LO = float(2 * np.pi - TWO_PI_HI)
        pi_floor = float(np.nextafter(np.float32(np.pi), np.float32(0)))
        MAGIC = float(3 << 22)

        @block.sync
        def _(sp):
            sp.wait_ge(reduced, 1)
            with nc.allow_non_contiguous_dma(reason="two positions a token"):
                sp.dma_start(pos[:, 0:NTILE, :], fside_dram.rearrange("b (t p) a -> p (b t) a", p=P)).then_inc(loaded, 16)

        @block.scalar
        def _(act):
            for i, table in enumerate((chip.rot_sin, chip.rot_cos)):
                act.wait_ge(reduced, i + 2)
                odd = table[:, :, :].rearrange("p n (f two) -> p n f two", two=2)[:, :, :, 1]
                act.activation(odd, red[:, :, :], ACT.Sin).then_inc(taken, 1)

        @block.vector
        def _(dve):
            dve.memset(pos[:, :, :], 0.0).then_inc(reduced, 1)
            dve.wait_ge(loaded, 16)
            freq = chip.const[:, C_FREQ:C_FREQ + 4]
            for axis in range(2):
                dve.tensor_tensor(ang[:, :, 4 * axis:4 * axis + 4],
                                  pos[:, :, axis:axis + 1].to_broadcast([P, NT, 4]),
                                  freq.unsqueeze(1).to_broadcast([P, NT, 4]), ALU.mult)
            dve.drain()
            for i, (table, shift, sign) in enumerate(((chip.rot_sin, 0.0, -1.0), (chip.rot_cos, 0.25, 1.0))):
                dve.tensor_scalar(turns[:, :, :], ang[:, :, :], float(1 / (2 * np.pi)), shift, ALU.mult, ALU.add)
                dve.drain()
                dve.tensor_scalar(turns[:, :, :], turns[:, :, :], MAGIC, MAGIC, ALU.add, ALU.subtract)
                dve.drain()
                if i:
                    dve.wait_ge(taken, i)
                dve.scalar_tensor_tensor(red[:, :, :], turns[:, :, :], -TWO_PI_HI, ang[:, :, :], ALU.mult, ALU.add)
                dve.drain()
                dve.scalar_tensor_tensor(red[:, :, :], turns[:, :, :], -TWO_PI_LO, red[:, :, :], ALU.mult, ALU.add)
                dve.drain()
                if shift:
                    dve.tensor_scalar(red[:, :, :], red[:, :, :], float(np.pi / 2), None, ALU.add)
                    dve.drain()
                dve.tensor_scalar(red[:, :, :], red[:, :, :], -pi_floor, pi_floor, ALU.max, ALU.min)
                dve.drain().then_inc(reduced, 1)
                dve.wait_ge(taken, i + 1)
                pairs = table[:, :, :].rearrange("p n (f two) -> p n f two", two=2)
                dve.tensor_scalar(pairs[:, :, :, 0], pairs[:, :, :, 1], sign, None, ALU.mult)


def attention_narrow(nc, chip, wq_dram, wk_dram, wv_dram, wo_dram, ctx_dram=None, bias_dram=None,
                     fside_dram=None):
    cross = ctx_dram is not None
    tag = "y" if cross else "c"
    KC = CC if cross else DC
    KVH = NH if cross else 8
    KW = KVH * HW
    KB = NH // 2 if cross else KVH
    SCALE = 0.25
    PTS = 2

    c = ExitStack()
    if cross:
        rotary_tables(nc, chip, c, fside_dram)
    chip.sequence_buffers(c, tag)
    sb = lambda name, shape, dt=FP32: c.enter_context(nc.sbuf_tensor(f"{name}_{tag}", shape, dt))
    wq, wo = sb("wq", [P, DC, DIM]), sb("wo", [P, DC, DIM])
    wk, wv = sb("wk", [P, KC, KW]), sb("wv", [P, KC, KW])
    qT, kT = sb("qT", [P, 2, NH // 2, SEQ], FP32R), sb("kT", [P, 2, KB, SEQ], FP32R)
    v = sb("v", [P, 2, TILES, KVH, VW])
    parts = sb("parts", [P, 2, NH, 4 * HW])
    rot, turn = sb("rot", [P, DIM]), sb("turn", [P, DIM])
    mx, neg_hl = sb("mx", [P, TILES, NH]), sb("neg_hl", [P, TILES, 2, 2, NH])
    negT = sb("negT", [P, 2, SEQ], FP32R)
    select = sb("select", [P, NH], FP32R)
    probsT = sb("probsT", [P, PTS, 2 * SEQ])
    heads = sb("heads", [P, NH // 4, SEQ])
    rden = sb("rden", [P, NH // 2])
    heads_n = sb("heads_n", [P, TILES, DIM])
    scratch, tick = sb("scratch", [P, P]), sb("tick", [P, 1])
    if cross:
        ctx_sb, ctxT = sb("ctx", [P, TILES, CTX_DIM]), sb("ctxT", [P, CC, SEQ])
        bout = sb("bout", [P, DIM])
        headsT = heads[:, 0:DC, :]
        cos_now, sin_now = sb("cos_now", [P, TILES, HW]), sb("sin_now", [P, TILES, HW])
    else:
        ident16, hide16 = sb("ident16", [P, P], BF16), sb("hide16", [P, P], BF16)
    kv_src = ctxT if cross else chip.xT

    prep, score, scoreT, hbank = chip.bank[0:2], chip.bank[2:4], chip.bank[4:6], chip.bank[6:8]

    KU = KB // 4
    QU = NH // 2 // 4
    A_USES = ([("xT0", "act"), ("xT1", "act")] + ([("ctxT", "act")] if cross else [])
              + [("k0", "dve"), ("k1", "dve"), ("v0", "act"), ("v1", "act")]
              + [(f"kT0{n}", "act") for n in range(KU)] + [("q0", "dve")]
              + [(f"kT1{n}", "act") for n in range(KU)] + [("q1", "dve")]
              + [(f"qT{t}{n}", "act") for t in range(TILES) for n in range(QU)])
    FIN = ([(f"h{n}", "dve") for n in range(4)] + ([("hT0", "act"), ("hT1", "act")] if cross else [])
           + [("out0", "dve"), ("out1", "dve")])
    pad = lambda u: ([("spare", "act")] if len(u) % 2 else [])
    first = A_USES + [("neg", "dve")]
    first = pad(first) + first
    each = A_USES + FIN + [("neg", "dve")]
    each = pad(each) + each
    uses = Uses(first, each)

    with c:
        s = {n: c.enter_context(nc.semaphore(f"{n}_{tag}")) for n in (
            "wq_loaded", "wk_loaded", "wv_loaded", "wo_loaded", "bias_loaded", "consts_ready", "xs_ready",
            "ctx_loaded", "ctx_used", "prep_ready", "prep_act", "prep_dve", "split",
            "scores_ready", "scores_read", "neg_ready", "scoresT_ready", "exp_ready", "values_ready",
            "heads_ready", "heads_copied", "x_ready", "out_read", "rot_ready")}
        block = c.enter_context(nc.Block())

        def nxt(batch):
            return 0 if batch is None else batch + 1

        @block.sync
        def _(sp):
            sp.dma_start(wk[:, :, :], wk_dram.rearrange("(c p) n -> p c n", p=P)).then_inc(s["wk_loaded"], 16)
            sp.dma_start(wq[:, :, :], wq_dram.rearrange("(c p) n -> p c n", p=P)).then_inc(s["wq_loaded"], 16)
            sp.dma_start(wv[:, :, :], wv_dram.rearrange("(c p) n -> p c n", p=P)).then_inc(s["wv_loaded"], 16)
            if cross:
                sp.dma_start(ctx_sb[:, :, :], ctx_dram[0, :, :].rearrange("(t p) d -> p t d", p=P))\
                  .then_inc(s["ctx_loaded"], 16)
            sp.dma_start(wo[:, :, :], wo_dram.rearrange("(c p) n -> p c n", p=P)).then_inc(s["wo_loaded"], 16)
            if cross:
                sp.dma_start(bout[:, :], bias_dram.partition_broadcast(P)).then_inc(s["bias_loaded"], 16)
                with sp.Fori(1, BATCH) as it:
                    sp.wait_ge(s["ctx_used"], it)
                    sp.dma_start(ctx_sb[:, :, :], ctx_dram[bass.ds(it, 1), :, :].rearrange("b (t p) d -> p (b t) d", p=P))\
                      .then_inc(s["ctx_loaded"], 16)
                sp.wait_ge(s["ctx_used"], BATCH)
                sp.dma_start(ctx_sb[:, :, :], ctx_dram[0, :, :].rearrange("(t p) d -> p t d", p=P))\
                  .then_inc(s["ctx_loaded"], 16)
            sp.wait_ge(s["x_ready"], BATCH)

        AFTER = [n for n, _ in A_USES if n not in ("xT0", "xT1", "ctxT")]
        S_AT = 18

        def at_step(h):
            if h == 0:
                return (["spare"] if pad(A_USES + FIN + [0]) else []) + ["xT0", "xT1"] + (["ctxT"] if cross else [])
            n = len(AFTER)
            return AFTER[(h - 1) * n // (S_AT - 1):h * n // (S_AT - 1)] if h < S_AT else []

        def score_step(h):
            return [] if h < S_AT else [2 * (h - S_AT), 2 * (h - S_AT) + 1]

        @block.tensor
        def _(pe):
            def claim(name, batch):
                free = uses.before(name, batch)
                if free:
                    pe.wait_ge(s[f"prep_{free[0]}"], free[1])
                return prep[uses.place(name, batch)[0]]

            def read(name, batch):
                _, _, engine, n = uses.place(name, batch)
                pe.wait_ge(s[f"prep_{engine}"], n)

            def prepare(name, batch, par):
                n = nxt(batch)
                b = claim(name, batch)
                if name == "spare":
                    last = pe.transpose(b[:, 0:P], chip.ident, chip.ident)
                elif name in ("xT0", "xT1"):
                    if name == "xT0":
                        pe.wait_ge(s["xs_ready"], n + 1)
                    j = int(name[2])
                    for i in range(4):
                        cc, t = 2 * j + i // 2, i % 2
                        last = pe.transpose(b[:, P * i:P * i + P], chip.xs[:, t, cc * P:(cc + 1) * P], chip.ident)
                elif name == "ctxT":
                    pe.wait_ge(s["ctx_loaded"], 16 * (n + 1))
                    for i in range(4):
                        cc, t = i // 2, i % 2
                        last = pe.transpose(b[:, P * i:P * i + P], ctx_sb[:, t, cc * P:(cc + 1) * P], chip.ident)
                    pe.drain().then_inc(s["ctx_used"], 1)
                elif name[0] in "qkv" and name[1] != "T":
                    t = int(name[1])
                    if name == "k0":
                        read("xT1", batch)
                        if cross:
                            read("ctxT", batch)
                        if batch is None:
                            pe.wait_ge(s["wk_loaded"], 16)
                            pe.wait_ge(s["wv_loaded"], 16)
                            pe.wait_ge(s["wq_loaded"], 16)
                    w, src, chunks = {"q": (wq, chip.xT, DC), "k": (wk, kv_src, KC), "v": (wv, kv_src, KC)}[name[0]]
                    width = DIM if name[0] == "q" else KW
                    for cc in range(chunks):
                        last = pe.matmul(b[:, 0:width], src[:, cc, t * P:(t + 1) * P], w[:, cc, :],
                                         start=(cc == 0), stop=(cc == chunks - 1))
                elif name[0:2] in ("qT", "kT"):
                    k = name[0] == "k"
                    t, n4 = int(name[2]), int(name[3])
                    pe.wait_ge(s["split"], 4 * n + (0 if k else 2) + t + 1)
                    flat_parts = parts[:, t, :, :].rearrange("p h w -> p (h w)")
                    for i in range(4):
                        blk = 4 * n4 + i
                        last = pe.transpose(b[:, P * i:P * (i + 1)], flat_parts[:, P * blk:P * (blk + 1)], chip.ident)
                elif name == "neg":
                    pe.wait_ge(s["neg_ready"], n + 1)
                    for t in range(TILES):
                        last = pe.transpose(b[:, t * P:(t + 1) * P],
                                            neg_hl[:, t, :, :, :].rearrange("p a b h -> p (a b h)"), chip.ident)
                last.then_inc(s["prep_ready"], 1)

            def first_scores(h, batch, par):
                n = nxt(batch)
                if h == 0:
                    read(f"qT1{QU - 1}", batch)
                if h >= 2:
                    pe.wait_ge(s["scores_read"], n * NH + h - 1)
                r = 64 * (h % 2)
                kb = h // 2 if cross else h // 4
                for t in range(TILES):
                    last = pe.matmul(score[h % 2][:, t * SEQ:(t + 1) * SEQ], qT[r:r + 64, par, h // 2, t * P:(t + 1) * P],
                                     kT[r:r + 64, par, kb, :], start=True, stop=True)
                last.then_inc(s["scores_ready"], 1)

            def second_scores(h, batch, par):
                if h == 0:
                    pe.wait_ge(s["prep_dve"], uses.count(uses.first, "dve") + batch * uses.count(uses.each, "dve"))
                if h >= 2:
                    pe.wait_ge(s["exp_ready"], batch * NH + h - 1)
                r = 64 * (h % 2)
                kb = h // 2 if cross else h // 4
                b = scoreT[h % 2]
                for k in range(TILES):
                    dst = b[:, k * SEQ:(k + 1) * SEQ]
                    pe.matmul(dst, kT[r:r + 64, par, kb, k * P:(k + 1) * P], qT[r:r + 64, par, h // 2, :],
                              start=True, stop=False, skip_group_check=True)
                    last = pe.matmul(dst, select[r:r + 64, h:h + 1].to_broadcast([64, P]), negT[r:r + 64, par, :],
                                     start=False, stop=cross, skip_group_check=True)
                    if not cross:
                        last = pe.matmul(b[:, k * SEQ + k * P:k * SEQ + (k + 1) * P], ident16[:, :], hide16[:, :],
                                         start=False, stop=True, skip_group_check=True)
                last.then_inc(s["scoresT_ready"], 1)

            def values(h, batch, par):
                pe.wait_ge(s["exp_ready"], batch * NH + h + 1)
                if h % 8 == 0 and h >= 16:
                    pe.wait_ge(s["heads_copied"], batch * 4 + h // 8 - 1)
                r = VW * (h % 4)
                b = hbank[h // 8 % 2]
                col = h // 4 % 2 * SEQ
                kh = h if cross else h // 4
                for k in range(TILES):
                    q0 = 0 if cross else k * P
                    last = pe.matmul(b[r:r + VW, col + q0:col + SEQ], v[:, par, k, kh, :],
                                     probsT[:, h % PTS, k * SEQ + q0:(k + 1) * SEQ],
                                     start=(k == 0), stop=(k == TILES - 1), skip_group_check=True)
                last.then_inc(s["values_ready"], 1)
                if h % 8 == 7:
                    pe.drain().then_inc(s["heads_ready"], 1)

            def finish(name, batch):
                if name == "h0":
                    pe.wait_ge(s["heads_copied"], batch * 4 + 4)
                b = claim(name, batch)
                n = int(name[-1])
                if name[:-1] == "h":
                    t = n // 2
                    for i in range(4):
                        last = pe.transpose(b[:, P * i:P * (i + 1)], heads[:, 4 * (n % 2) + i, t * P:(t + 1) * P], chip.ident)
                elif name[:-1] == "hT":
                    read("h3", batch)
                    for i in range(4):
                        cc, t = 2 * n + i // 2, i % 2
                        last = pe.transpose(b[:, P * i:P * (i + 1)], heads_n[:, t, cc * P:(cc + 1) * P], chip.ident)
                else:
                    read("hT1" if cross else "h3", batch)
                    for i in range(DC):
                        if cross:
                            a = headsT[:, i, n * P:(n + 1) * P]
                        else:
                            a = heads_n[:, i % 2, 2 * n * P + i // 2:2 * (n + 1) * P:2]
                        last = pe.matmul(b[:, :], a, wo[:, i, :], start=(i == 0), stop=(i == DC - 1))
                last.then_inc(s["prep_ready"], 1)

            pe.wait_ge(s["consts_ready"], 1)
            for name, _ in uses.first[:-1]:
                prepare(name, None, 0)
            for h in range(NH):
                first_scores(h, None, 0)
            prepare("neg", None, 0)
            pe.wait_ge(s["wo_loaded"], 16)
            with pe.Fori(0, BATCH // 2) as pair:
                for par in range(2):
                    batch = pair * 2 + par
                    for h in range(NH):
                        second_scores(h, batch, par)
                        for name in at_step(h):
                            prepare(name, batch, 1 - par)
                        for hh in score_step(h):
                            first_scores(hh, batch, 1 - par)
                        if h >= 1:
                            values(h - 1, batch, par)
                    values(NH - 1, batch, par)
                    rest = 2 * (NH - S_AT)
                    finish("h0", batch)
                    finish("h1", batch)
                    first_scores(rest, batch, 1 - par)
                    finish("h2", batch)
                    finish("h3", batch)
                    first_scores(rest + 1, batch, 1 - par)
                    first_scores(rest + 2, batch, 1 - par)
                    if cross:
                        finish("hT0", batch)
                        finish("hT1", batch)
                    first_scores(rest + 3, batch, 1 - par)
                    finish("out0", batch)
                    finish("out1", batch)
                    prepare("neg", batch, 1 - par)

        @block.scalar
        def _(act):
            copy = lambda dst, src: act.activation(dst, src, ACT.Copy)
            flat = lambda a: a.rearrange("p a b -> p (a b)")

            def take(name, batch):
                bank, ready, _, _ = uses.place(name, batch)
                act.wait_ge(s["prep_ready"], ready)
                return prep[bank]

            def prepare(name, batch, par):
                n = nxt(batch)
                if name == "xT0":
                    if batch is None:
                        copy(chip.xs[:, :, :], chip.x[:, 0:TILES, :]).then_inc(s["xs_ready"], 1)
                    else:
                        copy(chip.xs[:, :, :], chip.x[:, bass.ds(batch * TILES + TILES, TILES), :])\
                            .then_inc(s["xs_ready"], 1)
                b = take(name, batch)
                if name == "spare":
                    last = copy(scratch[:, 0:P], b[:, 0:P])
                elif name in ("xT0", "xT1"):
                    j = int(name[2])
                    last = copy(flat(chip.xT[:, 2 * j:2 * j + 2, :]), b[:, :])
                elif name == "ctxT":
                    last = copy(flat(ctxT[:, :, :]), b[:, :])
                elif name in ("v0", "v1"):
                    last = copy(v[:, par, int(name[1]), :, 0:HW], b[:, 0:KW].rearrange("p (h w) -> p h w", w=HW))
                else:
                    t, n = int(name[2]), int(name[3])
                    dst = (kT if name[0] == "k" else qT)[:, par, 4 * n:4 * n + 4, t * P:(t + 1) * P]
                    last = copy(dst, b[:, :].rearrange("p (g q) -> p g q", g=4))
                last.then_inc(s["prep_act"], 1)

            def is_act(name):
                return dict(uses.each + uses.first)[name] == "act"

            act.wait_ge(s["consts_ready"], 1)
            for name, e in uses.first:
                if e == "act":
                    prepare(name, None, 0)
            with act.Fori(0, BATCH // 2) as pair:
                for par in range(2):
                    batch = pair * 2 + par
                    for h in range(NH):
                        act.wait_ge(s["scoresT_ready"], batch * NH + h + 1)
                        if h >= PTS:
                            act.wait_ge(s["values_ready"], batch * NH + h - PTS + 1)
                        act.activation(probsT[:, h % PTS, :], scoreT[h % 2][:, :], ACT.Exp, scale=SCALE)\
                           .then_inc(s["exp_ready"], 1)
                        for name in at_step(h):
                            if is_act(name):
                                prepare(name, batch, 1 - par)
                        if h % 8 == 1 and h > 1:
                            g = h // 8 - 1
                            act.wait_ge(s["heads_ready"], batch * 4 + g + 1)
                            copy(flat(heads[:, 2 * g:2 * g + 2, :]), hbank[g % 2][:, :]).then_inc(s["heads_copied"], 1)
                    act.wait_ge(s["heads_ready"], batch * 4 + 4)
                    copy(flat(heads[:, 6:8, :]), hbank[1][:, :]).then_inc(s["heads_copied"], 1)
                    if cross:
                        for n in range(2):
                            b = take(f"hT{n}", batch)
                            copy(flat(headsT[:, 2 * n:2 * n + 2, :]), b[:, :]).then_inc(s["prep_act"], 1)

        @block.vector
        def _(dve):
            def take(name, batch):
                bank, ready, _, _ = uses.place(name, batch)
                dve.wait_ge(s["prep_ready"], ready)
                return prep[bank]

            def rotate(name, batch, par):
                t = int(name[1])
                q = name[0] == "q"
                if q:
                    dve.wait_ge(s["prep_ready"], uses.place(f"kT{t}{KU - 1}", batch)[1])
                heads_ = NH if q else KVH
                width = heads_ * HW
                b = take(name, batch)[:, 0:width].rearrange("p (h w) -> p h w", w=HW)
                if cross:
                    cos, sin = cos_now[:, t, :], sin_now[:, t, :]
                else:
                    cos = chip.const[:, C_COS + HW * t:C_COS + HW * (t + 1)]
                    sin = chip.const[:, C_SIN + HW * t:C_SIN + HW * (t + 1)]
                wide = lambda a, n: a.unsqueeze(1).to_broadcast([P, heads_, n])
                r = rot[:, 0:width].rearrange("p (h w) -> p h w", w=HW)
                u = turn[:, 0:width].rearrange("p (h w) -> p h w", w=HW)
                dve.tensor_tensor(r, b, wide(cos, HW), ALU.mult)
                for i in range(2):
                    mine, other = ((slice(i, HW, 2), slice(1 - i, HW, 2)) if cross else
                                   (slice(8 * i, 8 * i + 8), slice(8 - 8 * i, 16 - 8 * i)))
                    last = dve.tensor_tensor(u[:, :, mine], b[:, :, other], wide(sin[:, mine], 8), ALU.mult)
                last.then_inc(s["prep_dve"], 1)
                dve.drain()
                dve.tensor_tensor(r, r, u, ALU.add)
                dve.drain()
                flat_parts = parts[:, t, :, :].rearrange("p h w -> p (h w)")
                if q:
                    d = parts[:, t, :, :].rearrange("p h (r l w) -> p l h r w", r=2, l=2)
                    hi, lo = [d[:, 0]], [d[:, 1]]
                elif cross:
                    d = parts[:, t, :, :].rearrange("p h (l r w) -> p l h r w", r=2, l=2)
                    hi, lo = [d[:, 0]], [d[:, 1]]
                else:
                    d = flat_parts[:, 0:KVH * P].rearrange("p (h c l r w) -> p l c h r w", c=2, r=2, l=2, w=HW)
                    hi, lo = [d[:, 0, 0], d[:, 0, 1]], [d[:, 1, 0], d[:, 1, 1]]
                twice = lambda a: a.unsqueeze(2).to_broadcast([P, heads_, 2, HW])
                for o in hi:
                    dve.tensor_copy(o.bitcast(FP32R), twice(r))
                dve.drain()
                for o in lo:
                    last = dve.tensor_tensor(o, twice(r), hi[0], ALU.subtract)
                last.then_inc(s["split"], 1)
                dve.drain()

            def prepare(name, batch, par):
                n = nxt(batch)
                if name == "k0" and cross:
                    first_tile = (batch + 1) * TILES if batch is not None else 0
                    dve.tensor_copy(cos_now[:, :, :], chip.rot_cos[:, bass.ds(first_tile, TILES), :])
                    dve.tensor_copy(sin_now[:, :, :], chip.rot_sin[:, bass.ds(first_tile, TILES), :])
                    dve.drain()
                if name[0] in "qk":
                    rotate(name, batch, par)
                else:
                    b = take(name, batch)
                    dve.tensor_copy(negT[:, par, :], b[:, 0:SEQ]).then_inc(s["prep_dve"], 1)

            def maxima(h, batch):
                n = nxt(batch)
                dve.wait_ge(s["scores_ready"], n * NH + h + 1)
                b = score[h % 2]
                if cross:
                    dve.tensor_reduce(mx[:, :, h], b[:, :].rearrange("p (t k) -> p t k", t=TILES), AX.X, ALU.max)\
                       .then_inc(s["scores_read"], 1)
                else:
                    dve.memset(tick[:, :], 0.0)
                    for t in range(TILES):
                        nk = (t + 1) * P
                        at_ = C_OWN if t == 0 else C_CAUSAL
                        dve.tensor_tensor_reduce(out=scratch2[t][:, 0:nk], in0=b[:, t * SEQ:t * SEQ + nk],
                                                 in1=chip.const[:, at_:at_ + nk], scale=1.0, scalar=FLOOR,
                                                 op0=ALU.add, op1=ALU.max, accum_out=mx[:, t, h:h + 1])
                    dve.drain().then_inc(s["scores_read"], 1)

            def negate():
                dve.drain()
                hi, lo = neg_hl[:, :, :, 0, :], neg_hl[:, :, :, 1, :]
                twice = mx[:, :, :].unsqueeze(2).to_broadcast([P, TILES, 2, NH])
                dve.tensor_scalar(mx[:, :, :], mx[:, :, :], -1.0, None, ALU.mult)
                dve.drain()
                dve.tensor_copy(hi.bitcast(FP32R), twice)
                dve.drain()
                dve.tensor_tensor(lo, twice, hi, ALU.subtract)
                dve.drain().then_inc(s["neg_ready"], 1)

            def is_dve(name):
                return dict(uses.each + uses.first)[name] == "dve"

            scratch2 = [rot, turn]
            dve.memset(v[:, :, :, :, :].rearrange("p a t h w -> p (a t h) w")[:, :, HW:HW + 1], 1.0)
            dve.memset(v[:, :, :, :, :].rearrange("p a t h w -> p (a t h) w")[:, :, HW + 1:], 0.0)
            for r in (0, 64):
                for i in (0, NH):
                    dve.tensor_copy(select[r + i:r + i + NH, :], chip.const[r + i:r + i + NH, C_ID + r + i:C_ID + r + i + NH])
            if not cross:
                dve.tensor_copy(ident16[:, :], chip.ident)
                dve.tensor_copy(hide16[:, :], chip.const[:, C_OWN_T:C_OWN_T + P])
            dve.drain().then_inc(s["consts_ready"], 1)
            for name, e in uses.first[:-1]:
                if e == "dve":
                    prepare(name, None, 0)
            for h in range(NH):
                maxima(h, None)
            negate()
            prepare("neg", None, 0)
            if cross:
                dve.wait_ge(s["bias_loaded"], 16)
            with dve.Fori(0, BATCH // 2) as pair:
                for par in range(2):
                    batch = pair * 2 + par
                    for h in range(NH):
                        for name in at_step(h):
                            if is_dve(name):
                                prepare(name, batch, 1 - par)
                        for hh in score_step(h):
                            maxima(hh, batch)
                    rest = 2 * (NH - S_AT)

                    def normalise(n):
                        b = take(f"h{n}", batch)[:, :].rearrange("p (h w) -> p h w", w=VW)
                        dve.reciprocal(rden[:, :], b[:, :, HW])
                        dve.drain()
                        t = n // 2
                        dst = heads_n[:, t, 256 * (n % 2):256 * (n % 2) + 256].rearrange("p (h w) -> p h w", w=HW)
                        dve.tensor_tensor(dst, b[:, :, 0:HW], rden[:, :].unsqueeze(2).to_broadcast([P, NH // 2, HW]),
                                          ALU.mult).then_inc(s["prep_dve"], 1)
                        dve.drain()

                    normalise(0)
                    normalise(1)
                    maxima(rest, batch)
                    normalise(2)
                    normalise(3)
                    for i in range(1, 4):
                        maxima(rest + i, batch)
                    negate()
                    for t in range(TILES):
                        b = take(f"out{t}", batch)
                        dve.tensor_tensor(chip.res[:, t, :], b[:, :], chip.x[:, bass.ds(batch * TILES + t, 1), :],
                                          ALU.add).then_inc(s["prep_dve"], 1)
                    prepare("neg", batch, 1 - par)
                    dve.drain()
                    if cross:
                        dve.tensor_tensor(chip.res[:, :, :], chip.res[:, :, :],
                                          bout[:, :].unsqueeze(1).to_broadcast([P, TILES, DIM]), ALU.add)
                        dve.drain()
                    ln_rows(dve, chip, batch, s)

INTER = 2048
MC = INTER // P
BLOCK = 2
NBLOCK = MC // BLOCK
GROUP = 512
NGROUP = NTILE * P // GROUP
GT = GROUP // P


def hadamard_inputs(nc, chip, y_hi, y_lo, down, sign_up_dram, down_dram, scale_down_dram):
    with ExitStack() as c:
        sb = lambda name, shape: c.enter_context(nc.sbuf_tensor(name, shape, FP32))
        rows = sb("down_rows", [P, DC, INTER])
        sign, scale = sb("sign_up", [P, DC]), sb("scale_down", [P, DC])
        half = sb("half_turned", [P, DC, SEQ])
        chip.sequence_buffers(c, "h")
        xs, xT = chip.xs, chip.xT
        s = {n: c.enter_context(nc.semaphore(f"{n}_h")) for n in (
            "small_loaded", "rows_loaded", "scaled", "ready", "copied", "folded", "xs_ready", "hi_ready", "lo_ready",
            "xT_ready", "xT_copied", "down_ready", "down_copied", "h_ready", "h_copied", "y_ready")}
        turn, had, xbank, ybank = chip.bank[0:2], chip.bank[2:4], chip.bank[4:6], chip.bank[6:8]
        h128 = chip.const[:, C_HAD:C_HAD + P]
        block = c.enter_context(nc.Block())

        @block.sync
        def _(sp):
            with nc.allow_non_contiguous_dma(reason="512 signs and scales onto the partitions"):
                sp.dma_start(sign[:, :], sign_up_dram.rearrange("(c p) -> p c", p=P)).then_inc(s["small_loaded"], 16)
                sp.dma_start(scale[:, :], scale_down_dram.rearrange("(c p) -> p c", p=P)).then_inc(s["small_loaded"], 16)
            for o in range(DC):
                sp.dma_start(rows[:, o, :], down_dram[o * P:(o + 1) * P, :]).then_inc(s["rows_loaded"], 16)
                sp.wait_ge(s["rows_loaded"], 16 * (o + 1))

        @block.tensor
        def _(pe):
            for b in range(BATCH):
                pe.wait_ge(s["xs_ready"], b + 1)
                for j in range(2):
                    if b >= 1:
                        pe.wait_ge(s["xT_copied"], 2 * b - 1 + j)
                    for i in range(4):
                        cc, t = 2 * j + i // 2, i % 2
                        last = pe.transpose(xbank[j][:, P * i:P * i + P], xs[:, t, cc * P:(cc + 1) * P], chip.ident)
                    last.then_inc(s["xT_ready"], 1)
                pe.wait_ge(s["folded"], b + 1)
                for j in range(2):
                    if b >= 1:
                        pe.wait_ge(s["lo_ready"], 2 * b - 1 + j)
                    for i in range(2):
                        last = pe.matmul(ybank[j][:, i * SEQ:(i + 1) * SEQ], h128, half[:, 2 * j + i, :],
                                         start=True, stop=True)
                    last.then_inc(s["y_ready"], 1)
                if b == 0:
                    pe.wait_ge(s["scaled"], DC)
                for m in (2 * b, 2 * b + 1):
                    if m >= 2:
                        pe.wait_ge(s["down_copied"], m - 1)
                    for o in range(DC):
                        last = pe.transpose(turn[m % 2][:, P * o:P * (o + 1)], rows[:, o, m * P:(m + 1) * P], chip.ident)
                    last.then_inc(s["down_ready"], 1)
                for m in (2 * b, 2 * b + 1):
                    pe.wait_ge(s["down_copied"], m + 1)
                    if m >= 2:
                        pe.wait_ge(s["h_copied"], m - 1)
                    pe.matmul(had[m % 2][:, :], h128, down[:, m, :], start=True, stop=True).then_inc(s["h_ready"], 1)

        @block.scalar
        def _(act):
            copy = lambda dst, src, **k: act.activation(dst, src, ACT.Copy, **k)
            act.wait_ge(s["small_loaded"], 32)
            for b in range(BATCH):
                if b >= 1:
                    act.wait_ge(s["xT_ready"], 2 * b)
                copy(xs[:, :, :], chip.x[:, b * TILES:(b + 1) * TILES, :]).then_inc(s["xs_ready"], 1)
                for j in range(2):
                    act.wait_ge(s["xT_ready"], 2 * b + j + 1)
                    for i in range(2):
                        cc = 2 * j + i
                        last = copy(half[:, cc, :], xbank[j][:, i * SEQ:(i + 1) * SEQ], scale=sign[:, cc:cc + 1])
                    last.then_inc(s["xT_copied"], 1)
                if b == 0:
                    for o in range(DC):
                        act.wait_ge(s["rows_loaded"], 16 * (o + 1))
                        copy(rows[:, o, :], rows[:, o, :], scale=scale[:, o:o + 1]).then_inc(s["scaled"], 1)
                for j in range(2):
                    act.wait_ge(s["y_ready"], 2 * b + j + 1)
                    copy(y_hi[:, 2 * j:2 * j + 2, b * SEQ:(b + 1) * SEQ],
                         ybank[j][:, :].rearrange("p (c q) -> p c q", c=2), scale=float(DIM ** -0.5))\
                        .then_inc(s["hi_ready"], 1)
                for m in (2 * b, 2 * b + 1):
                    act.wait_ge(s["down_ready"], m + 1)
                    copy(down[:, m, :], turn[m % 2][:, :]).then_inc(s["down_copied"], 1)
                for m in (2 * b, 2 * b + 1):
                    act.wait_ge(s["h_ready"], m + 1)
                    copy(down[:, m, :], had[m % 2][:, :]).then_inc(s["h_copied"], 1)

        @block.vector
        def _(dve):
            for b in range(BATCH):
                dve.wait_ge(s["xT_copied"], 2 * b + 2)
                near = lambda t: t.rearrange("p (a two) q -> p two a q", two=2)
                far = lambda t: t.rearrange("p (two a) q -> p two a q", two=2)
                h, x = near(half[:, :, :]), near(xT[:, :, :])
                dve.tensor_tensor(x[:, 0], h[:, 0], h[:, 1], ALU.add)
                dve.tensor_tensor(x[:, 1], h[:, 0], h[:, 1], ALU.subtract)
                dve.drain()
                h, x = far(half[:, :, :]), far(xT[:, :, :])
                dve.tensor_tensor(h[:, 0], x[:, 0], x[:, 1], ALU.add)
                dve.tensor_tensor(h[:, 1], x[:, 0], x[:, 1], ALU.subtract)
                dve.drain().then_inc(s["folded"], 1)
                for j in range(2):
                    dve.wait_ge(s["hi_ready"], 2 * b + j + 1)
                    dve.scalar_tensor_tensor(
                        y_lo[:, 2 * j:2 * j + 2, b * SEQ:(b + 1) * SEQ],
                        ybank[j][:, :].rearrange("p (c q) -> p c q", c=2), float(DIM ** -0.5),
                        y_hi[:, 2 * j:2 * j + 2, b * SEQ:(b + 1) * SEQ].bitcast(FP32), ALU.mult, ALU.subtract)\
                        .then_inc(s["lo_ready"], 1)
            dve.wait_ge(s["h_copied"], MC)
            other = rows[:, :, :].rearrange("p a (b o) -> p (a b) o", o=DIM)
            a, b = down[:, :, :], other
            for stage in range(4):
                w = 1 << stage
                v = lambda t: t.rearrange("p (g two w) o -> p two g (w o)", two=2, w=w)
                src, dst = v(a), v(b)
                dve.tensor_tensor(dst[:, 0], src[:, 0], src[:, 1], ALU.add)
                dve.tensor_tensor(dst[:, 1], src[:, 0], src[:, 1], ALU.subtract)
                dve.drain()
                a, b = b, a


def hadamard_ffn(nc, chip, sign_up_dram, sign_down_dram, scale_up_dram, scale_down_dram,
                 up_dram, gate_dram, down_dram):
    with ExitStack() as c:
        sb = lambda name, shape, dt=FP32: c.enter_context(nc.sbuf_tensor(name, shape, dt))
        y_hi, y_lo = sb("y_hi", [P, DC, NTILE * P], FP32R), sb("y_lo", [P, DC, NTILE * P], FP32R)
        down = sb("down", [P, MC, DIM])
        hadamard_inputs(nc, chip, y_hi, y_lo, down, sign_up_dram, down_dram, scale_down_dram)

        rows = sb("ug_rows", [P, BLOCK, 2, DIM])
        w_hi, w_lo = (sb(n, [P, 2, DC, 2 * BLOCK, P], FP32R) for n in ("ug_hi", "ug_lo"))
        d_hi, d_lo = (sb(n, [P, BLOCK, DIM], FP32R) for n in ("down_hi", "down_lo"))
        scale_ug, sign_down = sb("scale_ug", [P, 2, MC]), sb("sign_down", [P, MC])
        scale_now, sign_now = sb("scale_now", [P, 2, BLOCK]), sb("sign_now", [P, BLOCK])
        silu, h = sb("silu", [P, GROUP]), sb("h", [P, GROUP])
        h_hi, h_lo = (sb(n, [P, 2, BLOCK, GROUP], FP32R) for n in ("h_hi", "h_lo"))
        s = {n: c.enter_context(nc.semaphore(f"{n}_f")) for n in (
            "small_loaded", "rows_loaded", "rows_used", "scales_ready", "turned", "hi_ready", "lo_ready",
            "gate_ready", "up_ready", "silu_ready", "h_ready", "h_hi_ready", "h_lo_ready", "d_hi_ready",
            "d_lo_ready", "down_ready", "added")}
        turn, gate, up, dbank = chip.bank[0:2], chip.bank[2:4], chip.bank[4:6], chip.bank[6:8]
        block = c.enter_context(nc.Block())
        NA = NGROUP * BLOCK
        ND = NGROUP * GT

        @block.sync
        def _(sp):
            with nc.allow_non_contiguous_dma(reason="scales and signs onto the partitions"):
                sp.dma_start(scale_ug[:, :, :], scale_up_dram.rearrange("(k c p) -> p k c", p=P, k=2))\
                  .then_inc(s["small_loaded"], 16)
                sp.dma_start(sign_down[:, :], sign_down_dram.rearrange("(c p) -> p c", p=P)).then_inc(s["small_loaded"], 16)

            def load(blk):
                for kind, w in enumerate((gate_dram, up_dram)):
                    src = w[bass.ds(blk * (BLOCK * P), BLOCK * P), :].rearrange("(c p) n -> p c n", p=P)
                    sp.dma_start(rows[:, :, kind, :], src).then_inc(s["rows_loaded"], 16)

            load(0)
            with sp.Fori(1, NBLOCK) as blk:
                sp.wait_ge(s["rows_loaded"], 32 * blk)
                sp.wait_ge(s["rows_used"], blk)
                load(blk)
            sp.wait_ge(s["rows_loaded"], 32 * NBLOCK)
            sp.wait_ge(s["rows_used"], NBLOCK)
            load(0)
            sp.wait_ge(s["rows_loaded"], 32 * (NBLOCK + 1))

        @block.tensor
        def _(pe):
            def turn_weights(blk, par, n):
                if n == 0:
                    pe.wait_ge(s["rows_loaded"], 32 * blk + 32)
                if not (isinstance(blk, int) and n < 2):
                    pe.wait_ge(s["lo_ready"], 2 * BLOCK * blk + n - 1)
                for cc in range(DC):
                    last = pe.transpose(turn[n % 2][:, P * cc:P * (cc + 1)],
                                        rows[:, n // 2, n % 2, cc * P:(cc + 1) * P], chip.ident)
                last.then_inc(s["turned"], 1)
                if n == 2 * BLOCK - 1:
                    pe.drain().then_inc(s["rows_used"], 1)

            def gate_up(blk, par, g):
                for m in range(BLOCK):
                    a = g * BLOCK + m
                    for kind, banks, read in ((0, gate, "silu_ready"), (1, up, "h_ready")):
                        if a >= 2:
                            pe.wait_ge(s[read], blk * NA + a - 1)
                        n = 0
                        for w, y in ((w_hi, y_hi), (w_hi, y_lo), (w_lo, y_hi)):
                            for cc in range(DC):
                                last = pe.matmul(banks[m][:, :], w[:, par, cc, 2 * m + kind, :],
                                                 y[:, cc, g * GROUP:(g + 1) * GROUP], start=(n == 0), stop=(n == 11))
                                n += 1
                        last.then_inc(s["up_ready" if kind else "gate_ready"], 1)

            def down_product(blk, par, g):
                pe.wait_ge(s["h_lo_ready"], blk * NA + (g + 1) * BLOCK)
                for t in range(GT):
                    d = g * GT + t
                    pe.wait_ge(s["added"], blk * ND + d + 1)
                    n = 0
                    for hh, dd in ((h_hi, d_hi), (h_hi, d_lo), (h_lo, d_hi)):
                        for m in range(BLOCK):
                            last = pe.matmul(dbank[d % 2][:, :], hh[:, g % 2, m, t * P:(t + 1) * P], dd[:, m, :],
                                             start=(n == 0), stop=(n == 5))
                            n += 1
                    last.then_inc(s["down_ready"], 1)

            for n in range(2 * BLOCK):
                turn_weights(0, 0, n)
            with pe.Fori(0, NBLOCK // 2) as i:
                for par in range(2):
                    blk = 2 * i + par
                    for g in range(NGROUP):
                        turn_weights(blk + 1, 1 - par, g)
                        if g == 0:
                            pe.wait_ge(s["lo_ready"], 2 * BLOCK * blk + 2 * BLOCK)
                        gate_up(blk, par, g)
                        if g == 1:
                            pe.wait_ge(s["d_lo_ready"], blk + 1)
                        if g >= 1:
                            down_product(blk, par, g - 1)
                    down_product(blk, par, NGROUP - 1)

        @block.scalar
        def _(act):
            def split_weights(blk, par, n):
                act.wait_ge(s["turned"], 2 * BLOCK * blk + n + 1)
                act.activation(w_hi[:, par, :, n, :], turn[n % 2][:, :].rearrange("p (c n) -> p c n", c=DC), ACT.Copy)\
                   .then_inc(s["hi_ready"], 1)

            for n in range(2 * BLOCK):
                split_weights(0, 0, n)
            with act.Fori(0, NBLOCK // 2) as i:
                for par in range(2):
                    blk = 2 * i + par
                    for g in range(NGROUP):
                        split_weights(blk + 1, 1 - par, g)
                        if g == 0:
                            act.wait_ge(s["scales_ready"], blk + 1)
                        for m in range(BLOCK):
                            a = g * BLOCK + m
                            act.wait_ge(s["gate_ready"], blk * NA + a + 1)
                            act.activation(silu[:, :], gate[m][:, :], ACT.Silu, scale=scale_now[:, 1, m:m + 1])\
                               .then_inc(s["silu_ready"], 1)
                            act.wait_ge(s["h_ready"], blk * NA + a + 1)
                            act.activation(h_hi[:, g % 2, m, :], h[:, :], ACT.Copy).then_inc(s["h_hi_ready"], 1)

        @block.vector
        def _(dve):
            def split_weights(blk, par, n):
                dve.wait_ge(s["hi_ready"], 2 * BLOCK * blk + n + 1)
                dve.tensor_tensor(w_lo[:, par, :, n, :], turn[n % 2][:, :].rearrange("p (c n) -> p c n", c=DC),
                                  w_hi[:, par, :, n, :].bitcast(FP32), ALU.subtract).then_inc(s["lo_ready"], 1)

            def add_down(blk, g):
                for t in range(GT):
                    d = g * GT + t
                    dve.wait_ge(s["down_ready"], blk * ND + d + 1)
                    dve.tensor_tensor(chip.x[:, d, :], chip.x[:, d, :], dbank[d % 2][:, :], ALU.add)\
                       .then_inc(s["added"], 1)

            dve.drain().then_inc(s["added"], 2)
            dve.wait_ge(s["small_loaded"], 32)
            dve.tensor_scalar(sign_down[:, :], sign_down[:, :], float(INTER ** -0.5), None, ALU.mult)
            dve.drain()
            for n in range(2 * BLOCK):
                split_weights(0, 0, n)
            with dve.Fori(0, NBLOCK // 2) as i:
                for par in range(2):
                    blk = 2 * i + par
                    dve.tensor_copy(scale_now[:, :, :], scale_ug[:, :, bass.ds(blk * BLOCK, BLOCK)])
                    dve.tensor_copy(sign_now[:, :], sign_down[:, bass.ds(blk * BLOCK, BLOCK)])
                    dve.drain().then_inc(s["scales_ready"], 1)
                    for m in range(BLOCK):
                        rows_m = down[:, bass.ds(blk * BLOCK + m, 1), :]
                        dve.tensor_scalar(d_hi[:, m:m + 1, :], rows_m, sign_now[:, m:m + 1], None, ALU.mult)
                        dve.drain()
                        dve.scalar_tensor_tensor(d_lo[:, m:m + 1, :], rows_m, sign_now[:, m:m + 1],
                                                 d_hi[:, m:m + 1, :].bitcast(FP32), ALU.mult, ALU.subtract)
                    dve.drain().then_inc(s["d_lo_ready"], 1)
                    for g in range(NGROUP):
                        split_weights(blk + 1, 1 - par, g)
                        for m in range(BLOCK):
                            a = g * BLOCK + m
                            dve.wait_ge(s["silu_ready"], blk * NA + a + 1)
                            dve.wait_ge(s["up_ready"], blk * NA + a + 1)
                            dve.scalar_tensor_tensor(h[:, :], up[m][:, :], scale_now[:, 0, m:m + 1], silu[:, :],
                                                     ALU.mult, ALU.mult).then_inc(s["h_ready"], 1)
                            dve.wait_ge(s["h_hi_ready"], blk * NA + a + 1)
                            dve.tensor_tensor(h_lo[:, g % 2, m, :], h[:, :], h_hi[:, g % 2, m, :].bitcast(FP32),
                                              ALU.subtract).then_inc(s["h_lo_ready"], 1)
                            dve.drain()
                        if g >= 1:
                            add_down(blk, g - 1)
                    add_down(blk, NGROUP - 1)


def last_norm(nc, chip, out_dram):
    NT = 4
    with ExitStack() as c:
        sb = lambda name, shape: c.enter_context(nc.sbuf_tensor(name, shape, FP32))
        stat, agg = sb("last_stat", [P, NTILE, 6]), sb("last_agg", [P, NTILE, 2])
        var, rstd, newton = sb("last_var", [P, NTILE]), sb("last_rstd", [P, NTILE]), sb("last_newton", [P, NTILE])
        done, stored = c.enter_context(nc.semaphore("rows_done")), c.enter_context(nc.semaphore("rows_stored"))
        block = c.enter_context(nc.Block())

        @block.sync
        def _(sp):
            out = out_dram.rearrange("b (t p) d -> p (b t) d", p=P)
            for i in range(NTILE // NT):
                sp.wait_ge(done, i + 1)
                sp.dma_start(out[:, i * NT:(i + 1) * NT, :], chip.x[:, i * NT:(i + 1) * NT, :]).then_inc(stored, 16)
            sp.wait_ge(stored, 16 * (NTILE // NT))

        @block.vector
        def _(dve):
            for i in range(NTILE // NT):
                r = slice(i * NT, (i + 1) * NT)
                for t in range(i * NT, (i + 1) * NT):
                    dve.bn_stats(stat[:, t, :], chip.x[:, t, :])
                dve.drain()
                for t in range(i * NT, (i + 1) * NT):
                    dve.bn_aggr(agg[:, t, :], stat[:, t, :])
                dve.drain()
                rsqrt(dve, rstd[:, r], agg[:, r, 1], var[:, r], newton[:, r])
                for t in range(i * NT, (i + 1) * NT):
                    last = dve.tensor_scalar(chip.x[:, t, :], chip.x[:, t, :], agg[:, t, 0:1], rstd[:, t:t + 1],
                                             ALU.subtract, ALU.mult)
                last.then_inc(done, 1)

def decoder(nc, x, ctx_1024, fside, mask, const, a0_wq, a0_wk, a0_wv, a0_wo, x0_wq, x0_wk, x0_wv, x0_wo,
            gate_w, ffn_w, atoms, mix, importance, mask_idx, a1_wq, a1_wk, a1_wv, a1_wo,
            x1_wq, x1_wkv, x1_wout, x1_bout, su_ug, su_dp, ws_ug, ws_dp, w_up, w_gate, w_down, out):
    table = nc.dram_tensor("expert_table", (DIM * DIM + P, EXPERTS), FP32).ap()
    with ExitStack() as ctx:
        chip = Chip(nc, ctx)
        setup(nc, chip, x, const)
        attention_wide(nc, chip, a0_wq, a0_wk, a0_wv, a0_wo, 4, 1 / 128)
        attention_wide(nc, chip, x0_wq, x0_wk, x0_wv, x0_wo, 8, float(np.float32(1) / np.sqrt(np.float32(128))),
                       ctx_1024, mask)
        expert_table(nc, chip, table, atoms, mix, importance, mask_idx)
        experts(nc, chip, table, gate_w, ffn_w)
        attention_narrow(nc, chip, a1_wq, a1_wk, a1_wv, a1_wo)
        attention_narrow(nc, chip, x1_wq, x1_wkv[:, 0:DIM], x1_wkv[:, DIM:], x1_wout, ctx_1024, x1_bout, fside)
        hadamard_ffn(nc, chip, su_ug, su_dp, ws_ug, ws_dp, w_up, w_gate, w_down)
        last_norm(nc, chip, out)


_INS = ['x', 'ctx_1024', 'fside_BxSx2_0', 'mask_BxS2_bf1', 'const', 'L0_attn_Wq', 'L0_attn_Wk', 'L0_attn_Wv', 'L0_attn_Wo',
        'L0_xattn_Wq', 'L0_xattn_Wk', 'L0_xattn_Wv', 'L0_xattn_Wo', 'L0_ffn_gate_w', 'L0_ffn_W', 'L0_ffn_atoms',
        'L0_ffn_expert_atom_weights', 'L0_ffn_importance', 'L0_ffn_mask_idx', 'L1_attn_Wq', 'L1_attn_Wk', 'L1_attn_Wv',
        'L1_attn_Wo', 'L1_xattn_Wq', 'L1_xattn_Wkv', 'L1_xattn_Wout', 'L1_xattn_bout', 'L1_ffn_SU_ug', 'L1_ffn_SU_dp',
        'L1_ffn_Wscale_ug', 'L1_ffn_Wscale_dp', 'L1_ffn_W_up', 'L1_ffn_W_gate', 'L1_ffn_W_down']


def kernel(**inputs):
    import concourse.bacc as _bacc
    from concourse.bass_utils import run_bass_kernel_spmd as _run

    nc = _bacc.Bacc("TRN2", target_bir_lowering=False, num_devices=1)
    arrays, args = {}, []
    for name in _INS:
        a = constants() if name == 'const' else np.ascontiguousarray(inputs[name])
        arrays[f"in_{name}"] = a
        args.append(nc.dram_tensor(f"in_{name}", a.shape, mybir.dt.from_np(a.dtype), kind="ExternalInput").ap())
    args.append(nc.dram_tensor("out_0", (BATCH, SEQ, DIM), FP32, kind="ExternalOutput").ap())
    decoder(nc, *args)
    r = _run(nc, [arrays], core_ids=[0])
    return r.results[0]["out_0"]
```

```python
import numpy as np
import concourse.bass as bass
from concourse import mybir
from contextlib import ExitStack

FP32 = mybir.dt.float32
INT32 = mybir.dt.int32
BF16 = mybir.dt.bfloat16
ALU = mybir.AluOpType
ACT = mybir.ActivationFunctionType
AX = mybir.AxisListType

P = 128
BATCH, SEQ, DIM = 8, 256, 512
TILES = SEQ // P
NTILE = BATCH * TILES
DC = DIM // P
CTX_DIM = 256
CC = CTX_DIM // P
EXPERTS, ATOMS, NSPARSE = 8, 64, 4096
LOW = -1e30
FLOOR = -3e38
EPS = 1e-5

C_ID, C_OWN, C_BAND, C_CAUSAL, C_HAD, C_NHAD, C_COS, C_SIN, C_FREQ, C_RANK, C_BEFORE, C_SPARE, C_OWN_T, C_SLOT = (
    0, 128, 256, 512, 768, 896, 1024, 1056, 1088, 1096, 1112, 1240, 1241, 1369)
C_COLS = C_SLOT + 2 * NTILE + EXPERTS


def constants():
    c = np.zeros((P, C_COLS), np.float32)
    i = np.arange(P)
    c[:, C_ID:C_ID + P] = np.eye(P)
    own = np.where(i[None, :] <= i[:, None], 0.0, LOW)
    prev = np.where(i[None, :] > i[:, None], 0.0, LOW)
    c[:, C_OWN:C_OWN + P] = own
    c[:, C_BAND:C_BAND + P] = prev
    c[:, C_BAND + P:C_BAND + 2 * P] = own
    c[:, C_CAUSAL + P:C_CAUSAL + 2 * P] = own
    h = np.ones((1, 1), np.float32)
    while h.shape[0] < P:
        h = np.block([[h, h], [h, -h]])
    c[:, C_HAD:C_HAD + P] = h
    c[:, C_NHAD:C_NHAD + P] = -h
    half = 8
    inv = (np.float32(1.0) / np.float32(10000.0) ** (np.arange(half, dtype=np.float32) * np.float32(2.0) / np.float32(16))).astype(np.float32)
    pos = np.arange(SEQ, dtype=np.float32).reshape(TILES, P)
    ang = (pos[:, :, None] * inv).astype(np.float32)
    cos, sin = np.cos(ang), np.sin(ang)
    for t in range(TILES):
        c[:, C_COS + 16 * t:C_COS + 16 * t + 16] = np.concatenate([cos[t], cos[t]], 1)
        c[:, C_SIN + 16 * t:C_SIN + 16 * t + 16] = np.concatenate([-sin[t], sin[t]], 1)
    c[:, C_FREQ:C_FREQ + 4] = (np.float32(10000.0) ** (-np.arange(4, dtype=np.float32) / np.float32(4))).astype(np.float32)
    c[:, C_RANK:C_RANK + TILES * EXPERTS] = np.tile(EXPERTS - np.arange(EXPERTS), TILES)
    c[:, C_BEFORE:C_BEFORE + P] = i[None, :] < i[:, None]
    c[:, C_OWN_T:C_OWN_T + P] = own.T
    c[:, C_SPARE] = DIM * DIM + i
    c[:, C_SLOT:] = np.arange(C_COLS - C_SLOT)
    return c


class Chip:

    def __init__(self, nc, ctx):
        sb = lambda name, shape, dt=FP32: ctx.enter_context(nc.sbuf_tensor(name, shape, dt))
        self.nc = nc
        self.x = sb("x_all", [P, NTILE + TILES, DIM])
        self.const = sb("const", [P, C_COLS])
        self.ident = self.const[:, C_ID:C_ID + P]
        self.bank = [ctx.enter_context(nc.psum_tensor(f"bank{i}", [P, 512], FP32)) for i in range(8)]

    def sequence_buffers(self, ctx, tag):
        sb = lambda name, shape: ctx.enter_context(self.nc.sbuf_tensor(f"{name}_{tag}", shape, FP32))
        self.xs = sb("x_static", [P, TILES, DIM])
        self.xT = sb("xT", [P, DC, SEQ])
        self.res = sb("residual", [P, TILES, DIM])
        self.stat = sb("ln_stats", [P, TILES, 8])
        self.var, self.rstd, self.newton = (sb(n, [P, TILES]) for n in ("ln_var", "ln_rstd", "ln_newton"))


class Carve:

    def __init__(self, buf, size):
        self.buf, self.size, self.at = buf, size, 0

    def __call__(self, *shape):
        n = int(np.prod(shape))
        flat = self.buf[:, self.at:self.at + n]
        self.at += n
        assert self.at <= self.size, self.at
        names = "abcd"[:len(shape)]
        if len(shape) == 1:
            return flat
        return flat.rearrange(f"p ({' '.join(names)}) -> p {' '.join(names)}",
                              **{n_: s for n_, s in zip(names, shape)})


def clear_semaphores(nc, semaphores):
    with nc.Block() as block:
        @block.sync
        def _(sp):
            for sem in semaphores:
                sp.sem_clear(sem)


def ln_vector(dve, chip, out_banks, batch, s, it):
    for t in range(TILES):
        last = dve.tensor_tensor(chip.res[:, t, :], out_banks[t][:, :],
                                 chip.x[:, bass.ds(batch * TILES + t, 1), :], ALU.add)
    last.then_inc(s["out_read"], 1)
    dve.drain()
    ln_rows(dve, chip, batch, s)


def rsqrt(dve, out, variance, var, newton):
    dve.tensor_scalar(var, variance, EPS, None, ALU.add)
    dve.drain()
    dve.tensor_scalar(out.bitcast(INT32), var.bitcast(INT32), -0.5, float(0x5F3759DF), ALU.mult, ALU.add)
    dve.drain()
    for _ in range(3):
        dve.tensor_tensor(newton, out, out, ALU.mult)
        dve.drain()
        dve.scalar_tensor_tensor(newton, newton, -0.5, var, ALU.mult, ALU.mult)
        dve.drain()
        dve.scalar_tensor_tensor(out, newton, 1.5, out, ALU.add, ALU.mult)
        dve.drain()


def ln_rows(dve, chip, batch, s):
    for t in range(TILES):
        dve.bn_stats(chip.stat[:, t, 0:6], chip.res[:, t, :])
    dve.drain()
    for t in range(TILES):
        dve.bn_aggr(chip.stat[:, t, 6:8], chip.stat[:, t, 0:6])
    dve.drain()
    rsqrt(dve, chip.rstd[:, :], chip.stat[:, :, 7], chip.var[:, :], chip.newton[:, :])
    for t in range(TILES):
        last = dve.tensor_scalar(chip.x[:, bass.ds(batch * TILES + t, 1), :], chip.res[:, t, :],
                                 chip.stat[:, t, 6:7], chip.rstd[:, t:t + 1], ALU.subtract, ALU.mult)
    last.then_inc(s["x_ready"], 1)



QCHUNKS = 4


class WideWeights:

    def __init__(self, nc, ctx, tag, groups, kv_chunks):
        sb = lambda name, chunks, width: ctx.enter_context(nc.sbuf_tensor(f"{name}_{tag}", [P, chunks, width], FP32))
        self.wk, self.wv = sb("wk", kv_chunks, groups * P), sb("wv", kv_chunks, groups * P)
        self.wq, self.wo = sb("wq", DC, 16 * P), sb("wo", 16, DIM)
        sem = lambda name: ctx.enter_context(nc.semaphore(f"{name}_loaded_{tag}"))
        self.wk_loaded, self.wv_loaded, self.wo_loaded = sem("wk"), sem("wv"), sem("wo")
        self.wq_loaded = [sem(f"wq{i}") for i in range(QCHUNKS)]

    def load(self, sp, wq_dram, wk_dram, wv_dram, wo_dram):
        rows = lambda a: a.rearrange("(c p) n -> p c n", p=P)
        sp.dma_start(self.wk[:, :, :], rows(wk_dram)).then_inc(self.wk_loaded, 16)
        sp.dma_start(self.wv[:, :, :], rows(wv_dram)).then_inc(self.wv_loaded, 16)
        n = 16 * P // QCHUNKS
        for i in range(QCHUNKS):
            sp.dma_start(self.wq[:, :, i * n:(i + 1) * n], rows(wq_dram)[:, :, i * n:(i + 1) * n])\
              .then_inc(self.wq_loaded[i], 16)
        sp.dma_start(self.wo[:, :, :], rows(wo_dram)).then_inc(self.wo_loaded, 16)

    def semaphores(self):
        return [self.wk_loaded, self.wv_loaded, self.wo_loaded] + self.wq_loaded


def attention_wide(nc, chip, w, groups, scale, load=None, ctx_dram=None, mask_dram=None, pool_work=None):
    H, HD = 16, 128
    cross = ctx_dram is not None
    KC = CC if cross else DC
    KVW = groups * HD
    PAIRS = H // 2
    NK, NV = groups // 2, TILES * KVW // 512
    NJ = NK + NV + PAIRS + 2 + (2 if cross else 0)
    assert NJ % 2 == 0
    SLOTS = 5
    tag = "x" if cross else "s"

    c = ExitStack()
    chip.sequence_buffers(c, tag)
    wk, wv, wq, wo = w.wk, w.wv, w.wq, w.wo
    carve = Carve(c.enter_context(nc.sbuf_tensor(f"work_{tag}", [P, 14848], FP32)), 14848)
    qT = carve(2, 512)
    kT = carve(groups, SEQ)
    v = carve(TILES, KVW)
    probs = carve(SLOTS, 2 * SEQ)
    probsT = carve(2, 2 * SEQ)
    oT = carve(H, SEQ)
    mx, neg, den, inv = carve(SLOTS, 2), carve(SLOTS, 2), carve(SLOTS, 2), carve(SLOTS, 2)
    tick = carve(1)
    if cross:
        ctx_sb, ctxT = carve(TILES, CTX_DIM), carve(CC, SEQ)
        mask8 = carve(BATCH * SEQ // 4).bitcast(mybir.dt.uint8)
        bias, maskcol8 = carve(SEQ), carve(BATCH * TILES // 4).bitcast(mybir.dt.uint8)
        maskcol = carve(BATCH * TILES)
        mc = carve(TILES)
    kv_src = ctxT if cross else chip.xT

    KEYS = [(0, 2), (0, 2)] if cross else [(0, 1), (0, 2)]
    COL = [0, 256]
    proj = chip.bank[0:2]
    score = chip.bank[2:4]
    trans = chip.bank[4]
    obank = chip.bank[5]
    out = chip.bank[6:8]

    with c:
        s = {n: c.enter_context(nc.semaphore(f"{n}_{tag}")) for n in (
            "xs_ready", "proj_ready", "proj_copied",
            "scores_ready", "masked", "exp_ready", "probs_ready", "probsT_ready",
            "probsT_copied", "heads_ready", "heads_copied", "out_ready", "x_ready", "out_read", "ctx_loaded", "ctx_used", "mask_loaded", "bias_ready")}
        c.callback(clear_semaphores, nc, list(s.values()) + w.semaphores())
        block = c.enter_context(nc.Block())

        @block.sync
        def _(sp):
            if cross:
                sp.dma_start(mask8, mask_dram.rearrange("b s -> (b s)").partition_broadcast(P)).then_inc(s["mask_loaded"], 16)
                with nc.allow_non_contiguous_dma(reason="2048 mask bytes onto the partitions"):
                    sp.dma_start(maskcol8, mask_dram.rearrange("b (t p) -> p (b t)", p=P)).then_inc(s["mask_loaded"], 16)
            if load:
                w.load(sp, *load)
            if cross:
                sp.dma_start(ctx_sb, ctx_dram[0, :, :].rearrange("(t p) d -> p t d", p=P)).then_inc(s["ctx_loaded"], 16)
                with sp.Fori(1, BATCH) as it:
                    sp.wait_ge(s["ctx_used"], it)
                    sp.dma_start(ctx_sb, ctx_dram[bass.ds(it, 1), :, :].rearrange("b (t p) d -> p (b t) d", p=P))\
                      .then_inc(s["ctx_loaded"], 16)
            sp.wait_ge(s["x_ready"], BATCH)

        @block.tensor
        def _(pe):
            def transpose_x():
                for j in range(2):
                    for i in range(4):
                        cc, t = 2 * j + i // 2, i % 2
                        last = pe.transpose(proj[j][:, 128 * i:128 * i + 128],
                                            chip.xs[:, t, cc * P:(cc + 1) * P], chip.ident)
                    last.then_inc(s["proj_ready"], 1)

            pe.wait_ge(s["xs_ready"], 1)
            transpose_x()
            with pe.Fori(0, BATCH) as it:
                j = 0

                def bank():
                    nonlocal j
                    pe.wait_ge(s["proj_copied"], it * NJ + j + 1)
                    j += 1
                    return proj[(j - 1) % 2]

                if cross:
                    pe.wait_ge(s["ctx_loaded"], it * 16 + 16)
                    for cc in range(CC):
                        b = bank()
                        for t in range(TILES):
                            last = pe.transpose(b[:, P * t:P * t + P], ctx_sb[:, t, cc * P:(cc + 1) * P], chip.ident)
                        last.then_inc(s["proj_ready"], 1)
                    pe.drain().then_inc(s["ctx_used"], 1)
                pe.wait_ge(w.wk_loaded, 16)
                for n in range(NK):
                    b = bank()
                    if n == 0:
                        pe.wait_ge(s["proj_copied"], it * NJ + j + 1)
                    for i in range(2):
                        g = 2 * n + i
                        for cc in range(KC):
                            last = pe.matmul(b[:, i * SEQ:(i + 1) * SEQ], wk[:, cc, g * HD:(g + 1) * HD],
                                             kv_src[:, cc, :], start=(cc == 0), stop=(cc == KC - 1))
                    last.then_inc(s["proj_ready"], 1)
                pe.wait_ge(w.wv_loaded, 16)
                for n in range(NV):
                    b = bank()
                    t, col = n % TILES, n // TILES * 512
                    for cc in range(KC):
                        last = pe.matmul(b[:, :], kv_src[:, cc, t * P:(t + 1) * P], wv[:, cc, col:col + 512],
                                         start=(cc == 0), stop=(cc == KC - 1))
                    last.then_inc(s["proj_ready"], 1)

                def query(pair):
                    if pair % (PAIRS // QCHUNKS) == 0:
                        pe.wait_ge(w.wq_loaded[pair * QCHUNKS // PAIRS], 16)
                    b = bank()
                    for i in range(2):
                        h = 2 * pair + i
                        for cc in range(DC):
                            last = pe.matmul(b[:, i * SEQ:(i + 1) * SEQ], wq[:, cc, h * HD:(h + 1) * HD],
                                             chip.xT[:, cc, :], start=(cc == 0), stop=(cc == DC - 1))
                    last.then_inc(s["proj_ready"], 1)

                def scores(h):
                    pe.wait_ge(s["proj_copied"], it * NJ + (NJ - 2 - PAIRS) + h // 2 + 3)
                    if h >= 2:
                        pe.wait_ge(s["masked"], it * H + h - 1)
                    g = h * groups // H
                    for t, (k0, nk) in enumerate(KEYS):
                        q = qT[:, h // 2 % 2, (h % 2) * SEQ + t * P:(h % 2) * SEQ + (t + 1) * P]
                        last = pe.matmul(score[h % 2][:, COL[t]:COL[t] + nk * P], q, kT[:, g, k0 * P:(k0 + nk) * P],
                                         start=True, stop=True)
                    last.then_inc(s["scores_ready"], 1)

                def turn(h):
                    pe.wait_ge(s["probs_ready"], it * H + h + 1)
                    if h >= 1:
                        pe.wait_ge(s["probsT_copied"], it * H + h)
                    for t, (k0, nk) in enumerate(KEYS):
                        for k in range(nk):
                            last = pe.transpose(trans[:, k * SEQ + t * P:k * SEQ + (t + 1) * P],
                                                probs[:, h % SLOTS, COL[t] + k * P:COL[t] + (k + 1) * P], chip.ident)
                    last.then_inc(s["probsT_ready"], 1)

                def values(h):
                    pe.wait_ge(s["probsT_copied"], it * H + h + 1)
                    if h >= 1:
                        pe.wait_ge(s["heads_copied"], it * H + h)
                    g = h * groups // H
                    for k in range(TILES):
                        q0 = 0 if cross else k * P
                        last = pe.matmul(obank[:, (h % 2) * SEQ + q0:(h % 2 + 1) * SEQ], v[:, k, g * HD:(g + 1) * HD],
                                         probsT[:, h % 2, k * SEQ + q0:(k + 1) * SEQ],
                                         start=(k == 0), stop=(k == TILES - 1), skip_group_check=True)
                    last.then_inc(s["heads_ready"], 1)

                def output(h0, h1):
                    if h0 == 0:
                        pe.wait_ge(w.wo_loaded, 16)
                    pe.wait_ge(s["heads_copied"], it * H + h1)
                    for t in range(TILES):
                        for h in range(h0, h1):
                            last = pe.matmul(out[t][:, :], oT[:, h, t * P:(t + 1) * P], wo[:, h, :],
                                             start=(h == 0), stop=(h == H - 1), skip_group_check=True)
                    if h1 == H:
                        last.then_inc(s["out_ready"], 1)

                for step in range(H + 5):
                    if step < H and step % 2 == 0:
                        query(step // 2)
                    if 1 <= step <= H:
                        scores(step - 1)
                    if step == H:
                        pe.wait_ge(s["xs_ready"], it + 2)
                        pe.wait_ge(s["proj_copied"], it * NJ + NJ)
                        transpose_x()
                        j += 2
                        output(0, 6)
                    if 4 <= step < H + 4:
                        turn(step - 4)
                    if step >= 5:
                        values(step - 5)
                    if step == H + 1:
                        output(6, 12)
                output(12, H)
                assert j == NJ

        @block.scalar
        def _(act):
            copy = lambda dst, src: act.activation(dst, src, ACT.Copy)
            xt_half = lambda i: chip.xT[:, 2 * i:2 * i + 2, :].rearrange("p c q -> p (c q)")
            copy(chip.xs[:, :, :], chip.x[:, 0:TILES, :]).then_inc(s["xs_ready"], 1)
            for i in range(2):
                act.wait_ge(s["proj_ready"], i + 1)
                copy(xt_half(i), proj[i][:, :]).then_inc(s["proj_copied"], 1)
            with act.Fori(0, BATCH) as it:
                j = 0

                def evacuate(dst, cols=512):
                    nonlocal j
                    act.wait_ge(s["proj_ready"], it * NJ + j + 3)
                    copy(dst, proj[j % 2][:, 0:cols]).then_inc(s["proj_copied"], 1)
                    j += 1

                if cross:
                    for cc in range(CC):
                        evacuate(ctxT[:, cc, :], SEQ)
                for n in range(NK):
                    evacuate(kT[:, 2 * n:2 * n + 2, :].rearrange("p g q -> p (g q)"))
                for n in range(NV):
                    t, col = n % TILES, n // TILES * 512
                    if cross:
                        if n == 0:
                            act.wait_ge(s["bias_ready"], it + 1)
                        act.wait_ge(s["proj_ready"], it * NJ + j + 3)
                        act.activation(v[:, t, col:col + 512], proj[j % 2][:, :], ACT.Copy, scale=mc[:, t:t + 1])\
                           .then_inc(s["proj_copied"], 1)
                        j += 1
                    else:
                        evacuate(v[:, t, col:col + 512])
                for step in range(H + 5):
                    if step < H and step % 2 == 0:
                        evacuate(qT[:, step // 2 % 2, :])
                    if 1 <= step <= H:
                        h = step - 1
                        act.wait_ge(s["masked"], it * H + h + 1)
                        for t, (k0, nk) in enumerate(KEYS):
                            pr = probs[:, h % SLOTS, COL[t]:COL[t] + nk * P]
                            last = act.activation(pr, pr, ACT.Exp, bias=neg[:, h % SLOTS, t:t + 1],
                                                  accum_out=den[:, h % SLOTS, t:t + 1])
                        last.then_inc(s["exp_ready"], 1)
                    if step == H // 2:
                        copy(chip.xs[:, :, :], chip.x[:, bass.ds(it * TILES + TILES, TILES), :]).then_inc(s["xs_ready"], 1)
                    if step == H:
                        for i in range(2):
                            evacuate(xt_half(i))
                    if step >= 5:
                        h = step - 5
                        act.wait_ge(s["heads_ready"], it * H + h + 1)
                        copy(oT[:, h, :], obank[:, (h % 2) * SEQ:(h % 2 + 1) * SEQ]).then_inc(s["heads_copied"], 1)

        @block.vector
        def _(dve):
            if cross:
                dve.wait_ge(s["mask_loaded"], 32)
                dve.tensor_copy(maskcol, maskcol8)
                dve.drain()
            with dve.Fori(0, BATCH) as it:
                if cross:
                    dve.tensor_copy(mc, maskcol[:, bass.ds(it * TILES, TILES)])
                    dve.tensor_copy(bias, mask8[:, bass.ds(it * SEQ, SEQ)])
                    dve.drain()
                    dve.tensor_scalar(bias, bias, 1.0, -LOW, ALU.subtract, ALU.mult).then_inc(s["bias_ready"], 1)
                    dve.drain()
                for step in range(H + 4):
                    if step >= 4:
                        h = step - 4
                        dve.wait_ge(s["probsT_ready"], it * H + h + 1)
                        if cross:
                            dve.tensor_copy(probsT[:, h % 2, :], trans[:, :]).then_inc(s["probsT_copied"], 1)
                        else:
                            dve.tensor_copy(probsT[:, h % 2, 0:SEQ], trans[:, 0:SEQ])
                            dve.tensor_copy(probsT[:, h % 2, SEQ + P:], trans[:, SEQ + P:])\
                               .then_inc(s["probsT_copied"], 1)
                    if step < H:
                        h = step
                        dve.wait_ge(s["scores_ready"], it * H + h + 1)
                        dve.memset(tick, 0.0)
                        for t, (k0, nk) in enumerate(KEYS):
                            if cross:
                                hide = bias
                            else:
                                at_ = C_OWN if t == 0 else C_BAND
                                hide = chip.const[:, at_:at_ + nk * P]
                            dve.tensor_tensor_reduce(
                                out=probs[:, h % SLOTS, COL[t]:COL[t] + nk * P],
                                in0=score[h % 2][:, COL[t]:COL[t] + nk * P], in1=hide, scale=scale,
                                scalar=FLOOR, op0=ALU.add, op1=ALU.max, accum_out=mx[:, h % SLOTS, t:t + 1])
                        dve.drain()
                        dve.tensor_scalar(neg[:, h % SLOTS, :], mx[:, h % SLOTS, :], -1.0, None, ALU.mult)\
                           .then_inc(s["masked"], 1)
                    if 1 <= step <= H:
                        h = step - 1
                        dve.wait_ge(s["exp_ready"], it * H + h + 1)
                        dve.reciprocal(inv[:, h % SLOTS, :], den[:, h % SLOTS, :])
                        dve.drain()
                        for t, (k0, nk) in enumerate(KEYS):
                            pr = probs[:, h % SLOTS, COL[t]:COL[t] + nk * P]
                            last = dve.tensor_scalar(pr, pr, inv[:, h % SLOTS, t:t + 1], None, ALU.mult)
                        last.then_inc(s["probs_ready"], 1)
                dve.wait_ge(s["out_ready"], it + 1)
                ln_vector(dve, chip, out, it, s, it)

        if pool_work:
            block.gpsimd(pool_work)

SETS = NSPARSE // P
TABLE_ROWS = DIM * DIM + P
SLOTS_OF_TOKENS = 2 * NTILE + EXPERTS
ZERO_PARTS = 16


class ExpertTable:

    def __init__(self, nc, ctx):
        sb = lambda name, width, dt: ctx.enter_context(nc.sbuf_tensor(name, [P, width], dt))
        self.table = nc.dram_tensor("expert_table", (TABLE_ROWS, EXPERTS), FP32).ap()
        self.rows = nc.dram_tensor("expert_rows", (SLOTS_OF_TOKENS * P, DIM), FP32).ap()
        self.products = nc.dram_tensor("expert_products", (SLOTS_OF_TOKENS * P, DIM), FP32).ap()
        self.zero = sb("table_zero", DIM * DIM * EXPERTS // ZERO_PARTS // P, FP32)
        self.dest = sb("table_dest", SETS, INT32)
        self.summed = sb("table_summed", SETS * EXPERTS, FP32)
        self.table_clear, self.set_added = (ctx.enter_context(nc.semaphore(n)) for n in ("table_clear", "set_added"))
        ctx.callback(clear_semaphores, nc, [self.table_clear, self.set_added])

    def clear(self, sp):
        part = DIM * DIM // ZERO_PARTS
        for i in range(ZERO_PARTS):
            sp.dma_start(self.table[i * part:(i + 1) * part, :].rearrange("(p n) e -> p (n e)", p=P), self.zero[:, :])\
              .then_inc(self.table_clear, 16)
        sp.dma_start(self.table[ZERO_PARTS * part:, :], self.zero[:, 0:EXPERTS]).then_inc(self.table_clear, 16)
        for i in range(0, SLOTS_OF_TOKENS, 2):
            sp.dma_start(self.rows[i * P:(i + 2) * P, :].rearrange("(p n) d -> p (n d)", p=P), self.zero[:, 0:2 * DIM])\
              .then_inc(self.table_clear, 16)

    def add_sets(self, pool):
        pool.wait_ge(self.table_clear, 16 * (ZERO_PARTS + 1 + SLOTS_OF_TOKENS // 2))
        for i in range(SETS):
            pool.indirect_dma_start(
                out=self.table, out_offset=bass.IndirectOffsetOnAxis(ap=self.dest[:, i:i + 1].bitcast(mybir.dt.uint32), axis=0),
                in_=self.summed[:, i * EXPERTS:(i + 1) * EXPERTS], in_offset=None, compute_op=ALU.add)\
                .then_inc(self.set_added, 16)
            pool.wait_ge(self.set_added, 16 * (i + 1))


def start(nc, chip, x_dram, const_dram, t, atoms_dram, mix_dram, importance_dram, index_dram, load_weights):
    c = ExitStack()
    big = c.enter_context(nc.sbuf_tensor("expert_big", [P, 12288], FP32))
    carve = Carve(c.enter_context(nc.sbuf_tensor("expert_work", [P, 4096], FP32)), 4096)
    zero = t.zero[:, :]
    atoms = big[0:ATOMS, 0:NSPARSE]
    importance = big[0:EXPERTS, 4096:4096 + NSPARSE]
    same = big[:, 8192:8192 + SETS * P].rearrange("p (i s) -> p i s", i=SETS)
    mix = carve(ATOMS)[0:EXPERTS]
    mixT = carve(EXPERTS)[0:ATOMS]
    mstat = carve(4)[0:EXPERTS]
    index, col, row = carve(SETS).bitcast(INT32), carve(SETS).bitcast(INT32), carve(SETS).bitcast(INT32)
    indexf, colf, rowf, dest = carve(SETS), carve(SETS), carve(SETS), carve(SETS)
    before = carve(SETS)
    earlier = big[:, 4096:4096 + SETS * P].rearrange("p (i s) -> p i s", i=SETS)
    weighted = carve(SETS, EXPERTS)
    gate = carve(SETS, EXPERTS)
    flat = lambda a: a.rearrange("p a b -> p (a b)")

    with c:
        s = {n: c.enter_context(nc.semaphore(f"{n}_e")) for n in (
            "const_loaded", "x_loaded", "zeros_ready", "mix_loaded", "atoms_loaded", "importance_loaded", "index_loaded",
            "mix_max", "mix_exp", "mix_ready", "mixT_ready", "mixT_copied", "deltas_ready", "imp_ready",
            "imp_exp", "weighted_ready", "index_ready", "row_ready", "same_ready", "sums_ready")}
        c.callback(clear_semaphores, nc, list(s.values()))
        block = c.enter_context(nc.Block())

        @block.sync
        def _(sp):
            sp.dma_start(index, index_dram.rearrange("(p i) -> p i", i=SETS)).then_inc(s["index_loaded"], 16)
            sp.dma_start(mix, mix_dram).then_inc(s["mix_loaded"], 16)
            sp.dma_start(chip.const[:, :], const_dram).then_inc(s["const_loaded"], 16)
            sp.dma_start(importance, importance_dram).then_inc(s["importance_loaded"], 16)
            sp.dma_start(atoms, atoms_dram).then_inc(s["atoms_loaded"], 16)
            sp.dma_start(chip.x[:, 0:NTILE, :], x_dram.rearrange("b (t p) d -> p (b t) d", p=P)).then_inc(s["x_loaded"], 16)
            load_weights(sp)
            sp.wait_ge(s["zeros_ready"], 1)
            t.clear(sp)
            sp.wait_ge(s["x_loaded"], 16)

        @block.tensor
        def _(pe):
            ident8 = chip.const[0:EXPERTS, C_ID:C_ID + EXPERTS]
            pe.wait_ge(s["const_loaded"], 16)
            pe.wait_ge(s["mix_ready"], 1)
            pe.transpose(chip.bank[0][0:ATOMS, 0:EXPERTS], mix, ident8).then_inc(s["mixT_ready"], 1)
            pe.wait_ge(s["importance_loaded"], 16)
            for i in range(SETS):
                last = pe.transpose(chip.bank[1][:, EXPERTS * i:EXPERTS * (i + 1)],
                                    importance[:, i::SETS], ident8)
            last.then_inc(s["imp_ready"], 1)
            pe.wait_ge(s["mixT_copied"], 1)
            pe.wait_ge(s["atoms_loaded"], 16)
            for i in range(SETS):
                last = pe.matmul(chip.bank[2][:, EXPERTS * i:EXPERTS * (i + 1)], atoms[:, i::SETS], mixT,
                                 start=True, stop=True)
            last.then_inc(s["deltas_ready"], 1)
            pe.wait_ge(s["index_ready"], 1)
            for n in range(SETS // 4):
                if n >= 2:
                    pe.wait_ge(s["same_ready"], 4 * (n - 1))
                for i in range(4 * n, 4 * n + 4):
                    last = pe.matmul(chip.bank[3 + n % 2][:, P * (i % 4):P * (i % 4 + 1)],
                                     indexf[:, i:i + 1].to_broadcast([P, P]), chip.ident, start=True, stop=True)
                last.then_inc(s["row_ready"], 1)
            pe.wait_ge(s["same_ready"], SETS)
            pe.wait_ge(s["weighted_ready"], 1)
            for i in range(SETS):
                last = pe.matmul(chip.bank[5][:, EXPERTS * i:EXPERTS * (i + 1)], same[:, i, :], weighted[:, i, :],
                                 start=True, stop=True)
            last.then_inc(s["sums_ready"], 1)

        @block.scalar
        def _(act):
            act.wait_ge(s["mix_max"], 1)
            act.activation(mix, mix, ACT.Exp, bias=mstat[:, 1:2], accum_out=mstat[:, 2:3]).then_inc(s["mix_exp"], 1)
            act.wait_ge(s["imp_ready"], 1)
            act.activation(flat(gate), chip.bank[1][:, 0:SETS * EXPERTS], ACT.Exp, scale=-1.0)\
               .then_inc(s["imp_exp"], 1)

        @block.vector
        def _(dve):
            dve.memset(zero, 0.0).then_inc(s["zeros_ready"], 1)
            dve.memset(chip.x[:, NTILE:, :], 0.0)
            dve.wait_ge(s["mix_loaded"], 16)
            dve.tensor_reduce(mstat[:, 0:1], mix, AX.X, ALU.max)
            dve.drain()
            dve.tensor_scalar(mstat[:, 1:2], mstat[:, 0:1], -1.0, None, ALU.mult).then_inc(s["mix_max"], 1)
            dve.wait_ge(s["mix_exp"], 1)
            dve.reciprocal(mstat[:, 3:4], mstat[:, 2:3])
            dve.drain()
            dve.tensor_scalar(mix, mix, mstat[:, 3:4], None, ALU.mult).then_inc(s["mix_ready"], 1)
            dve.wait_ge(s["index_loaded"], 16)
            dve.tensor_copy(indexf, index)
            dve.tensor_scalar(col, index, DIM - 1, None, ALU.bitwise_and)
            dve.tensor_scalar(row, index, DIM.bit_length() - 1, None, ALU.logical_shift_right)
            dve.drain().then_inc(s["index_ready"], 1)
            dve.tensor_copy(colf, col)
            dve.tensor_copy(rowf, row)
            dve.drain()
            dve.scalar_tensor_tensor(dest, colf, float(DIM), rowf, ALU.mult, ALU.add)
            dve.wait_ge(s["mixT_ready"], 1)
            dve.tensor_copy(mixT, chip.bank[0][0:ATOMS, 0:EXPERTS]).then_inc(s["mixT_copied"], 1)
            dve.wait_ge(s["imp_exp"], 1)
            dve.tensor_scalar(flat(gate), flat(gate), 1.0, None, ALU.add)
            dve.drain()
            dve.reciprocal(flat(gate), flat(gate))
            dve.drain()
            dve.wait_ge(s["deltas_ready"], 1)
            dve.tensor_tensor(flat(weighted), chip.bank[2][:, 0:SETS * EXPERTS], flat(gate), ALU.mult)\
               .then_inc(s["weighted_ready"], 1)
            for i in range(SETS):
                if i % 4 == 0:
                    dve.wait_ge(s["row_ready"], i // 4 + 1)
                dve.tensor_scalar(same[:, i, :], chip.bank[3 + i // 4 % 2][:, P * (i % 4):P * (i % 4 + 1)],
                                  indexf[:, i:i + 1], None, ALU.is_equal).then_inc(s["same_ready"], 1)
            dve.drain()
            dve.tensor_tensor(earlier, same, chip.const[:, C_BEFORE:C_BEFORE + P].unsqueeze(1)
                              .to_broadcast([P, SETS, P]), ALU.mult)
            dve.drain()
            dve.tensor_reduce(before, earlier, AX.X, ALU.add)
            dve.drain()
            dve.tensor_scalar(before, before, 0.0, None, ALU.is_gt)
            dve.wait_ge(s["const_loaded"], 16)
            dve.tensor_scalar(colf, dest, -1.0, chip.const[:, C_SPARE:C_SPARE + 1], ALU.mult, ALU.add)
            dve.drain()
            dve.tensor_tensor(colf, colf, before, ALU.mult)
            dve.drain()
            dve.tensor_tensor(dest, dest, colf, ALU.add)
            dve.drain()
            dve.tensor_copy(t.dest[:, :], dest)
            dve.wait_ge(s["sums_ready"], 1)
            dve.tensor_copy(t.summed[:, :], chip.bank[5][:, 0:SETS * EXPERTS])


def experts(nc, chip, t, gate_dram, w_dram):
    UNROLL = 4
    c = ExitStack()
    chip.sequence_buffers(c, "m")
    weights = c.enter_context(nc.sbuf_tensor("weights_m", [P, 26624], FP32))
    WT = weights[:, 0:DC * DIM].rearrange("p (c r) -> p c r", c=DC)
    at = DC * DIM
    M = weights[:, at:at + DC * EXPERTS * DIM].rearrange("p (c e r) -> p c e r", c=DC, e=EXPERTS)
    at += DC * EXPERTS * DIM
    stage = weights[:, at:at + 2 * EXPERTS * DIM].rearrange("p (s n) -> p s n", s=2)
    total = weights[:, at:at + NTILE * DIM].rearrange("p (t d) -> p t d", t=NTILE)
    carve = Carve(c.enter_context(nc.sbuf_tensor("work_m", [P, 10240], FP32)), 10240)
    xT = [chip.xT, carve(DC, SEQ)]
    shared = carve(2 * UNROLL * DIM)
    w_rows = shared[:, 0:DC * DIM].rearrange("p (c n) -> p c n", c=DC)
    slot_rows = shared[:, 0:UNROLL * DIM].rearrange("p (k d) -> p k d", k=UNROLL)
    product = shared[:, UNROLL * DIM:].rearrange("p (k d) -> p k d", k=UNROLL)
    fetched = shared.rearrange("p (u t k d) -> p u t k d", u=2, t=TILES, k=2)
    slotT = carve(2, DC, P)
    gate_rows = carve(DIM)[0:EXPERTS]
    gateT = carve(DC, EXPERTS)
    logit, low, key, one, two, sent, place, count = (carve(NTILE, EXPERTS) for _ in range(8))
    before = carve(NTILE + 1, EXPERTS)
    m1, m2, k1, k2, d, g1, g2 = (carve(NTILE) for _ in range(7))
    dest = carve(2, NTILE)
    dest_int = carve(2, NTILE).bitcast(INT32)
    full = carve(EXPERTS).bitcast(INT32)
    slots, end = carve(EXPERTS), carve(EXPERTS)
    ended = carve(SLOTS_OF_TOKENS, EXPERTS)
    slot_expert = carve(SLOTS_OF_TOKENS)
    slot_expert_int = carve(SLOTS_OF_TOKENS).bitcast(INT32)
    tick = carve(1)
    rank = chip.const[:, C_RANK:C_RANK + EXPERTS].unsqueeze(1).to_broadcast([P, NTILE, EXPERTS])
    logits_bank, rank_bank, count_bank = chip.bank[0], chip.bank[1], chip.bank[2]
    turn_bank, out = chip.bank[4:6], chip.bank[6:8]
    wide = lambda a: a.unsqueeze(2).to_broadcast([P, NTILE, EXPERTS])
    by_tile = lambda bank: bank[:, 0:NTILE * EXPERTS].rearrange("p (t e) -> p t e", t=NTILE)
    LOOKED = BATCH + 1

    with c:
        s = {n: c.enter_context(nc.semaphore(f"{n}_m")) for n in (
            "w_loaded", "gate_loaded", "chunk_used", "chunk_used2", "wT_ready", "wT_copied", "xs_ready",
            "xT_ready", "xT_copied", "logits_ready", "logits_read", "margin_ready", "exp_ready", "sent_ready",
            "ranks_ready", "dest_ready", "slots_known", "rows_sent", "dense_ready", "dense_read", "slot_turned",
            "slot_copied", "slot_done", "product_copied", "x_ready")}
        ring = lambda name, n: [c.enter_context(nc.semaphore(f"{name}{i}_m")) for i in range(n)]
        chunk_loaded, slot_loaded, stored, back = (
            ring("chunk_loaded", 2), ring("slot_loaded", UNROLL), ring("stored", UNROLL), ring("back", 2))
        returned = c.enter_context(nc.semaphore("returned_m"))
        block = c.enter_context(nc.Block())

        @block.sync
        def _(sp):
            sp.dma_start(gate_rows, gate_dram).then_inc(s["gate_loaded"], 16)
            sp.dma_start(w_rows, w_dram.rearrange("(c p) n -> p c n", p=P)).then_inc(s["w_loaded"], 16)
            for cc in range(DC):
                if cc >= 2:
                    sp.wait_ge(s["chunk_used"], cc - 1)
                    sp.wait_ge(s["chunk_used2"], cc - 1)
                sp.dma_start(stage[:, cc % 2, :], t.table[cc * P * DIM:(cc + 1) * P * DIM, :].rearrange("(p r) e -> p (r e)", p=P))\
                  .then_inc(chunk_loaded[cc % 2], 16)
            sp.wait_ge(s["rows_sent"], 16 * 2 * NTILE)
            sp.wait_ge(s["wT_copied"], DC + 1)
            for k in range(UNROLL):
                sp.dma_start(slot_rows[:, k, :], t.rows[k * P:(k + 1) * P, :]).then_inc(slot_loaded[k], 16)
            with sp.Fori(1, SLOTS_OF_TOKENS // UNROLL) as it:
                for k in range(UNROLL):
                    sp.wait_ge(s["slot_turned"], it * UNROLL + k + 1 - UNROLL)
                    sp.dma_start(slot_rows[:, k, :], t.rows[bass.ds(it * (UNROLL * P) + k * P, P), :]).then_inc(slot_loaded[k], 16)
            sp.wait_ge(s["x_ready"], BATCH)

        @block.tensor
        def _(pe):
            def transpose_x(n):
                pe.wait_ge(s["xs_ready"], n + 1)
                pe.wait_ge(s["xT_copied"], 2 * n + 1)
                for j in range(2):
                    for i in range(4):
                        cc, tile = 2 * j + i // 2, i % 2
                        last = pe.transpose(turn_bank[j][:, P * i:P * i + P],
                                            chip.xs[:, tile, cc * P:(cc + 1) * P], chip.ident)
                    last.then_inc(s["xT_ready"], 1)

            pe.wait_ge(s["w_loaded"], 16)
            for cc in range(DC):
                if cc >= 2:
                    pe.wait_ge(s["wT_copied"], cc - 1)
                for ro in range(DC):
                    last = pe.transpose(turn_bank[cc % 2][:, P * ro:P * (ro + 1)],
                                        w_rows[:, ro, cc * P:(cc + 1) * P], chip.ident)
                last.then_inc(s["wT_ready"], 1)
            pe.wait_ge(s["gate_loaded"], 16)
            for cc in range(DC):
                last = pe.transpose(logits_bank[:, EXPERTS * cc:EXPERTS * (cc + 1)], gate_rows[:, cc * P:(cc + 1) * P],
                                    chip.const[0:EXPERTS, C_ID:C_ID + EXPERTS])
            last.then_inc(s["wT_ready"], 1)
            pe.wait_ge(s["wT_copied"], DC + 1)
            transpose_x(0)
            with pe.Fori(0, BATCH // 2) as it:
                for u in range(2):
                    n = 2 * it + u
                    transpose_x(n + 1)
                    pe.wait_ge(s["logits_read"], n + 1)
                    for tile in range(TILES):
                        for cc in range(DC):
                            last = pe.matmul(logits_bank[:, EXPERTS * tile:EXPERTS * (tile + 1)],
                                             xT[u][:, cc, tile * P:(tile + 1) * P],
                                             gateT[:, cc, :], start=(cc == 0), stop=(cc == DC - 1))
                    last.then_inc(s["logits_ready"], 1)
            transpose_x(LOOKED)
            pe.wait_ge(s["sent_ready"], 1)
            pe.matmul(by_tile(rank_bank), chip.const[:, C_BEFORE:C_BEFORE + P], sent, start=True, stop=True)
            pe.matmul(by_tile(count_bank), chip.const[:, C_HAD:C_HAD + 1].to_broadcast([P, P]), sent, start=True, stop=True)\
              .then_inc(s["ranks_ready"], 1)
            with pe.Fori(0, BATCH // 2) as it:
                for u in range(2):
                    n = 2 * it + u
                    transpose_x(n + LOOKED + 1)
                    for tile in range(TILES):
                        pe.wait_ge(s["dense_read"], 2 * n + tile + 1)
                        for cc in range(DC):
                            last = pe.matmul(out[tile][:, :], xT[(u + LOOKED) % 2][:, cc, tile * P:(tile + 1) * P], WT[:, cc, :],
                                             start=(cc == 0), stop=(cc == DC - 1))
                        last.then_inc(s["dense_ready"], 1)
            pe.wait_ge(s["xT_copied"], 2 * 2 * LOOKED + 1)
            pe.wait_ge(s["dense_read"], 2 * BATCH + 2)

            def turn_slot(it, k):
                pe.wait_ge(slot_loaded[k], 16 * it + 16)
                pe.wait_ge(s["slot_copied"], it * UNROLL + k + 1)
                for cc in range(DC):
                    last = pe.transpose(turn_bank[k % 2][:, P * cc:P * (cc + 1)], slot_rows[:, k, cc * P:(cc + 1) * P], chip.ident)
                last.then_inc(s["slot_turned"], 1)

            def slot_body(it, last_slots):
                for k in range(UNROLL):
                    if k + 1 < UNROLL:
                        turn_slot(it, k + 1)
                    elif not last_slots:
                        turn_slot(it + 1, 0)
                    expert = nc.values_load(slot_expert_int[0:1, bass.ds(it * UNROLL + k, 1)],
                                            engines=[mybir.EngineType.PE], min_val=0, max_val=EXPERTS - 1,
                                            skip_runtime_bounds_check_because="a minimum with the last expert bounds it")
                    pe.wait_ge(s["slot_copied"], it * UNROLL + k + 3)
                    pe.wait_ge(s["product_copied"], it * UNROLL + k + 1)
                    for cc in range(DC):
                        last = pe.matmul(out[k % 2][:, :], slotT[:, k % 2, cc, :], M[:, cc, bass.ds(expert, 1), :],
                                         start=(cc == 0), stop=(cc == DC - 1))
                    last.then_inc(s["slot_done"], 1)

            pe.wait_ge(s["chunk_used"], DC)
            pe.wait_ge(s["chunk_used2"], DC)
            pe.wait_ge(s["slots_known"], 1)
            turn_slot(0, 0)
            with pe.Fori(0, SLOTS_OF_TOKENS // UNROLL - 1) as it:
                slot_body(it, False)
            slot_body(SLOTS_OF_TOKENS // UNROLL - 1, True)

        @block.scalar
        def _(act):
            copy = lambda dst, src: act.activation(dst, src, ACT.Copy)

            def transposed(n, half):
                for j in range(2):
                    act.wait_ge(s["xT_ready"], 2 * n + j + 1)
                    copy(xT[half][:, 2 * j:2 * j + 2, :].rearrange("p c q -> p (c q)"), turn_bank[j][:, :])\
                        .then_inc(s["xT_copied"], 1)

            copy(chip.xs[:, :, :], chip.x[:, 0:TILES, :]).then_inc(s["xs_ready"], 1)
            for cc in range(DC):
                act.wait_ge(s["wT_ready"], cc + 1)
                copy(WT[:, cc, :], turn_bank[cc % 2][:, :]).then_inc(s["wT_copied"], 1)
            act.wait_ge(s["wT_ready"], DC + 1)
            copy(gateT.rearrange("p c e -> p (c e)"), logits_bank[:, 0:DC * EXPERTS]).then_inc(s["wT_copied"], 1)
            act.drain().then_inc(s["xT_copied"], 1)
            for first in (0, LOOKED):
                if first:
                    copy(chip.xs[:, :, :], chip.x[:, 0:TILES, :]).then_inc(s["xs_ready"], 1)
                transposed(first, first % 2)
                if first:
                    act.wait_ge(s["sent_ready"], 1)
                with act.Fori(0, BATCH // 2) as it:
                    for u in range(2):
                        n = 2 * it + u
                        copy(chip.xs[:, :, :], chip.x[:, bass.ds((n + 1) * TILES, TILES), :]).then_inc(s["xs_ready"], 1)
                        transposed(n + first + 1, (u + first + 1) % 2)
                if not first:
                    act.wait_ge(s["margin_ready"], 1)
                    act.activation(d, d, ACT.Exp).then_inc(s["exp_ready"], 1)
                    for cc in range(DC):
                        act.wait_ge(chunk_loaded[cc % 2], 16 * (cc // 2 + 1))
                        copy(M[:, cc, :, DIM // 2:], stage[:, cc % 2, :].rearrange("p (r e) -> p e r", e=EXPERTS)[:, :, DIM // 2:])\
                            .then_inc(s["chunk_used"], 1)
            act.drain().then_inc(s["slot_copied"], 2)
            with act.Fori(0, SLOTS_OF_TOKENS // UNROLL) as it:
                for k in range(UNROLL):
                    act.wait_ge(s["slot_turned"], it * UNROLL + k + 1)
                    copy(slotT[:, k % 2, :, :].rearrange("p c q -> p (c q)"), turn_bank[k % 2][:, :]).then_inc(s["slot_copied"], 1)

        @block.vector
        def _(dve):
            dve.drain().then_inc(s["logits_read"], 1)
            with dve.Fori(0, BATCH) as it:
                dve.wait_ge(s["logits_ready"], it + 1)
                dve.memset(tick, 0.0)
                dve.tensor_scalar(logit[:, bass.ds(it * TILES, TILES), :],
                                  logits_bank[:, 0:TILES * EXPERTS].rearrange("p (t e) -> p t e", t=TILES),
                                  -50.0, 50.0, ALU.max, ALU.min).then_inc(s["logits_read"], 1)
            dve.drain()

            def pick(values, top, rank_top, chosen):
                dve.tensor_reduce(top, values, AX.X, ALU.max)
                dve.drain()
                dve.tensor_tensor(key, values, wide(top), ALU.is_equal)
                dve.drain()
                dve.tensor_tensor(key, key, rank, ALU.mult)
                dve.drain()
                dve.tensor_reduce(rank_top, key, AX.X, ALU.max)
                dve.drain()
                dve.tensor_tensor(chosen, rank, wide(rank_top), ALU.is_equal)
                dve.drain()

            pick(logit, m1, k1, one)
            dve.scalar_tensor_tensor(low, one, -1000.0, logit, ALU.mult, ALU.add)
            dve.drain()
            pick(low, m2, k2, two)
            dve.tensor_tensor(sent, one, two, ALU.add).then_inc(s["sent_ready"], 1)
            dve.tensor_tensor(d, m2, m1, ALU.subtract).then_inc(s["margin_ready"], 1)
            dve.wait_ge(s["ranks_ready"], 1)
            dve.tensor_copy(count, by_tile(count_bank))
            dve.memset(before[:, 0, :], 0.0)
            dve.drain()
            for tile in range(NTILE):
                dve.tensor_tensor(before[:, tile + 1, :], before[:, tile, :], count[:, tile, :], ALU.add)
                dve.drain()
            dve.tensor_scalar(full, before[:, NTILE, :], float(P - 1), None, ALU.add)
            dve.drain()
            dve.tensor_scalar(full, full, P.bit_length() - 1, None, ALU.logical_shift_right)
            dve.drain()
            dve.tensor_copy(slots, full)
            dve.drain()
            dve.tensor_copy(end, slots)
            dve.drain()
            for e in range(1, EXPERTS):
                dve.tensor_tensor(end[:, e:e + 1], end[:, e:e + 1], end[:, e - 1:e], ALU.add)
                dve.drain()
            dve.tensor_tensor(slots, end, slots, ALU.subtract)
            dve.drain()
            dve.tensor_scalar(slots, slots, float(P), None, ALU.mult)
            dve.tensor_tensor(place, before[:, 0:NTILE, :], by_tile(rank_bank), ALU.add)
            dve.drain()
            dve.tensor_tensor(place, place, slots.unsqueeze(1).to_broadcast([P, NTILE, EXPERTS]), ALU.add)
            dve.drain()
            for i, chosen in enumerate((one, two)):
                dve.tensor_tensor(key, place, chosen, ALU.mult)
                dve.drain()
                dve.tensor_reduce(dest[:, i, :], key, AX.X, ALU.add)
                dve.drain()
            dve.tensor_copy(dest_int, dest).then_inc(s["dest_ready"], 1)
            dve.tensor_tensor(ended, chip.const[:, C_SLOT:C_SLOT + SLOTS_OF_TOKENS].unsqueeze(2)
                              .to_broadcast([P, SLOTS_OF_TOKENS, EXPERTS]),
                              end.unsqueeze(1).to_broadcast([P, SLOTS_OF_TOKENS, EXPERTS]), ALU.is_ge)
            dve.drain()
            dve.tensor_reduce(slot_expert, ended, AX.X, ALU.add)
            dve.drain()
            dve.tensor_scalar(slot_expert, slot_expert, float(EXPERTS - 1), None, ALU.min)
            dve.drain()
            dve.tensor_copy(slot_expert_int, slot_expert)
            dve.drain().then_inc(s["slots_known"], 1)
            dve.wait_ge(s["exp_ready"], 1)
            dve.tensor_scalar(g1, d, 1.0, None, ALU.add)
            dve.drain()
            dve.reciprocal(g1, g1)
            dve.drain()
            dve.tensor_tensor(g2, d, g1, ALU.mult)
            dve.wait_ge(s["chunk_used"], DC)
            dve.wait_ge(s["chunk_used2"], DC)
            dve.drain().then_inc(s["dense_read"], 2)
            with dve.Fori(0, BATCH) as it:
                for tile in range(TILES):
                    dve.wait_ge(s["dense_ready"], it * TILES + tile + 1)
                    dve.tensor_tensor(total[:, bass.ds(it * TILES + tile, 1), :], out[tile][:, :],
                                      chip.x[:, bass.ds(it * TILES + tile, 1), :], ALU.add).then_inc(s["dense_read"], 1)
            dve.drain().then_inc(s["product_copied"], 2)

            for k in range(UNROLL):
                dve.wait_ge(s["slot_done"], k + 1)
                dve.tensor_copy(product[:, k, :], out[k % 2][:, :]).then_inc(s["product_copied"], 1)
            with dve.Fori(1, SLOTS_OF_TOKENS // UNROLL) as it:
                for k in range(UNROLL):
                    dve.wait_ge(s["slot_done"], it * UNROLL + k + 1)
                    dve.wait_ge(stored[k], 16 * it)
                    dve.tensor_copy(product[:, k, :], out[k % 2][:, :]).then_inc(s["product_copied"], 1)
            with dve.Fori(0, BATCH // 2) as it:
                for u in range(2):
                    n = 2 * it + u
                    dve.wait_ge(back[u], 64 * it + 64)
                    dve.memset(tick, 0.0)
                    for i, gate in enumerate((g1, g2)):
                        for tile in range(TILES):
                            before_ = total[:, bass.ds(n * TILES + tile, 1), :] if i == 0 else chip.res[:, tile, :]
                            last = dve.scalar_tensor_tensor(chip.res[:, tile, :], fetched[:, u, tile, i, :],
                                                            gate[:, bass.ds(n * TILES + tile, 1)], before_, ALU.mult, ALU.add)
                        if i == 0:
                            dve.drain()
                    last.then_inc(returned, 1)
                    dve.drain()
                    ln_rows(dve, chip, n, s)
                    dve.drain()

        @block.gpsimd
        def _(pool):
            for cc in range(DC):
                pool.wait_ge(chunk_loaded[cc % 2], 16 * (cc // 2 + 1))
                pool.tensor_copy(M[:, cc, :, 0:DIM // 2], stage[:, cc % 2, :].rearrange("p (r e) -> p e r", e=EXPERTS)[:, :, 0:DIM // 2])\
                    .then_inc(s["chunk_used2"], 1)
            pool.wait_ge(s["dest_ready"], 1)
            place_of = lambda tile, i: bass.IndirectOffsetOnAxis(ap=dest_int[:, i, tile:tile + 1].bitcast(mybir.dt.uint32), axis=0)
            for tile in range(NTILE):
                for i in range(2):
                    pool.indirect_dma_start(out=t.rows, out_offset=place_of(tile, i), in_=chip.x[:, tile, :], in_offset=None)\
                        .then_inc(s["rows_sent"], 16)
            with pool.Fori(0, SLOTS_OF_TOKENS // UNROLL) as it:
                for k in range(UNROLL):
                    pool.wait_ge(s["product_copied"], it * UNROLL + k + 3)
                    pool.dma_start(t.products[bass.ds(it * (UNROLL * P) + k * P, P), :], product[:, k, :]).then_inc(stored[k], 16)
            for k in range(UNROLL):
                pool.wait_ge(stored[k], 16 * (SLOTS_OF_TOKENS // UNROLL))
            for n in range(BATCH):
                if n >= 2:
                    pool.wait_ge(returned, n - 1)
                for tile in range(TILES):
                    for i in range(2):
                        pool.indirect_dma_start(out=fetched[:, n % 2, tile, i, :], out_offset=None, in_=t.products,
                                                in_offset=place_of(TILES * n + tile, i)).then_inc(back[n % 2], 16)

FP32R = mybir.dt.float32r
NH, HW, VW = 32, 16, 32


class Uses:

    def __init__(self, first, each):
        assert len(first) % 2 == 0 and len(each) % 2 == 0
        self.first, self.each = first, each
        self.name = {n: j for j, (n, _) in enumerate(each)}
        self.name_first = {n: j for j, (n, _) in enumerate(first)}

    def count(self, uses, engine):
        return sum(e == engine for _, e in uses)

    def place(self, name, batch):
        if batch is None:
            j = self.name_first[name]
            e = self.first[j][1]
            return j % 2, j + 1, e, self.count(self.first[:j + 1], e)
        j = self.name[name]
        e = self.each[j][1]
        return (j % 2, len(self.first) + batch * len(self.each) + j + 1, e,
                self.count(self.first, e) + batch * self.count(self.each, e) + self.count(self.each[:j + 1], e))

    def before(self, name, batch):
        if batch is None:
            j = self.name_first[name]
            return None if j < 2 else (self.first[j - 2][1], self.count(self.first[:j - 1], self.first[j - 2][1]))
        j = self.name[name]
        if j >= 2:
            e = self.each[j - 2][1]
            return e, (self.count(self.first, e) + batch * self.count(self.each, e)
                       + self.count(self.each[:j - 1], e))
        e = self.each[j - 2][1]
        later = self.count(self.each[len(self.each) + j - 1:], e)
        return e, self.count(self.first, e) + batch * self.count(self.each, e) - later


def rotary_tables(nc, chip, keep, fside_dram):
    NT = NTILE + TILES
    chip.rot_sin, chip.rot_cos = (keep.enter_context(nc.sbuf_tensor(n, [P, NT, HW], FP32)) for n in ("rot_sin", "rot_cos"))
    with ExitStack() as c:
        sb = lambda name, shape: c.enter_context(nc.sbuf_tensor(name, shape, FP32))
        pos = sb("pos", [P, NT, 2])
        ang, turns, red = sb("ang", [P, NT, 8]), sb("turns", [P, NT, 8]), sb("red", [P, NT, 8])
        loaded, reduced, taken = (c.enter_context(nc.semaphore(n)) for n in ("pos_loaded", "ang_reduced", "sin_taken"))
        block = c.enter_context(nc.Block())
        PI, TWO_PI_HI = float(np.float32(np.pi)), 6.28125
        TWO_PI_LO = float(2 * np.pi - TWO_PI_HI)
        pi_floor = float(np.nextafter(np.float32(np.pi), np.float32(0)))
        MAGIC = float(3 << 22)

        @block.sync
        def _(sp):
            sp.wait_ge(reduced, 1)
            with nc.allow_non_contiguous_dma(reason="two positions a token"):
                sp.dma_start(pos[:, 0:NTILE, :], fside_dram.rearrange("b (t p) a -> p (b t) a", p=P)).then_inc(loaded, 16)

        @block.scalar
        def _(act):
            for i, table in enumerate((chip.rot_sin, chip.rot_cos)):
                act.wait_ge(reduced, i + 2)
                odd = table[:, :, :].rearrange("p n (f two) -> p n f two", two=2)[:, :, :, 1]
                act.activation(odd, red[:, :, :], ACT.Sin).then_inc(taken, 1)

        @block.vector
        def _(dve):
            dve.memset(pos[:, :, :], 0.0).then_inc(reduced, 1)
            dve.wait_ge(loaded, 16)
            freq = chip.const[:, C_FREQ:C_FREQ + 4]
            for axis in range(2):
                dve.tensor_tensor(ang[:, :, 4 * axis:4 * axis + 4],
                                  pos[:, :, axis:axis + 1].to_broadcast([P, NT, 4]),
                                  freq.unsqueeze(1).to_broadcast([P, NT, 4]), ALU.mult)
            dve.drain()
            for i, (table, shift, sign) in enumerate(((chip.rot_sin, 0.0, -1.0), (chip.rot_cos, 0.25, 1.0))):
                dve.tensor_scalar(turns[:, :, :], ang[:, :, :], float(1 / (2 * np.pi)), shift, ALU.mult, ALU.add)
                dve.drain()
                dve.tensor_scalar(turns[:, :, :], turns[:, :, :], MAGIC, MAGIC, ALU.add, ALU.subtract)
                dve.drain()
                if i:
                    dve.wait_ge(taken, i)
                dve.scalar_tensor_tensor(red[:, :, :], turns[:, :, :], -TWO_PI_HI, ang[:, :, :], ALU.mult, ALU.add)
                dve.drain()
                dve.scalar_tensor_tensor(red[:, :, :], turns[:, :, :], -TWO_PI_LO, red[:, :, :], ALU.mult, ALU.add)
                dve.drain()
                if shift:
                    dve.tensor_scalar(red[:, :, :], red[:, :, :], float(np.pi / 2), None, ALU.add)
                    dve.drain()
                dve.tensor_scalar(red[:, :, :], red[:, :, :], -pi_floor, pi_floor, ALU.max, ALU.min)
                dve.drain().then_inc(reduced, 1)
                dve.wait_ge(taken, i + 1)
                pairs = table[:, :, :].rearrange("p n (f two) -> p n f two", two=2)
                dve.tensor_scalar(pairs[:, :, :, 0], pairs[:, :, :, 1], sign, None, ALU.mult)


def attention_narrow(nc, chip, wq_dram, wk_dram, wv_dram, wo_dram, ctx_dram=None, bias_dram=None,
                     fside_dram=None):
    cross = ctx_dram is not None
    tag = "y" if cross else "c"
    KC = CC if cross else DC
    KVH = NH if cross else 8
    KW = KVH * HW
    KB = NH // 2 if cross else KVH
    SCALE = 0.25
    PTS = 2

    c = ExitStack()
    if cross:
        rotary_tables(nc, chip, c, fside_dram)
    chip.sequence_buffers(c, tag)
    sb = lambda name, shape, dt=FP32: c.enter_context(nc.sbuf_tensor(f"{name}_{tag}", shape, dt))
    wq, wo = sb("wq", [P, DC, DIM]), sb("wo", [P, DC, DIM])
    wk, wv = sb("wk", [P, KC, KW]), sb("wv", [P, KC, KW])
    qT, kT = sb("qT", [P, 2, NH // 2, SEQ], FP32R), sb("kT", [P, 2, KB, SEQ], FP32R)
    v = sb("v", [P, 2, TILES, KVH, VW])
    parts = sb("parts", [P, 2, NH, 4 * HW])
    rot, turn = sb("rot", [P, DIM]), sb("turn", [P, DIM])
    mx, neg_hl = sb("mx", [P, TILES, NH]), sb("neg_hl", [P, TILES, 2, 2, NH])
    negT = sb("negT", [P, 2, SEQ], FP32R)
    select = sb("select", [P, NH], FP32R)
    probsT = sb("probsT", [P, PTS, 2 * SEQ])
    heads = sb("heads", [P, NH // 4, SEQ])
    rden = sb("rden", [P, NH // 2])
    heads_n = sb("heads_n", [P, TILES, DIM])
    scratch, tick = sb("scratch", [P, P]), sb("tick", [P, 1])
    if cross:
        ctx_sb, ctxT = sb("ctx", [P, TILES, CTX_DIM]), sb("ctxT", [P, CC, SEQ])
        bout = sb("bout", [P, DIM])
        headsT = heads[:, 0:DC, :]
        cos_now, sin_now = sb("cos_now", [P, TILES, HW]), sb("sin_now", [P, TILES, HW])
    else:
        ident16, hide16 = sb("ident16", [P, P], BF16), sb("hide16", [P, P], BF16)
    kv_src = ctxT if cross else chip.xT

    prep, score, scoreT, hbank = chip.bank[0:2], chip.bank[2:4], chip.bank[4:6], chip.bank[6:8]

    KU = KB // 4
    QU = NH // 2 // 4
    A_USES = ([("xT0", "act"), ("xT1", "act")] + ([("ctxT", "act")] if cross else [])
              + [("k0", "dve"), ("k1", "dve"), ("v0", "act"), ("v1", "act")]
              + [(f"kT0{n}", "act") for n in range(KU)] + [("q0", "dve")]
              + [(f"kT1{n}", "act") for n in range(KU)] + [("q1", "dve")]
              + [(f"qT{t}{n}", "act") for t in range(TILES) for n in range(QU)])
    FIN = ([(f"h{n}", "dve") for n in range(4)] + ([("hT0", "act"), ("hT1", "act")] if cross else [])
           + [("out0", "dve"), ("out1", "dve")])
    pad = lambda u: ([("spare", "act")] if len(u) % 2 else [])
    first = A_USES + [("neg", "dve")]
    first = pad(first) + first
    each = A_USES + FIN + [("neg", "dve")]
    each = pad(each) + each
    uses = Uses(first, each)

    with c:
        s = {n: c.enter_context(nc.semaphore(f"{n}_{tag}")) for n in (
            "wq_loaded", "wk_loaded", "wv_loaded", "wo_loaded", "bias_loaded", "consts_ready", "xs_ready",
            "ctx_loaded", "ctx_used", "prep_ready", "prep_act", "prep_dve", "split",
            "scores_ready", "scores_read", "neg_ready", "scoresT_ready", "exp_ready", "values_ready",
            "heads_ready", "heads_copied", "x_ready", "out_read", "rot_ready")}
        block = c.enter_context(nc.Block())

        def nxt(batch):
            return 0 if batch is None else batch + 1

        @block.sync
        def _(sp):
            sp.dma_start(wk[:, :, :], wk_dram.rearrange("(c p) n -> p c n", p=P)).then_inc(s["wk_loaded"], 16)
            sp.dma_start(wq[:, :, :], wq_dram.rearrange("(c p) n -> p c n", p=P)).then_inc(s["wq_loaded"], 16)
            sp.dma_start(wv[:, :, :], wv_dram.rearrange("(c p) n -> p c n", p=P)).then_inc(s["wv_loaded"], 16)
            if cross:
                sp.dma_start(ctx_sb[:, :, :], ctx_dram[0, :, :].rearrange("(t p) d -> p t d", p=P))\
                  .then_inc(s["ctx_loaded"], 16)
            sp.dma_start(wo[:, :, :], wo_dram.rearrange("(c p) n -> p c n", p=P)).then_inc(s["wo_loaded"], 16)
            if cross:
                sp.dma_start(bout[:, :], bias_dram.partition_broadcast(P)).then_inc(s["bias_loaded"], 16)
                with sp.Fori(1, BATCH) as it:
                    sp.wait_ge(s["ctx_used"], it)
                    sp.dma_start(ctx_sb[:, :, :], ctx_dram[bass.ds(it, 1), :, :].rearrange("b (t p) d -> p (b t) d", p=P))\
                      .then_inc(s["ctx_loaded"], 16)
                sp.wait_ge(s["ctx_used"], BATCH)
                sp.dma_start(ctx_sb[:, :, :], ctx_dram[0, :, :].rearrange("(t p) d -> p t d", p=P))\
                  .then_inc(s["ctx_loaded"], 16)
            sp.wait_ge(s["x_ready"], BATCH)

        AFTER = [n for n, _ in A_USES if n not in ("xT0", "xT1", "ctxT")]
        S_AT = 18

        def at_step(h):
            if h == 0:
                return (["spare"] if pad(A_USES + FIN + [0]) else []) + ["xT0", "xT1"] + (["ctxT"] if cross else [])
            n = len(AFTER)
            return AFTER[(h - 1) * n // (S_AT - 1):h * n // (S_AT - 1)] if h < S_AT else []

        def score_step(h):
            return [] if h < S_AT else [2 * (h - S_AT), 2 * (h - S_AT) + 1]

        @block.tensor
        def _(pe):
            def claim(name, batch):
                free = uses.before(name, batch)
                if free:
                    pe.wait_ge(s[f"prep_{free[0]}"], free[1])
                return prep[uses.place(name, batch)[0]]

            def read(name, batch):
                _, _, engine, n = uses.place(name, batch)
                pe.wait_ge(s[f"prep_{engine}"], n)

            def prepare(name, batch, par):
                n = nxt(batch)
                b = claim(name, batch)
                if name == "spare":
                    last = pe.transpose(b[:, 0:P], chip.ident, chip.ident)
                elif name in ("xT0", "xT1"):
                    if name == "xT0":
                        pe.wait_ge(s["xs_ready"], n + 1)
                    j = int(name[2])
                    for i in range(4):
                        cc, t = 2 * j + i // 2, i % 2
                        last = pe.transpose(b[:, P * i:P * i + P], chip.xs[:, t, cc * P:(cc + 1) * P], chip.ident)
                elif name == "ctxT":
                    pe.wait_ge(s["ctx_loaded"], 16 * (n + 1))
                    for i in range(4):
                        cc, t = i // 2, i % 2
                        last = pe.transpose(b[:, P * i:P * i + P], ctx_sb[:, t, cc * P:(cc + 1) * P], chip.ident)
                    pe.drain().then_inc(s["ctx_used"], 1)
                elif name[0] in "qkv" and name[1] != "T":
                    t = int(name[1])
                    if name == "k0":
                        read("xT1", batch)
                        if cross:
                            read("ctxT", batch)
                        if batch is None:
                            pe.wait_ge(s["wk_loaded"], 16)
                            pe.wait_ge(s["wv_loaded"], 16)
                            pe.wait_ge(s["wq_loaded"], 16)
                    w, src, chunks = {"q": (wq, chip.xT, DC), "k": (wk, kv_src, KC), "v": (wv, kv_src, KC)}[name[0]]
                    width = DIM if name[0] == "q" else KW
                    for cc in range(chunks):
                        last = pe.matmul(b[:, 0:width], src[:, cc, t * P:(t + 1) * P], w[:, cc, :],
                                         start=(cc == 0), stop=(cc == chunks - 1))
                elif name[0:2] in ("qT", "kT"):
                    k = name[0] == "k"
                    t, n4 = int(name[2]), int(name[3])
                    pe.wait_ge(s["split"], 4 * n + (0 if k else 2) + t + 1)
                    flat_parts = parts[:, t, :, :].rearrange("p h w -> p (h w)")
                    for i in range(4):
                        blk = 4 * n4 + i
                        last = pe.transpose(b[:, P * i:P * (i + 1)], flat_parts[:, P * blk:P * (blk + 1)], chip.ident)
                elif name == "neg":
                    pe.wait_ge(s["neg_ready"], n + 1)
                    for t in range(TILES):
                        last = pe.transpose(b[:, t * P:(t + 1) * P],
                                            neg_hl[:, t, :, :, :].rearrange("p a b h -> p (a b h)"), chip.ident)
                last.then_inc(s["prep_ready"], 1)

            def first_scores(h, batch, par):
                n = nxt(batch)
                if h == 0:
                    read(f"qT1{QU - 1}", batch)
                if h >= 2:
                    pe.wait_ge(s["scores_read"], n * NH + h - 1)
                r = 64 * (h % 2)
                kb = h // 2 if cross else h // 4
                for t in range(TILES):
                    last = pe.matmul(score[h % 2][:, t * SEQ:(t + 1) * SEQ], qT[r:r + 64, par, h // 2, t * P:(t + 1) * P],
                                     kT[r:r + 64, par, kb, :], start=True, stop=True)
                last.then_inc(s["scores_ready"], 1)

            def second_scores(h, batch, par):
                if h == 0:
                    pe.wait_ge(s["prep_dve"], uses.count(uses.first, "dve") + batch * uses.count(uses.each, "dve"))
                if h >= 2:
                    pe.wait_ge(s["exp_ready"], batch * NH + h - 1)
                r = 64 * (h % 2)
                kb = h // 2 if cross else h // 4
                b = scoreT[h % 2]
                for k in range(TILES):
                    dst = b[:, k * SEQ:(k + 1) * SEQ]
                    pe.matmul(dst, kT[r:r + 64, par, kb, k * P:(k + 1) * P], qT[r:r + 64, par, h // 2, :],
                              start=True, stop=False, skip_group_check=True)
                    last = pe.matmul(dst, select[r:r + 64, h:h + 1].to_broadcast([64, P]), negT[r:r + 64, par, :],
                                     start=False, stop=cross, skip_group_check=True)
                    if not cross:
                        last = pe.matmul(b[:, k * SEQ + k * P:k * SEQ + (k + 1) * P], ident16[:, :], hide16[:, :],
                                         start=False, stop=True, skip_group_check=True)
                last.then_inc(s["scoresT_ready"], 1)

            def values(h, batch, par):
                pe.wait_ge(s["exp_ready"], batch * NH + h + 1)
                if h % 8 == 0 and h >= 16:
                    pe.wait_ge(s["heads_copied"], batch * 4 + h // 8 - 1)
                r = VW * (h % 4)
                b = hbank[h // 8 % 2]
                col = h // 4 % 2 * SEQ
                kh = h if cross else h // 4
                for k in range(TILES):
                    q0 = 0 if cross else k * P
                    last = pe.matmul(b[r:r + VW, col + q0:col + SEQ], v[:, par, k, kh, :],
                                     probsT[:, h % PTS, k * SEQ + q0:(k + 1) * SEQ],
                                     start=(k == 0), stop=(k == TILES - 1), skip_group_check=True)
                last.then_inc(s["values_ready"], 1)
                if h % 8 == 7:
                    pe.drain().then_inc(s["heads_ready"], 1)

            def finish(name, batch):
                if name == "h0":
                    pe.wait_ge(s["heads_copied"], batch * 4 + 4)
                b = claim(name, batch)
                n = int(name[-1])
                if name[:-1] == "h":
                    t = n // 2
                    for i in range(4):
                        last = pe.transpose(b[:, P * i:P * (i + 1)], heads[:, 4 * (n % 2) + i, t * P:(t + 1) * P], chip.ident)
                elif name[:-1] == "hT":
                    read("h3", batch)
                    for i in range(4):
                        cc, t = 2 * n + i // 2, i % 2
                        last = pe.transpose(b[:, P * i:P * (i + 1)], heads_n[:, t, cc * P:(cc + 1) * P], chip.ident)
                else:
                    read("hT1" if cross else "h3", batch)
                    for i in range(DC):
                        if cross:
                            a = headsT[:, i, n * P:(n + 1) * P]
                        else:
                            a = heads_n[:, i % 2, 2 * n * P + i // 2:2 * (n + 1) * P:2]
                        last = pe.matmul(b[:, :], a, wo[:, i, :], start=(i == 0), stop=(i == DC - 1))
                last.then_inc(s["prep_ready"], 1)

            pe.wait_ge(s["consts_ready"], 1)
            for name, _ in uses.first[:-1]:
                prepare(name, None, 0)
            for h in range(NH):
                first_scores(h, None, 0)
            prepare("neg", None, 0)
            pe.wait_ge(s["wo_loaded"], 16)
            with pe.Fori(0, BATCH // 2) as pair:
                for par in range(2):
                    batch = pair * 2 + par
                    for h in range(NH):
                        second_scores(h, batch, par)
                        for name in at_step(h):
                            prepare(name, batch, 1 - par)
                        for hh in score_step(h):
                            first_scores(hh, batch, 1 - par)
                        if h >= 1:
                            values(h - 1, batch, par)
                    values(NH - 1, batch, par)
                    rest = 2 * (NH - S_AT)
                    finish("h0", batch)
                    finish("h1", batch)
                    first_scores(rest, batch, 1 - par)
                    finish("h2", batch)
                    finish("h3", batch)
                    first_scores(rest + 1, batch, 1 - par)
                    first_scores(rest + 2, batch, 1 - par)
                    if cross:
                        finish("hT0", batch)
                        finish("hT1", batch)
                    first_scores(rest + 3, batch, 1 - par)
                    finish("out0", batch)
                    finish("out1", batch)
                    prepare("neg", batch, 1 - par)

        @block.scalar
        def _(act):
            copy = lambda dst, src: act.activation(dst, src, ACT.Copy)
            flat = lambda a: a.rearrange("p a b -> p (a b)")

            def take(name, batch):
                bank, ready, _, _ = uses.place(name, batch)
                act.wait_ge(s["prep_ready"], ready)
                return prep[bank]

            def prepare(name, batch, par):
                n = nxt(batch)
                if name == "xT0":
                    if batch is None:
                        copy(chip.xs[:, :, :], chip.x[:, 0:TILES, :]).then_inc(s["xs_ready"], 1)
                    else:
                        copy(chip.xs[:, :, :], chip.x[:, bass.ds(batch * TILES + TILES, TILES), :])\
                            .then_inc(s["xs_ready"], 1)
                b = take(name, batch)
                if name == "spare":
                    last = copy(scratch[:, 0:P], b[:, 0:P])
                elif name in ("xT0", "xT1"):
                    j = int(name[2])
                    last = copy(flat(chip.xT[:, 2 * j:2 * j + 2, :]), b[:, :])
                elif name == "ctxT":
                    last = copy(flat(ctxT[:, :, :]), b[:, :])
                elif name in ("v0", "v1"):
                    last = copy(v[:, par, int(name[1]), :, 0:HW], b[:, 0:KW].rearrange("p (h w) -> p h w", w=HW))
                else:
                    t, n = int(name[2]), int(name[3])
                    dst = (kT if name[0] == "k" else qT)[:, par, 4 * n:4 * n + 4, t * P:(t + 1) * P]
                    last = copy(dst, b[:, :].rearrange("p (g q) -> p g q", g=4))
                last.then_inc(s["prep_act"], 1)

            def is_act(name):
                return dict(uses.each + uses.first)[name] == "act"

            act.wait_ge(s["consts_ready"], 1)
            for name, e in uses.first:
                if e == "act":
                    prepare(name, None, 0)
            with act.Fori(0, BATCH // 2) as pair:
                for par in range(2):
                    batch = pair * 2 + par
                    for h in range(NH):
                        act.wait_ge(s["scoresT_ready"], batch * NH + h + 1)
                        if h >= PTS:
                            act.wait_ge(s["values_ready"], batch * NH + h - PTS + 1)
                        act.activation(probsT[:, h % PTS, :], scoreT[h % 2][:, :], ACT.Exp, scale=SCALE)\
                           .then_inc(s["exp_ready"], 1)
                        for name in at_step(h):
                            if is_act(name):
                                prepare(name, batch, 1 - par)
                        if h % 8 == 1 and h > 1:
                            g = h // 8 - 1
                            act.wait_ge(s["heads_ready"], batch * 4 + g + 1)
                            copy(flat(heads[:, 2 * g:2 * g + 2, :]), hbank[g % 2][:, :]).then_inc(s["heads_copied"], 1)
                    act.wait_ge(s["heads_ready"], batch * 4 + 4)
                    copy(flat(heads[:, 6:8, :]), hbank[1][:, :]).then_inc(s["heads_copied"], 1)
                    if cross:
                        for n in range(2):
                            b = take(f"hT{n}", batch)
                            copy(flat(headsT[:, 2 * n:2 * n + 2, :]), b[:, :]).then_inc(s["prep_act"], 1)

        @block.vector
        def _(dve):
            def take(name, batch):
                bank, ready, _, _ = uses.place(name, batch)
                dve.wait_ge(s["prep_ready"], ready)
                return prep[bank]

            def rotate(name, batch, par):
                t = int(name[1])
                q = name[0] == "q"
                if q:
                    dve.wait_ge(s["prep_ready"], uses.place(f"kT{t}{KU - 1}", batch)[1])
                heads_ = NH if q else KVH
                width = heads_ * HW
                b = take(name, batch)[:, 0:width].rearrange("p (h w) -> p h w", w=HW)
                if cross:
                    cos, sin = cos_now[:, t, :], sin_now[:, t, :]
                else:
                    cos = chip.const[:, C_COS + HW * t:C_COS + HW * (t + 1)]
                    sin = chip.const[:, C_SIN + HW * t:C_SIN + HW * (t + 1)]
                wide = lambda a, n: a.unsqueeze(1).to_broadcast([P, heads_, n])
                r = rot[:, 0:width].rearrange("p (h w) -> p h w", w=HW)
                u = turn[:, 0:width].rearrange("p (h w) -> p h w", w=HW)
                dve.tensor_tensor(r, b, wide(cos, HW), ALU.mult)
                for i in range(2):
                    mine, other = ((slice(i, HW, 2), slice(1 - i, HW, 2)) if cross else
                                   (slice(8 * i, 8 * i + 8), slice(8 - 8 * i, 16 - 8 * i)))
                    last = dve.tensor_tensor(u[:, :, mine], b[:, :, other], wide(sin[:, mine], 8), ALU.mult)
                last.then_inc(s["prep_dve"], 1)
                dve.drain()
                dve.tensor_tensor(r, r, u, ALU.add)
                dve.drain()
                flat_parts = parts[:, t, :, :].rearrange("p h w -> p (h w)")
                if q:
                    d = parts[:, t, :, :].rearrange("p h (r l w) -> p l h r w", r=2, l=2)
                    hi, lo = [d[:, 0]], [d[:, 1]]
                elif cross:
                    d = parts[:, t, :, :].rearrange("p h (l r w) -> p l h r w", r=2, l=2)
                    hi, lo = [d[:, 0]], [d[:, 1]]
                else:
                    d = flat_parts[:, 0:KVH * P].rearrange("p (h c l r w) -> p l c h r w", c=2, r=2, l=2, w=HW)
                    hi, lo = [d[:, 0, 0], d[:, 0, 1]], [d[:, 1, 0], d[:, 1, 1]]
                twice = lambda a: a.unsqueeze(2).to_broadcast([P, heads_, 2, HW])
                for o in hi:
                    dve.tensor_copy(o.bitcast(FP32R), twice(r))
                dve.drain()
                for o in lo:
                    last = dve.tensor_tensor(o, twice(r), hi[0], ALU.subtract)
                last.then_inc(s["split"], 1)
                dve.drain()

            def prepare(name, batch, par):
                n = nxt(batch)
                if name == "k0" and cross:
                    first_tile = (batch + 1) * TILES if batch is not None else 0
                    dve.tensor_copy(cos_now[:, :, :], chip.rot_cos[:, bass.ds(first_tile, TILES), :])
                    dve.tensor_copy(sin_now[:, :, :], chip.rot_sin[:, bass.ds(first_tile, TILES), :])
                    dve.drain()
                if name[0] in "qk":
                    rotate(name, batch, par)
                else:
                    b = take(name, batch)
                    dve.tensor_copy(negT[:, par, :], b[:, 0:SEQ]).then_inc(s["prep_dve"], 1)

            def maxima(h, batch):
                n = nxt(batch)
                dve.wait_ge(s["scores_ready"], n * NH + h + 1)
                b = score[h % 2]
                if cross:
                    dve.tensor_reduce(mx[:, :, h], b[:, :].rearrange("p (t k) -> p t k", t=TILES), AX.X, ALU.max)\
                       .then_inc(s["scores_read"], 1)
                else:
                    dve.memset(tick[:, :], 0.0)
                    for t in range(TILES):
                        nk = (t + 1) * P
                        at_ = C_OWN if t == 0 else C_CAUSAL
                        dve.tensor_tensor_reduce(out=scratch2[t][:, 0:nk], in0=b[:, t * SEQ:t * SEQ + nk],
                                                 in1=chip.const[:, at_:at_ + nk], scale=1.0, scalar=FLOOR,
                                                 op0=ALU.add, op1=ALU.max, accum_out=mx[:, t, h:h + 1])
                    dve.drain().then_inc(s["scores_read"], 1)

            def negate():
                dve.drain()
                hi, lo = neg_hl[:, :, :, 0, :], neg_hl[:, :, :, 1, :]
                twice = mx[:, :, :].unsqueeze(2).to_broadcast([P, TILES, 2, NH])
                dve.tensor_scalar(mx[:, :, :], mx[:, :, :], -1.0, None, ALU.mult)
                dve.drain()
                dve.tensor_copy(hi.bitcast(FP32R), twice)
                dve.drain()
                dve.tensor_tensor(lo, twice, hi, ALU.subtract)
                dve.drain().then_inc(s["neg_ready"], 1)

            def is_dve(name):
                return dict(uses.each + uses.first)[name] == "dve"

            scratch2 = [rot, turn]
            dve.memset(v[:, :, :, :, :].rearrange("p a t h w -> p (a t h) w")[:, :, HW:HW + 1], 1.0)
            dve.memset(v[:, :, :, :, :].rearrange("p a t h w -> p (a t h) w")[:, :, HW + 1:], 0.0)
            for r in (0, 64):
                for i in (0, NH):
                    dve.tensor_copy(select[r + i:r + i + NH, :], chip.const[r + i:r + i + NH, C_ID + r + i:C_ID + r + i + NH])
            if not cross:
                dve.tensor_copy(ident16[:, :], chip.ident)
                dve.tensor_copy(hide16[:, :], chip.const[:, C_OWN_T:C_OWN_T + P])
            dve.drain().then_inc(s["consts_ready"], 1)
            for name, e in uses.first[:-1]:
                if e == "dve":
                    prepare(name, None, 0)
            for h in range(NH):
                maxima(h, None)
            negate()
            prepare("neg", None, 0)
            if cross:
                dve.wait_ge(s["bias_loaded"], 16)
            with dve.Fori(0, BATCH // 2) as pair:
                for par in range(2):
                    batch = pair * 2 + par
                    for h in range(NH):
                        for name in at_step(h):
                            if is_dve(name):
                                prepare(name, batch, 1 - par)
                        for hh in score_step(h):
                            maxima(hh, batch)
                    rest = 2 * (NH - S_AT)

                    def normalise(n):
                        b = take(f"h{n}", batch)[:, :].rearrange("p (h w) -> p h w", w=VW)
                        dve.reciprocal(rden[:, :], b[:, :, HW])
                        dve.drain()
                        t = n // 2
                        dst = heads_n[:, t, 256 * (n % 2):256 * (n % 2) + 256].rearrange("p (h w) -> p h w", w=HW)
                        dve.tensor_tensor(dst, b[:, :, 0:HW], rden[:, :].unsqueeze(2).to_broadcast([P, NH // 2, HW]),
                                          ALU.mult).then_inc(s["prep_dve"], 1)
                        dve.drain()

                    normalise(0)
                    normalise(1)
                    maxima(rest, batch)
                    normalise(2)
                    normalise(3)
                    for i in range(1, 4):
                        maxima(rest + i, batch)
                    negate()
                    for t in range(TILES):
                        b = take(f"out{t}", batch)
                        dve.tensor_tensor(chip.res[:, t, :], b[:, :], chip.x[:, bass.ds(batch * TILES + t, 1), :],
                                          ALU.add).then_inc(s["prep_dve"], 1)
                    prepare("neg", batch, 1 - par)
                    dve.drain()
                    if cross:
                        dve.tensor_tensor(chip.res[:, :, :], chip.res[:, :, :],
                                          bout[:, :].unsqueeze(1).to_broadcast([P, TILES, DIM]), ALU.add)
                        dve.drain()
                    ln_rows(dve, chip, batch, s)

INTER = 2048
MC = INTER // P
BLOCK = 2
NBLOCK = MC // BLOCK
GROUP = 512
NGROUP = NTILE * P // GROUP
GT = GROUP // P


def hadamard_inputs(nc, chip, y_hi, y_lo, down, sign_up_dram, down_dram, scale_down_dram):
    with ExitStack() as c:
        sb = lambda name, shape: c.enter_context(nc.sbuf_tensor(name, shape, FP32))
        rows = sb("down_rows", [P, DC, INTER])
        sign, scale = sb("sign_up", [P, DC]), sb("scale_down", [P, DC])
        half = sb("half_turned", [P, DC, SEQ])
        chip.sequence_buffers(c, "h")
        xs, xT = chip.xs, chip.xT
        s = {n: c.enter_context(nc.semaphore(f"{n}_h")) for n in (
            "small_loaded", "rows_loaded", "scaled", "ready", "copied", "folded", "xs_ready", "hi_ready", "lo_ready",
            "xT_ready", "xT_copied", "down_ready", "down_copied", "h_ready", "h_copied", "y_ready")}
        turn, had, xbank, ybank = chip.bank[0:2], chip.bank[2:4], chip.bank[4:6], chip.bank[6:8]
        h128 = chip.const[:, C_HAD:C_HAD + P]
        block = c.enter_context(nc.Block())

        @block.sync
        def _(sp):
            with nc.allow_non_contiguous_dma(reason="512 signs and scales onto the partitions"):
                sp.dma_start(sign[:, :], sign_up_dram.rearrange("(c p) -> p c", p=P)).then_inc(s["small_loaded"], 16)
                sp.dma_start(scale[:, :], scale_down_dram.rearrange("(c p) -> p c", p=P)).then_inc(s["small_loaded"], 16)
            for o in range(DC):
                sp.dma_start(rows[:, o, :], down_dram[o * P:(o + 1) * P, :]).then_inc(s["rows_loaded"], 16)
                sp.wait_ge(s["rows_loaded"], 16 * (o + 1))

        @block.tensor
        def _(pe):
            for b in range(BATCH):
                pe.wait_ge(s["xs_ready"], b + 1)
                for j in range(2):
                    if b >= 1:
                        pe.wait_ge(s["xT_copied"], 2 * b - 1 + j)
                    for i in range(4):
                        cc, t = 2 * j + i // 2, i % 2
                        last = pe.transpose(xbank[j][:, P * i:P * i + P], xs[:, t, cc * P:(cc + 1) * P], chip.ident)
                    last.then_inc(s["xT_ready"], 1)
                pe.wait_ge(s["folded"], b + 1)
                for j in range(2):
                    if b >= 1:
                        pe.wait_ge(s["lo_ready"], 2 * b - 1 + j)
                    for i in range(2):
                        last = pe.matmul(ybank[j][:, i * SEQ:(i + 1) * SEQ], h128, half[:, 2 * j + i, :],
                                         start=True, stop=True)
                    last.then_inc(s["y_ready"], 1)
                if b == 0:
                    pe.wait_ge(s["scaled"], DC)
                for m in (2 * b, 2 * b + 1):
                    if m >= 2:
                        pe.wait_ge(s["down_copied"], m - 1)
                    for o in range(DC):
                        last = pe.transpose(turn[m % 2][:, P * o:P * (o + 1)], rows[:, o, m * P:(m + 1) * P], chip.ident)
                    last.then_inc(s["down_ready"], 1)
                for m in (2 * b, 2 * b + 1):
                    pe.wait_ge(s["down_copied"], m + 1)
                    if m >= 2:
                        pe.wait_ge(s["h_copied"], m - 1)
                    pe.matmul(had[m % 2][:, :], h128, down[:, m, :], start=True, stop=True).then_inc(s["h_ready"], 1)

        @block.scalar
        def _(act):
            copy = lambda dst, src, **k: act.activation(dst, src, ACT.Copy, **k)
            act.wait_ge(s["small_loaded"], 32)
            for b in range(BATCH):
                if b >= 1:
                    act.wait_ge(s["xT_ready"], 2 * b)
                copy(xs[:, :, :], chip.x[:, b * TILES:(b + 1) * TILES, :]).then_inc(s["xs_ready"], 1)
                for j in range(2):
                    act.wait_ge(s["xT_ready"], 2 * b + j + 1)
                    for i in range(2):
                        cc = 2 * j + i
                        last = copy(half[:, cc, :], xbank[j][:, i * SEQ:(i + 1) * SEQ], scale=sign[:, cc:cc + 1])
                    last.then_inc(s["xT_copied"], 1)
                if b == 0:
                    for o in range(DC):
                        act.wait_ge(s["rows_loaded"], 16 * (o + 1))
                        copy(rows[:, o, :], rows[:, o, :], scale=scale[:, o:o + 1]).then_inc(s["scaled"], 1)
                for j in range(2):
                    act.wait_ge(s["y_ready"], 2 * b + j + 1)
                    copy(y_hi[:, 2 * j:2 * j + 2, b * SEQ:(b + 1) * SEQ],
                         ybank[j][:, :].rearrange("p (c q) -> p c q", c=2), scale=float(DIM ** -0.5))\
                        .then_inc(s["hi_ready"], 1)
                for m in (2 * b, 2 * b + 1):
                    act.wait_ge(s["down_ready"], m + 1)
                    copy(down[:, m, :], turn[m % 2][:, :]).then_inc(s["down_copied"], 1)
                for m in (2 * b, 2 * b + 1):
                    act.wait_ge(s["h_ready"], m + 1)
                    copy(down[:, m, :], had[m % 2][:, :]).then_inc(s["h_copied"], 1)

        @block.vector
        def _(dve):
            for b in range(BATCH):
                dve.wait_ge(s["xT_copied"], 2 * b + 2)
                near = lambda t: t.rearrange("p (a two) q -> p two a q", two=2)
                far = lambda t: t.rearrange("p (two a) q -> p two a q", two=2)
                h, x = near(half[:, :, :]), near(xT[:, :, :])
                dve.tensor_tensor(x[:, 0], h[:, 0], h[:, 1], ALU.add)
                dve.tensor_tensor(x[:, 1], h[:, 0], h[:, 1], ALU.subtract)
                dve.drain()
                h, x = far(half[:, :, :]), far(xT[:, :, :])
                dve.tensor_tensor(h[:, 0], x[:, 0], x[:, 1], ALU.add)
                dve.tensor_tensor(h[:, 1], x[:, 0], x[:, 1], ALU.subtract)
                dve.drain().then_inc(s["folded"], 1)
                for j in range(2):
                    dve.wait_ge(s["hi_ready"], 2 * b + j + 1)
                    dve.scalar_tensor_tensor(
                        y_lo[:, 2 * j:2 * j + 2, b * SEQ:(b + 1) * SEQ],
                        ybank[j][:, :].rearrange("p (c q) -> p c q", c=2), float(DIM ** -0.5),
                        y_hi[:, 2 * j:2 * j + 2, b * SEQ:(b + 1) * SEQ].bitcast(FP32), ALU.mult, ALU.subtract)\
                        .then_inc(s["lo_ready"], 1)
            dve.wait_ge(s["h_copied"], MC)
            other = rows[:, :, :].rearrange("p a (b o) -> p (a b) o", o=DIM)
            a, b = down[:, :, :], other
            for stage in range(4):
                w = 1 << stage
                v = lambda t: t.rearrange("p (g two w) o -> p two g (w o)", two=2, w=w)
                src, dst = v(a), v(b)
                dve.tensor_tensor(dst[:, 0], src[:, 0], src[:, 1], ALU.add)
                dve.tensor_tensor(dst[:, 1], src[:, 0], src[:, 1], ALU.subtract)
                dve.drain()
                a, b = b, a


def hadamard_ffn(nc, chip, sign_up_dram, sign_down_dram, scale_up_dram, scale_down_dram,
                 up_dram, gate_dram, down_dram):
    with ExitStack() as c:
        sb = lambda name, shape, dt=FP32: c.enter_context(nc.sbuf_tensor(name, shape, dt))
        y_hi, y_lo = sb("y_hi", [P, DC, NTILE * P], FP32R), sb("y_lo", [P, DC, NTILE * P], FP32R)
        down = sb("down", [P, MC, DIM])
        hadamard_inputs(nc, chip, y_hi, y_lo, down, sign_up_dram, down_dram, scale_down_dram)

        rows = sb("ug_rows", [P, BLOCK, 2, DIM])
        w_hi, w_lo = (sb(n, [P, 2, DC, 2 * BLOCK, P], FP32R) for n in ("ug_hi", "ug_lo"))
        d_hi, d_lo = (sb(n, [P, BLOCK, DIM], FP32R) for n in ("down_hi", "down_lo"))
        scale_ug, sign_down = sb("scale_ug", [P, 2, MC]), sb("sign_down", [P, MC])
        scale_now, sign_now = sb("scale_now", [P, 2, BLOCK]), sb("sign_now", [P, BLOCK])
        silu, h = sb("silu", [P, GROUP]), sb("h", [P, GROUP])
        h_hi, h_lo = (sb(n, [P, 2, BLOCK, GROUP], FP32R) for n in ("h_hi", "h_lo"))
        s = {n: c.enter_context(nc.semaphore(f"{n}_f")) for n in (
            "small_loaded", "rows_loaded", "rows_used", "scales_ready", "turned", "hi_ready", "lo_ready",
            "gate_ready", "up_ready", "silu_ready", "h_ready", "h_hi_ready", "h_lo_ready", "d_hi_ready",
            "d_lo_ready", "down_ready", "added")}
        turn, gate, up, dbank = chip.bank[0:2], chip.bank[2:4], chip.bank[4:6], chip.bank[6:8]
        block = c.enter_context(nc.Block())
        NA = NGROUP * BLOCK
        ND = NGROUP * GT

        @block.sync
        def _(sp):
            with nc.allow_non_contiguous_dma(reason="scales and signs onto the partitions"):
                sp.dma_start(scale_ug[:, :, :], scale_up_dram.rearrange("(k c p) -> p k c", p=P, k=2))\
                  .then_inc(s["small_loaded"], 16)
                sp.dma_start(sign_down[:, :], sign_down_dram.rearrange("(c p) -> p c", p=P)).then_inc(s["small_loaded"], 16)

            def load(blk):
                for kind, w in enumerate((gate_dram, up_dram)):
                    src = w[bass.ds(blk * (BLOCK * P), BLOCK * P), :].rearrange("(c p) n -> p c n", p=P)
                    sp.dma_start(rows[:, :, kind, :], src).then_inc(s["rows_loaded"], 16)

            load(0)
            with sp.Fori(1, NBLOCK) as blk:
                sp.wait_ge(s["rows_loaded"], 32 * blk)
                sp.wait_ge(s["rows_used"], blk)
                load(blk)
            sp.wait_ge(s["rows_loaded"], 32 * NBLOCK)
            sp.wait_ge(s["rows_used"], NBLOCK)
            load(0)
            sp.wait_ge(s["rows_loaded"], 32 * (NBLOCK + 1))

        @block.tensor
        def _(pe):
            def turn_weights(blk, par, n):
                if n == 0:
                    pe.wait_ge(s["rows_loaded"], 32 * blk + 32)
                if not (isinstance(blk, int) and n < 2):
                    pe.wait_ge(s["lo_ready"], 2 * BLOCK * blk + n - 1)
                for cc in range(DC):
                    last = pe.transpose(turn[n % 2][:, P * cc:P * (cc + 1)],
                                        rows[:, n // 2, n % 2, cc * P:(cc + 1) * P], chip.ident)
                last.then_inc(s["turned"], 1)
                if n == 2 * BLOCK - 1:
                    pe.drain().then_inc(s["rows_used"], 1)

            def gate_up(blk, par, g):
                for m in range(BLOCK):
                    a = g * BLOCK + m
                    for kind, banks, read in ((0, gate, "silu_ready"), (1, up, "h_ready")):
                        if a >= 2:
                            pe.wait_ge(s[read], blk * NA + a - 1)
                        n = 0
                        for w, y in ((w_hi, y_hi), (w_hi, y_lo), (w_lo, y_hi)):
                            for cc in range(DC):
                                last = pe.matmul(banks[m][:, :], w[:, par, cc, 2 * m + kind, :],
                                                 y[:, cc, g * GROUP:(g + 1) * GROUP], start=(n == 0), stop=(n == 11))
                                n += 1
                        last.then_inc(s["up_ready" if kind else "gate_ready"], 1)

            def down_product(blk, par, g):
                pe.wait_ge(s["h_lo_ready"], blk * NA + (g + 1) * BLOCK)
                for t in range(GT):
                    d = g * GT + t
                    pe.wait_ge(s["added"], blk * ND + d + 1)
                    n = 0
                    for hh, dd in ((h_hi, d_hi), (h_hi, d_lo), (h_lo, d_hi)):
                        for m in range(BLOCK):
                            last = pe.matmul(dbank[d % 2][:, :], hh[:, g % 2, m, t * P:(t + 1) * P], dd[:, m, :],
                                             start=(n == 0), stop=(n == 5))
                            n += 1
                    last.then_inc(s["down_ready"], 1)

            for n in range(2 * BLOCK):
                turn_weights(0, 0, n)
            with pe.Fori(0, NBLOCK // 2) as i:
                for par in range(2):
                    blk = 2 * i + par
                    for g in range(NGROUP):
                        turn_weights(blk + 1, 1 - par, g)
                        if g == 0:
                            pe.wait_ge(s["lo_ready"], 2 * BLOCK * blk + 2 * BLOCK)
                        gate_up(blk, par, g)
                        if g == 1:
                            pe.wait_ge(s["d_lo_ready"], blk + 1)
                        if g >= 1:
                            down_product(blk, par, g - 1)
                    down_product(blk, par, NGROUP - 1)

        @block.scalar
        def _(act):
            def split_weights(blk, par, n):
                act.wait_ge(s["turned"], 2 * BLOCK * blk + n + 1)
                act.activation(w_hi[:, par, :, n, :], turn[n % 2][:, :].rearrange("p (c n) -> p c n", c=DC), ACT.Copy)\
                   .then_inc(s["hi_ready"], 1)

            for n in range(2 * BLOCK):
                split_weights(0, 0, n)
            with act.Fori(0, NBLOCK // 2) as i:
                for par in range(2):
                    blk = 2 * i + par
                    for g in range(NGROUP):
                        split_weights(blk + 1, 1 - par, g)
                        if g == 0:
                            act.wait_ge(s["scales_ready"], blk + 1)
                        for m in range(BLOCK):
                            a = g * BLOCK + m
                            act.wait_ge(s["gate_ready"], blk * NA + a + 1)
                            act.activation(silu[:, :], gate[m][:, :], ACT.Silu, scale=scale_now[:, 1, m:m + 1])\
                               .then_inc(s["silu_ready"], 1)
                            act.wait_ge(s["h_ready"], blk * NA + a + 1)
                            act.activation(h_hi[:, g % 2, m, :], h[:, :], ACT.Copy).then_inc(s["h_hi_ready"], 1)

        @block.vector
        def _(dve):
            def split_weights(blk, par, n):
                dve.wait_ge(s["hi_ready"], 2 * BLOCK * blk + n + 1)
                dve.tensor_tensor(w_lo[:, par, :, n, :], turn[n % 2][:, :].rearrange("p (c n) -> p c n", c=DC),
                                  w_hi[:, par, :, n, :].bitcast(FP32), ALU.subtract).then_inc(s["lo_ready"], 1)

            def add_down(blk, g):
                for t in range(GT):
                    d = g * GT + t
                    dve.wait_ge(s["down_ready"], blk * ND + d + 1)
                    dve.tensor_tensor(chip.x[:, d, :], chip.x[:, d, :], dbank[d % 2][:, :], ALU.add)\
                       .then_inc(s["added"], 1)

            dve.drain().then_inc(s["added"], 2)
            dve.wait_ge(s["small_loaded"], 32)
            dve.tensor_scalar(sign_down[:, :], sign_down[:, :], float(INTER ** -0.5), None, ALU.mult)
            dve.drain()
            for n in range(2 * BLOCK):
                split_weights(0, 0, n)
            with dve.Fori(0, NBLOCK // 2) as i:
                for par in range(2):
                    blk = 2 * i + par
                    dve.tensor_copy(scale_now[:, :, :], scale_ug[:, :, bass.ds(blk * BLOCK, BLOCK)])
                    dve.tensor_copy(sign_now[:, :], sign_down[:, bass.ds(blk * BLOCK, BLOCK)])
                    dve.drain().then_inc(s["scales_ready"], 1)
                    for m in range(BLOCK):
                        rows_m = down[:, bass.ds(blk * BLOCK + m, 1), :]
                        dve.tensor_scalar(d_hi[:, m:m + 1, :], rows_m, sign_now[:, m:m + 1], None, ALU.mult)
                        dve.drain()
                        dve.scalar_tensor_tensor(d_lo[:, m:m + 1, :], rows_m, sign_now[:, m:m + 1],
                                                 d_hi[:, m:m + 1, :].bitcast(FP32), ALU.mult, ALU.subtract)
                    dve.drain().then_inc(s["d_lo_ready"], 1)
                    for g in range(NGROUP):
                        split_weights(blk + 1, 1 - par, g)
                        for m in range(BLOCK):
                            a = g * BLOCK + m
                            dve.wait_ge(s["silu_ready"], blk * NA + a + 1)
                            dve.wait_ge(s["up_ready"], blk * NA + a + 1)
                            dve.scalar_tensor_tensor(h[:, :], up[m][:, :], scale_now[:, 0, m:m + 1], silu[:, :],
                                                     ALU.mult, ALU.mult).then_inc(s["h_ready"], 1)
                            dve.wait_ge(s["h_hi_ready"], blk * NA + a + 1)
                            dve.tensor_tensor(h_lo[:, g % 2, m, :], h[:, :], h_hi[:, g % 2, m, :].bitcast(FP32),
                                              ALU.subtract).then_inc(s["h_lo_ready"], 1)
                            dve.drain()
                        if g >= 1:
                            add_down(blk, g - 1)
                    add_down(blk, NGROUP - 1)


def last_norm(nc, chip, out_dram):
    NT = 4
    with ExitStack() as c:
        sb = lambda name, shape: c.enter_context(nc.sbuf_tensor(name, shape, FP32))
        stat, agg = sb("last_stat", [P, NTILE, 6]), sb("last_agg", [P, NTILE, 2])
        var, rstd, newton = sb("last_var", [P, NTILE]), sb("last_rstd", [P, NTILE]), sb("last_newton", [P, NTILE])
        done, stored = c.enter_context(nc.semaphore("rows_done")), c.enter_context(nc.semaphore("rows_stored"))
        block = c.enter_context(nc.Block())

        @block.sync
        def _(sp):
            out = out_dram.rearrange("b (t p) d -> p (b t) d", p=P)
            for i in range(NTILE // NT):
                sp.wait_ge(done, i + 1)
                sp.dma_start(out[:, i * NT:(i + 1) * NT, :], chip.x[:, i * NT:(i + 1) * NT, :]).then_inc(stored, 16)
            sp.wait_ge(stored, 16 * (NTILE // NT))

        @block.vector
        def _(dve):
            for i in range(NTILE // NT):
                r = slice(i * NT, (i + 1) * NT)
                for t in range(i * NT, (i + 1) * NT):
                    dve.bn_stats(stat[:, t, :], chip.x[:, t, :])
                dve.drain()
                for t in range(i * NT, (i + 1) * NT):
                    dve.bn_aggr(agg[:, t, :], stat[:, t, :])
                dve.drain()
                rsqrt(dve, rstd[:, r], agg[:, r, 1], var[:, r], newton[:, r])
                for t in range(i * NT, (i + 1) * NT):
                    last = dve.tensor_scalar(chip.x[:, t, :], chip.x[:, t, :], agg[:, t, 0:1], rstd[:, t:t + 1],
                                             ALU.subtract, ALU.mult)
                last.then_inc(done, 1)

def decoder(nc, x, ctx_1024, fside, mask, const, a0_wq, a0_wk, a0_wv, a0_wo, x0_wq, x0_wk, x0_wv, x0_wo,
            gate_w, ffn_w, atoms, mix, importance, mask_idx, a1_wq, a1_wk, a1_wv, a1_wo,
            x1_wq, x1_wkv, x1_wout, x1_bout, su_ug, su_dp, ws_ug, ws_dp, w_up, w_gate, w_down, out):
    with ExitStack() as ctx:
        chip = Chip(nc, ctx)
        with ExitStack() as c:
            table = ExpertTable(nc, c)
            weights = WideWeights(nc, c, "s", 4, DC)
            start(nc, chip, x, const, table, atoms, mix, importance, mask_idx,
                  lambda sp: weights.load(sp, a0_wq, a0_wk, a0_wv, a0_wo))
            attention_wide(nc, chip, weights, 4, 1 / 128, pool_work=table.add_sets)
        with ExitStack() as c:
            weights = WideWeights(nc, c, "x", 8, CC)
            attention_wide(nc, chip, weights, 8, float(np.float32(1) / np.sqrt(np.float32(128))),
                           (x0_wq, x0_wk, x0_wv, x0_wo), ctx_1024, mask)
        experts(nc, chip, table, gate_w, ffn_w)
        attention_narrow(nc, chip, a1_wq, a1_wk, a1_wv, a1_wo)
        attention_narrow(nc, chip, x1_wq, x1_wkv[:, 0:DIM], x1_wkv[:, DIM:], x1_wout, ctx_1024, x1_bout, fside)
        hadamard_ffn(nc, chip, su_ug, su_dp, ws_ug, ws_dp, w_up, w_gate, w_down)
        last_norm(nc, chip, out)


_INS = ['x', 'ctx_1024', 'fside_BxSx2_0', 'mask_BxS2_bf1', 'const', 'L0_attn_Wq', 'L0_attn_Wk', 'L0_attn_Wv', 'L0_attn_Wo',
        'L0_xattn_Wq', 'L0_xattn_Wk', 'L0_xattn_Wv', 'L0_xattn_Wo', 'L0_ffn_gate_w', 'L0_ffn_W', 'L0_ffn_atoms',
        'L0_ffn_expert_atom_weights', 'L0_ffn_importance', 'L0_ffn_mask_idx', 'L1_attn_Wq', 'L1_attn_Wk', 'L1_attn_Wv',
        'L1_attn_Wo', 'L1_xattn_Wq', 'L1_xattn_Wkv', 'L1_xattn_Wout', 'L1_xattn_bout', 'L1_ffn_SU_ug', 'L1_ffn_SU_dp',
        'L1_ffn_Wscale_ug', 'L1_ffn_Wscale_dp', 'L1_ffn_W_up', 'L1_ffn_W_gate', 'L1_ffn_W_down']


def kernel(**inputs):
    import concourse.bacc as _bacc
    from concourse.bass_utils import run_bass_kernel_spmd as _run

    nc = _bacc.Bacc("TRN2", target_bir_lowering=False, num_devices=1)
    arrays, args = {}, []
    for name in _INS:
        a = constants() if name == 'const' else np.ascontiguousarray(inputs[name])
        arrays[f"in_{name}"] = a
        args.append(nc.dram_tensor(f"in_{name}", a.shape, mybir.dt.from_np(a.dtype), kind="ExternalInput").ap())
    args.append(nc.dram_tensor("out_0", (BATCH, SEQ, DIM), FP32, kind="ExternalOutput").ap())
    decoder(nc, *args)
    r = _run(nc, [arrays], core_ids=[0])
    return r.results[0]["out_0"]
```

```python
import numpy as np
import concourse.bass as bass
from concourse import mybir
from contextlib import ExitStack

FP32 = mybir.dt.float32
INT32 = mybir.dt.int32
FP32R = mybir.dt.float32r
BF16 = mybir.dt.bfloat16
ALU = mybir.AluOpType
ACT = mybir.ActivationFunctionType
AX = mybir.AxisListType

P = 128
BATCH, SEQ, DIM = 8, 256, 512
TILES = SEQ // P
NTILE = BATCH * TILES
DC = DIM // P
CTX_DIM = 256
CC = CTX_DIM // P
EXPERTS, ATOMS, NSPARSE = 8, 64, 4096
HW = 16
SETS = NSPARSE // P
LOW = -1e30
FLOOR = -3e38
EPS = 1e-5

C_ID, C_OWN, C_BAND, C_CAUSAL, C_HAD, C_NHAD, C_COS, C_SIN, C_FREQ, C_RANK, C_BEFORE, C_SPARE, C_OWN_T, C_SLOT = (
    0, 128, 256, 512, 768, 896, 1024, 1056, 1088, 1096, 1112, 1240, 1241, 1369)
C_COLS = C_SLOT + 2 * NTILE + EXPERTS


def constants():
    c = np.zeros((P, C_COLS), np.float32)
    i = np.arange(P)
    c[:, C_ID:C_ID + P] = np.eye(P)
    own = np.where(i[None, :] <= i[:, None], 0.0, LOW)
    prev = np.where(i[None, :] > i[:, None], 0.0, LOW)
    c[:, C_OWN:C_OWN + P] = own
    c[:, C_BAND:C_BAND + P] = prev
    c[:, C_BAND + P:C_BAND + 2 * P] = own
    c[:, C_CAUSAL + P:C_CAUSAL + 2 * P] = own
    h = np.ones((1, 1), np.float32)
    while h.shape[0] < P:
        h = np.block([[h, h], [h, -h]])
    c[:, C_HAD:C_HAD + P] = h
    c[:, C_NHAD:C_NHAD + P] = -h
    half = 8
    inv = (np.float32(1.0) / np.float32(10000.0) ** (np.arange(half, dtype=np.float32) * np.float32(2.0) / np.float32(16))).astype(np.float32)
    pos = np.arange(SEQ, dtype=np.float32).reshape(TILES, P)
    ang = (pos[:, :, None] * inv).astype(np.float32)
    cos, sin = np.cos(ang), np.sin(ang)
    for t in range(TILES):
        c[:, C_COS + 16 * t:C_COS + 16 * t + 16] = np.concatenate([cos[t], cos[t]], 1)
        c[:, C_SIN + 16 * t:C_SIN + 16 * t + 16] = np.concatenate([-sin[t], sin[t]], 1)
    c[:, C_FREQ:C_FREQ + 4] = (np.float32(10000.0) ** (-np.arange(4, dtype=np.float32) / np.float32(4))).astype(np.float32)
    c[:, C_RANK:C_RANK + TILES * EXPERTS] = np.tile(EXPERTS - np.arange(EXPERTS), TILES)
    c[:, C_BEFORE:C_BEFORE + P] = i[None, :] < i[:, None]
    c[:, C_OWN_T:C_OWN_T + P] = own.T
    c[:, C_SPARE] = DIM * DIM + i
    c[:, C_SLOT:] = np.arange(C_COLS - C_SLOT)
    return c


class Chip:

    def __init__(self, nc, ctx):
        sb = lambda name, shape, dt=FP32: ctx.enter_context(nc.sbuf_tensor(name, shape, dt))
        self.nc = nc
        self.x = sb("x_all", [P, NTILE + TILES, DIM])
        self.const = sb("const", [P, C_COLS])
        self.ident = self.const[:, C_ID:C_ID + P]
        self.bank = [ctx.enter_context(nc.psum_tensor(f"bank{i}", [P, 512], FP32)) for i in range(8)]

        ring = lambda name, n: [ctx.enter_context(nc.semaphore(f"{name}{i}")) for i in range(n)]
        self.lo_stored = {tag: ring(f"lo_stored_{tag}", 2) for tag in "sx"}
        self.lo_there = {tag: ring(f"lo_there_{tag}", 2) for tag in "sx"}
        self.products_stored, self.products_back = ring("products_stored", 4), ring("products_back", 2)
        self.set_added, self.rows_sent = (ctx.enter_context(nc.semaphore(n)) for n in ("set_added", "rows_sent"))

    def sequence_buffers(self, ctx, tag, shared=None):
        sb = lambda name, shape: ctx.enter_context(self.nc.sbuf_tensor(f"{name}_{tag}", shape, FP32))
        self.xs = sb("x_static", [P, TILES, DIM])
        if shared is None:
            self.xT = sb("xT", [P, DC, SEQ])
            self.res = sb("residual", [P, TILES, DIM])
        else:
            self.res = shared[:, 0:TILES * DIM // SEQ, :].rearrange("p a b -> p (a b)").rearrange("p (t d) -> p t d", t=TILES)
        self.stat = sb("ln_stats", [P, TILES, 8])
        self.var, self.rstd, self.newton = (sb(n, [P, TILES]) for n in ("ln_var", "ln_rstd", "ln_newton"))


class Carve:

    def __init__(self, buf, size):
        self.buf, self.size, self.at = buf, size, 0

    def __call__(self, *shape):
        n = int(np.prod(shape))
        flat = self.buf[:, self.at:self.at + n]
        self.at += n
        assert self.at <= self.size, self.at
        names = "abcd"[:len(shape)]
        if len(shape) == 1:
            return flat
        return flat.rearrange(f"p ({' '.join(names)}) -> p {' '.join(names)}",
                              **{n_: s for n_, s in zip(names, shape)})


def clear_semaphores(nc, semaphores):
    with nc.Block() as block:
        @block.sync
        def _(sp):
            for sem in semaphores:
                sp.sem_clear(sem)


def ln_vector(dve, chip, out_banks, batch, s, it):
    for t in range(TILES):
        last = dve.tensor_tensor(chip.res[:, t, :], out_banks[t][:, :],
                                 chip.x[:, bass.ds(batch * TILES + t, 1), :], ALU.add)
    last.then_inc(s["out_read"], 1)
    dve.drain()
    ln_rows(dve, chip, batch, s)


def rsqrt(dve, out, variance, var, newton):
    dve.tensor_scalar(var, variance, EPS, None, ALU.add)
    dve.drain()
    dve.tensor_scalar(out.bitcast(INT32), var.bitcast(INT32), -0.5, float(0x5F3759DF), ALU.mult, ALU.add)
    dve.drain()
    for _ in range(3):
        dve.tensor_tensor(newton, out, out, ALU.mult)
        dve.drain()
        dve.scalar_tensor_tensor(newton, newton, -0.5, var, ALU.mult, ALU.mult)
        dve.drain()
        dve.scalar_tensor_tensor(out, newton, 1.5, out, ALU.add, ALU.mult)
        dve.drain()


def ln_rows(dve, chip, batch, s):
    for t in range(TILES):
        dve.bn_stats(chip.stat[:, t, 0:6], chip.res[:, t, :])
    dve.drain()
    for t in range(TILES):
        dve.bn_aggr(chip.stat[:, t, 6:8], chip.stat[:, t, 0:6])
    dve.drain()
    rsqrt(dve, chip.rstd[:, :], chip.stat[:, :, 7], chip.var[:, :], chip.newton[:, :])
    for t in range(TILES):
        last = dve.tensor_scalar(chip.x[:, bass.ds(batch * TILES + t, 1), :], chip.res[:, t, :],
                                 chip.stat[:, t, 6:7], chip.rstd[:, t:t + 1], ALU.subtract, ALU.mult)
    last.then_inc(s["x_ready"], 1)



QCHUNKS = 4


class WideWeights:

    def __init__(self, nc, ctx, tag, groups, kv_chunks):
        sb = lambda name, chunks, width, dt=FP32: ctx.enter_context(nc.sbuf_tensor(f"{name}_{tag}", [P, chunks, width], dt))
        self.wk, self.wv = sb("wk", kv_chunks, groups * P), sb("wv", kv_chunks, groups * P)
        self.wq_hi, self.wo = sb("wq_hi", DC, 16 * P, FP32R), sb("wo", 16, DIM)
        self.wq_whole = self.wo[:, :, :].rearrange("p a b -> p (a b)").rearrange("p (c n) -> p c n", c=DC)
        sem = lambda name: ctx.enter_context(nc.semaphore(f"{name}_{tag}"))
        self.wk_loaded, self.wv_loaded, self.wo_loaded = sem("wk_loaded"), sem("wv_loaded"), sem("wo_loaded")
        self.wq_loaded = [sem(f"wq{i}_loaded") for i in range(QCHUNKS)]
        self.wq_rounded = sem("wq_rounded")

    def columns(self, i):
        n = 16 * P // QCHUNKS
        return slice(i * n, (i + 1) * n)

    def load(self, sp, wq_dram, wk_dram, wv_dram):
        rows = lambda a: a.rearrange("(c p) n -> p c n", p=P)
        sp.dma_start(self.wk[:, :, :], rows(wk_dram)).then_inc(self.wk_loaded, 16)
        sp.dma_start(self.wv[:, :, :], rows(wv_dram)).then_inc(self.wv_loaded, 16)
        for i in range(QCHUNKS):
            sp.dma_start(self.wq_whole[:, :, self.columns(i)], rows(wq_dram)[:, :, self.columns(i)])\
              .then_inc(self.wq_loaded[i], 16)

    def semaphores(self):
        return [self.wk_loaded, self.wv_loaded, self.wo_loaded, self.wq_rounded] + self.wq_loaded


def attention_wide(nc, chip, w, groups, scale, wo_dram, load=None, ctx_dram=None, mask_dram=None, table=None):
    H, HD = 16, 128
    cross = ctx_dram is not None
    KC = CC if cross else DC
    KVW = groups * HD
    PAIRS = H // 2
    NK, NV = groups // 2, TILES * KVW // 512
    NJ = NK + NV + PAIRS + 2 + (2 if cross else 0)
    assert NJ % 2 == 0
    SLOTS = 5
    tag = "x" if cross else "s"

    c = ExitStack()
    x_hi, x_lo = (c.enter_context(nc.sbuf_tensor(f"xT_{n}_{tag}", [P, DC, SEQ], FP32R)) for n in ("hi", "lo"))
    wq_lo = [c.enter_context(nc.sbuf_tensor(f"wq_lo{i}_{tag}", [P, DC, 2 * HD], FP32R)) for i in range(2)]
    wq_lo_dram = nc.dram_tensor(f"wq_lo_{tag}", (H // 2, P, DC, 2 * HD), FP32R).ap()
    wk, wv, wo = w.wk, w.wv, w.wo
    WORK = 14848 if cross else 10880
    carve = Carve(c.enter_context(nc.sbuf_tensor(f"work_{tag}", [P, WORK], FP32)), WORK)
    qT = carve(2, 512)
    kT = carve(groups, SEQ)
    v = carve(TILES, KVW)
    probs = carve(SLOTS, 2 * SEQ)
    probsT = carve(2, 2 * SEQ)
    oT = carve(H, SEQ)
    chip.sequence_buffers(c, tag, oT if cross else None)
    mx, neg, den, inv = carve(SLOTS, 2), carve(SLOTS, 2), carve(SLOTS, 2), carve(SLOTS, 2)
    tick = carve(1)
    if cross:
        ctx_sb, ctxT = carve(TILES, CTX_DIM), carve(CC, SEQ)
        mask8 = carve(BATCH * SEQ // 4).bitcast(mybir.dt.uint8)
        bias, maskcol8 = carve(SEQ), carve(BATCH * TILES // 4).bitcast(mybir.dt.uint8)
        maskcol = carve(BATCH * TILES)
        mc = carve(TILES)
    kv_src = ctxT if cross else chip.xT

    KEYS = [(0, 2), (0, 2)] if cross else [(0, 1), (0, 2)]
    COL = [0, 256]
    proj = chip.bank[0:2]
    score = chip.bank[2:4]
    trans = chip.bank[4]
    obank = chip.bank[5]
    out = chip.bank[6:8]

    with c:
        s = {n: c.enter_context(nc.semaphore(f"{n}_{tag}")) for n in (
            "xs_ready", "proj_ready", "proj_copied",
            "scores_ready", "masked", "exp_ready", "probs_ready", "probsT_ready",
            "probsT_copied", "heads_ready", "heads_copied", "out_ready", "x_ready", "out_read", "ctx_loaded", "ctx_used", "mask_loaded", "bias_ready",
            "x_lo_ready")}
        lo_made = [c.enter_context(nc.semaphore(f"lo_made{i}_{tag}")) for i in range(2)]
        lo_stored, lo_there = chip.lo_stored[tag], chip.lo_there[tag]
        c.callback(clear_semaphores, nc, list(s.values()) + lo_made + w.semaphores())

        def queries_done(it, pair):
            return it * NJ + (NJ - 2 - PAIRS) + pair + 3

        block = c.enter_context(nc.Block())

        @block.sync
        def _(sp):
            if cross:
                sp.dma_start(ctx_sb, ctx_dram[0, :, :].rearrange("(t p) d -> p t d", p=P)).then_inc(s["ctx_loaded"], 16)
                sp.dma_start(mask8, mask_dram.rearrange("b s -> (b s)").partition_broadcast(P)).then_inc(s["mask_loaded"], 16)
                with nc.allow_non_contiguous_dma(reason="2048 mask bytes onto the partitions"):
                    sp.dma_start(maskcol8, mask_dram.rearrange("b (t p) -> p (b t)", p=P)).then_inc(s["mask_loaded"], 16)
            if load:
                w.load(sp, *load)
            for slot in range(2):
                sp.wait_ge(lo_made[slot], PAIRS // 2)
            sp.dma_start(wo[:, :, :], wo_dram.rearrange("(c p) n -> p c n", p=P)).then_inc(w.wo_loaded, 16)
            if table:
                table.clear_rows(sp)
            if cross:
                with sp.Fori(1, BATCH) as it:
                    sp.wait_ge(s["ctx_used"], it)
                    sp.dma_start(ctx_sb, ctx_dram[bass.ds(it, 1), :, :].rearrange("b (t p) d -> p (b t) d", p=P))\
                      .then_inc(s["ctx_loaded"], 16)
            sp.wait_ge(s["x_ready"], BATCH)

        @block.gpsimd
        def _(pool):
            for pair in range(PAIRS):
                cols, slot = slice(2 * pair * HD, 2 * (pair + 1) * HD), pair % 2
                whole, hi = w.wq_whole[:, :, cols], w.wq_hi[:, :, cols]
                if pair % (PAIRS // QCHUNKS) == 0:
                    pool.wait_ge(w.wq_loaded[pair * QCHUNKS // PAIRS], 16)
                pool.tensor_copy(hi, whole).then_inc(w.wq_rounded, 1)
                pool.wait_ge(w.wq_rounded, pair + 1)
                if pair >= 2:
                    pool.wait_ge(s["proj_ready"], queries_done(0, pair - 2))
                    pool.wait_ge(lo_stored[slot], 16 * (pair // 2))
                pool.tensor_tensor(wq_lo[slot][:, :, :], whole, hi.bitcast(FP32), ALU.subtract).then_inc(lo_made[slot], 1)
                pool.wait_ge(lo_made[slot], pair // 2 + 1)
                pool.dma_start(wq_lo_dram[pair, :, :, :], wq_lo[slot][:, :, :]).then_inc(lo_stored[slot], 16)
            for slot in range(2):
                pool.wait_ge(lo_stored[slot], 16 * (PAIRS // 2))

            def read_back(it, sets):
                for pair in range(PAIRS):
                    pool.wait_ge(s["proj_ready"], queries_done(it, pair - 2) if pair >= 2 else queries_done(it - 1, pair + PAIRS - 2))
                    pool.dma_start(wq_lo[pair % 2][:, :, :], wq_lo_dram[pair, :, :, :]).then_inc(lo_there[pair % 2], 16)
                    if sets:
                        n = (it - 1) * PAIRS + pair
                        table.add_sets(pool, range(sets * n, sets * (n + 1)))

            WITH_SETS = 2 if table else 0
            for it in range(1, BATCH):
                read_back(it, SETS // (WITH_SETS * PAIRS) if it <= WITH_SETS else 0)
            for slot in range(2):
                pool.wait_ge(lo_there[slot], 16 * (PAIRS // 2) * (BATCH - 1))

        @block.tensor
        def _(pe):
            def transpose_x():
                for j in range(2):
                    for i in range(4):
                        cc, t = 2 * j + i // 2, i % 2
                        last = pe.transpose(proj[j][:, 128 * i:128 * i + 128],
                                            chip.xs[:, t, cc * P:(cc + 1) * P], chip.ident)
                    last.then_inc(s["proj_ready"], 1)

            pe.wait_ge(s["xs_ready"], 1)
            transpose_x()

            def sequence(it):
                j = 0

                def bank():
                    nonlocal j
                    pe.wait_ge(s["proj_copied"], it * NJ + j + 1)
                    if j < 2:
                        pe.wait_ge(s["x_lo_ready"], 2 * it + j + 1)
                    j += 1
                    return proj[(j - 1) % 2]

                if cross:
                    pe.wait_ge(s["ctx_loaded"], it * 16 + 16)
                    for cc in range(CC):
                        b = bank()
                        for t in range(TILES):
                            last = pe.transpose(b[:, P * t:P * t + P], ctx_sb[:, t, cc * P:(cc + 1) * P], chip.ident)
                        last.then_inc(s["proj_ready"], 1)
                    pe.drain().then_inc(s["ctx_used"], 1)
                pe.wait_ge(w.wk_loaded, 16)
                for n in range(NK):
                    b = bank()
                    if n == 0:
                        pe.wait_ge(s["proj_copied"], it * NJ + j + 1)
                    for i in range(2):
                        g = 2 * n + i
                        for cc in range(KC):
                            last = pe.matmul(b[:, i * SEQ:(i + 1) * SEQ], wk[:, cc, g * HD:(g + 1) * HD],
                                             kv_src[:, cc, :], start=(cc == 0), stop=(cc == KC - 1))
                    last.then_inc(s["proj_ready"], 1)
                pe.wait_ge(w.wv_loaded, 16)
                for n in range(NV):
                    b = bank()
                    t, col = n % TILES, n // TILES * 512
                    for cc in range(KC):
                        last = pe.matmul(b[:, :], kv_src[:, cc, t * P:(t + 1) * P], wv[:, cc, col:col + 512],
                                         start=(cc == 0), stop=(cc == KC - 1))
                    last.then_inc(s["proj_ready"], 1)

                pair_bank = None

                def query(h):
                    nonlocal pair_bank
                    pair, i = divmod(h, 2)
                    if i == 0:
                        if isinstance(it, int):
                            pe.wait_ge(lo_made[pair % 2], pair // 2 + 1)
                        else:
                            pe.wait_ge(lo_there[pair % 2], (it - 1) * (16 * (PAIRS // 2)) + 16 * (pair // 2 + 1))
                        pair_bank = bank()
                    n = 0
                    hi, lo = w.wq_hi[:, :, h * HD:(h + 1) * HD], wq_lo[pair % 2][:, :, i * HD:(i + 1) * HD]
                    for wq, x in ((hi, x_hi), (hi, x_lo), (lo, x_hi)):
                        for cc in range(DC):
                            last = pe.matmul(pair_bank[:, i * SEQ:(i + 1) * SEQ], wq[:, cc, :],
                                             x[:, cc, :], start=(n == 0), stop=(n == 3 * DC - 1))
                            n += 1
                    if i == 1:
                        last.then_inc(s["proj_ready"], 1)

                def scores(h):
                    pe.wait_ge(s["proj_copied"], it * NJ + (NJ - 2 - PAIRS) + h // 2 + 3)
                    if h >= 2:
                        pe.wait_ge(s["masked"], it * H + h - 1)
                    g = h * groups // H
                    for t, (k0, nk) in enumerate(KEYS):
                        q = qT[:, h // 2 % 2, (h % 2) * SEQ + t * P:(h % 2) * SEQ + (t + 1) * P]
                        last = pe.matmul(score[h % 2][:, COL[t]:COL[t] + nk * P], q, kT[:, g, k0 * P:(k0 + nk) * P],
                                         start=True, stop=True)
                    last.then_inc(s["scores_ready"], 1)

                def turn(h):
                    pe.wait_ge(s["probs_ready"], it * H + h + 1)
                    if h >= 1:
                        pe.wait_ge(s["probsT_copied"], it * H + h)
                    for t, (k0, nk) in enumerate(KEYS):
                        for k in range(nk):
                            last = pe.transpose(trans[:, k * SEQ + t * P:k * SEQ + (t + 1) * P],
                                                probs[:, h % SLOTS, COL[t] + k * P:COL[t] + (k + 1) * P], chip.ident)
                    last.then_inc(s["probsT_ready"], 1)

                def values(h):
                    pe.wait_ge(s["probsT_copied"], it * H + h + 1)
                    if h >= 1:
                        pe.wait_ge(s["heads_copied"], it * H + h)
                    g = h * groups // H
                    for k in range(TILES):
                        q0 = 0 if cross else k * P
                        last = pe.matmul(obank[:, (h % 2) * SEQ + q0:(h % 2 + 1) * SEQ], v[:, k, g * HD:(g + 1) * HD],
                                         probsT[:, h % 2, k * SEQ + q0:(k + 1) * SEQ],
                                         start=(k == 0), stop=(k == TILES - 1), skip_group_check=True)
                    last.then_inc(s["heads_ready"], 1)

                def output(h0, h1):
                    if h0 == 0:
                        pe.wait_ge(w.wo_loaded, 16)
                    pe.wait_ge(s["heads_copied"], it * H + h1)
                    for t in range(TILES):
                        for h in range(h0, h1):
                            last = pe.matmul(out[t][:, :], oT[:, h, t * P:(t + 1) * P], wo[:, h, :],
                                             start=(h == 0), stop=(h == H - 1), skip_group_check=True)
                    if h1 == H:
                        last.then_inc(s["out_ready"], 1)

                for step in range(H + 6):
                    if step < H:
                        query(step)
                    if 2 <= step < H + 2:
                        scores(step - 2)
                    if step == H + 1:
                        pe.wait_ge(s["xs_ready"], it + 2)
                        pe.wait_ge(s["proj_copied"], it * NJ + NJ)
                        transpose_x()
                        j += 2
                        output(0, 6)
                    if 5 <= step < H + 5:
                        turn(step - 5)
                    if step >= 6:
                        values(step - 6)
                    if H + 2 <= step <= H + 4:
                        output(2 * (step - H) + 2, 2 * (step - H) + 4)
                output(12, H)
                assert j == NJ

            sequence(0)
            with pe.Fori(1, BATCH) as it:
                sequence(it)

        @block.scalar
        def _(act):
            copy = lambda dst, src: act.activation(dst, src, ACT.Copy)

            def take_x(i):
                half = lambda a: a[:, 2 * i:2 * i + 2, :].rearrange("p c q -> p (c q)")
                last = copy(half(x_hi), proj[i][:, :])
                return last if cross else copy(half(chip.xT), proj[i][:, :])

            copy(chip.xs[:, :, :], chip.x[:, 0:TILES, :]).then_inc(s["xs_ready"], 1)
            for i in range(2):
                act.wait_ge(s["proj_ready"], i + 1)
                take_x(i).then_inc(s["proj_copied"], 1)
            with act.Fori(0, BATCH) as it:
                j = 0

                def evacuate(dst, cols=512):
                    nonlocal j
                    act.wait_ge(s["proj_ready"], it * NJ + j + 3)
                    copy(dst, proj[j % 2][:, 0:cols]).then_inc(s["proj_copied"], 1)
                    j += 1

                if cross:
                    for cc in range(CC):
                        evacuate(ctxT[:, cc, :], SEQ)
                for n in range(NK):
                    evacuate(kT[:, 2 * n:2 * n + 2, :].rearrange("p g q -> p (g q)"))
                for n in range(NV):
                    t, col = n % TILES, n // TILES * 512
                    if cross:
                        if n == 0:
                            act.wait_ge(s["bias_ready"], it + 1)
                        act.wait_ge(s["proj_ready"], it * NJ + j + 3)
                        act.activation(v[:, t, col:col + 512], proj[j % 2][:, :], ACT.Copy, scale=mc[:, t:t + 1])\
                           .then_inc(s["proj_copied"], 1)
                        j += 1
                    else:
                        evacuate(v[:, t, col:col + 512])
                for step in range(H + 5):
                    if step < H and step % 2 == 0:
                        evacuate(qT[:, step // 2 % 2, :])
                    if 1 <= step <= H:
                        h = step - 1
                        act.wait_ge(s["masked"], it * H + h + 1)
                        for t, (k0, nk) in enumerate(KEYS):
                            pr = probs[:, h % SLOTS, COL[t]:COL[t] + nk * P]
                            last = act.activation(pr, pr, ACT.Exp, bias=neg[:, h % SLOTS, t:t + 1],
                                                  accum_out=den[:, h % SLOTS, t:t + 1])
                        last.then_inc(s["exp_ready"], 1)
                    if step == H // 2:
                        copy(chip.xs[:, :, :], chip.x[:, bass.ds(it * TILES + TILES, TILES), :]).then_inc(s["xs_ready"], 1)
                    if step == H:
                        for i in range(2):
                            act.wait_ge(s["proj_ready"], it * NJ + j + 3)
                            take_x(i).then_inc(s["proj_copied"], 1)
                            j += 1
                    if step >= 5:
                        h = step - 5
                        act.wait_ge(s["heads_ready"], it * H + h + 1)
                        copy(oT[:, h, :], obank[:, (h % 2) * SEQ:(h % 2 + 1) * SEQ]).then_inc(s["heads_copied"], 1)

        @block.vector
        def _(dve):
            def take_x_lo(n):
                for i in range(2):
                    dve.wait_ge(s["proj_copied"], n * NJ + i + 1)
                    half = lambda a: a[:, 2 * i:2 * i + 2, :].rearrange("p c q -> p (c q)")
                    dve.tensor_tensor(half(x_lo), proj[i][:, :], half(x_hi).bitcast(FP32), ALU.subtract)\
                       .then_inc(s["x_lo_ready"], 1)

            take_x_lo(0)
            if cross:
                dve.wait_ge(s["mask_loaded"], 32)
                dve.tensor_copy(maskcol, maskcol8)
                dve.drain()
            with dve.Fori(0, BATCH) as it:
                if cross:
                    dve.tensor_copy(mc, maskcol[:, bass.ds(it * TILES, TILES)])
                    dve.tensor_copy(bias, mask8[:, bass.ds(it * SEQ, SEQ)])
                    dve.drain()
                    dve.tensor_scalar(bias, bias, 1.0, -LOW, ALU.subtract, ALU.mult).then_inc(s["bias_ready"], 1)
                    dve.drain()
                for step in range(H + 4):
                    if step >= 4:
                        h = step - 4
                        dve.wait_ge(s["probsT_ready"], it * H + h + 1)
                        if cross:
                            dve.tensor_copy(probsT[:, h % 2, :], trans[:, :]).then_inc(s["probsT_copied"], 1)
                        else:
                            dve.tensor_copy(probsT[:, h % 2, 0:SEQ], trans[:, 0:SEQ])
                            dve.tensor_copy(probsT[:, h % 2, SEQ + P:], trans[:, SEQ + P:])\
                               .then_inc(s["probsT_copied"], 1)
                    if step < H:
                        h = step
                        dve.wait_ge(s["scores_ready"], it * H + h + 1)
                        dve.memset(tick, 0.0)
                        for t, (k0, nk) in enumerate(KEYS):
                            if cross:
                                hide = bias
                            else:
                                at_ = C_OWN if t == 0 else C_BAND
                                hide = chip.const[:, at_:at_ + nk * P]
                            dve.tensor_tensor_reduce(
                                out=probs[:, h % SLOTS, COL[t]:COL[t] + nk * P],
                                in0=score[h % 2][:, COL[t]:COL[t] + nk * P], in1=hide, scale=scale,
                                scalar=FLOOR, op0=ALU.add, op1=ALU.max, accum_out=mx[:, h % SLOTS, t:t + 1])
                        dve.drain()
                        dve.tensor_scalar(neg[:, h % SLOTS, :], mx[:, h % SLOTS, :], -1.0, None, ALU.mult)\
                           .then_inc(s["masked"], 1)
                    if 1 <= step <= H:
                        h = step - 1
                        dve.wait_ge(s["exp_ready"], it * H + h + 1)
                        dve.reciprocal(inv[:, h % SLOTS, :], den[:, h % SLOTS, :])
                        dve.drain()
                        for t, (k0, nk) in enumerate(KEYS):
                            pr = probs[:, h % SLOTS, COL[t]:COL[t] + nk * P]
                            last = dve.tensor_scalar(pr, pr, inv[:, h % SLOTS, t:t + 1], None, ALU.mult)
                        last.then_inc(s["probs_ready"], 1)
                    if step == H:
                        take_x_lo(it + 1)
                dve.wait_ge(s["out_ready"], it + 1)
                ln_vector(dve, chip, out, it, s, it)


TABLE_ROWS = DIM * DIM + P
SLOTS_OF_TOKENS = 2 * NTILE + EXPERTS
ZERO_PARTS = 16


class ExpertTable:

    def __init__(self, nc, chip, ctx):
        sb = lambda name, width, dt: ctx.enter_context(nc.sbuf_tensor(name, [P, width], dt))
        self.table = nc.dram_tensor("expert_table", (TABLE_ROWS, EXPERTS), FP32).ap()
        self.rows = nc.dram_tensor("expert_rows", (SLOTS_OF_TOKENS * P, DIM), FP32).ap()
        self.products = nc.dram_tensor("expert_products", (SLOTS_OF_TOKENS * P, DIM), FP32).ap()
        self.zero = sb("table_zero", DIM * DIM * EXPERTS // ZERO_PARTS // P, FP32)
        self.dest = sb("table_dest", SETS, INT32)
        self.summed = sb("table_summed", SETS * EXPERTS, FP32)
        self.set_added = chip.set_added
        self.table_clear, self.rows_clear = (ctx.enter_context(nc.semaphore(n)) for n in ("table_clear", "rows_clear"))
        ctx.callback(clear_semaphores, nc, [self.table_clear, self.rows_clear])

    def clear(self, sp):
        part = DIM * DIM // ZERO_PARTS
        for i in range(ZERO_PARTS):
            sp.dma_start(self.table[i * part:(i + 1) * part, :].rearrange("(p n) e -> p (n e)", p=P), self.zero[:, :])\
              .then_inc(self.table_clear, 16)
        sp.dma_start(self.table[ZERO_PARTS * part:, :], self.zero[:, 0:EXPERTS]).then_inc(self.table_clear, 16)

    def clear_rows(self, sp):
        for i in range(0, SLOTS_OF_TOKENS, 2):
            sp.dma_start(self.rows[i * P:(i + 2) * P, :].rearrange("(p n) d -> p (n d)", p=P), self.zero[:, 0:2 * DIM])\
              .then_inc(self.rows_clear, 16)

    def add_sets(self, pool, sets):
        if 0 in sets:
            pool.wait_ge(self.table_clear, 16 * (ZERO_PARTS + 1))
            pool.wait_ge(self.rows_clear, 16 * (SLOTS_OF_TOKENS // 2))
        for i in sets:
            pool.indirect_dma_start(
                out=self.table, out_offset=bass.IndirectOffsetOnAxis(ap=self.dest[:, i:i + 1].bitcast(mybir.dt.uint32), axis=0),
                in_=self.summed[:, i * EXPERTS:(i + 1) * EXPERTS], in_offset=None, compute_op=ALU.add)\
                .then_inc(self.set_added, 16)
            pool.wait_ge(self.set_added, 16 * (i + 1))


def start(nc, chip, x_dram, const_dram, t, atoms_dram, mix_dram, importance_dram, index_dram, load_weights):
    c = ExitStack()
    big = c.enter_context(nc.sbuf_tensor("expert_big", [P, 12288], FP32))
    carve = Carve(c.enter_context(nc.sbuf_tensor("expert_work", [P, 4096], FP32)), 4096)
    zero = t.zero[:, :]
    atoms = big[0:ATOMS, 0:NSPARSE]
    importance = big[0:EXPERTS, 4096:4096 + NSPARSE]
    same = big[:, 8192:8192 + SETS * P].rearrange("p (i s) -> p i s", i=SETS)
    mix = carve(ATOMS)[0:EXPERTS]
    mixT = carve(EXPERTS)[0:ATOMS]
    mstat = carve(4)[0:EXPERTS]
    index, col, row = carve(SETS).bitcast(INT32), carve(SETS).bitcast(INT32), carve(SETS).bitcast(INT32)
    indexf, colf, rowf, dest = carve(SETS), carve(SETS), carve(SETS), carve(SETS)
    before = carve(SETS)
    earlier = big[:, 4096:4096 + SETS * P].rearrange("p (i s) -> p i s", i=SETS)
    weighted = carve(SETS, EXPERTS)
    gate = carve(SETS, EXPERTS)
    flat = lambda a: a.rearrange("p a b -> p (a b)")

    with c:
        s = {n: c.enter_context(nc.semaphore(f"{n}_e")) for n in (
            "const_loaded", "x_loaded", "zeros_ready", "mix_loaded", "atoms_loaded", "importance_loaded", "index_loaded",
            "mix_max", "mix_exp", "mix_ready", "mixT_ready", "mixT_copied", "deltas_ready", "imp_ready",
            "imp_exp", "weighted_ready", "index_ready", "row_ready", "same_ready", "sums_ready")}
        c.callback(clear_semaphores, nc, list(s.values()))
        block = c.enter_context(nc.Block())

        @block.sync
        def _(sp):
            sp.dma_start(index, index_dram.rearrange("(p i) -> p i", i=SETS)).then_inc(s["index_loaded"], 16)
            sp.dma_start(mix, mix_dram).then_inc(s["mix_loaded"], 16)
            sp.dma_start(chip.const[:, :], const_dram).then_inc(s["const_loaded"], 16)
            sp.dma_start(importance, importance_dram).then_inc(s["importance_loaded"], 16)
            sp.dma_start(atoms, atoms_dram).then_inc(s["atoms_loaded"], 16)
            sp.dma_start(chip.x[:, 0:NTILE, :], x_dram.rearrange("b (t p) d -> p (b t) d", p=P)).then_inc(s["x_loaded"], 16)
            load_weights(sp)
            sp.wait_ge(s["zeros_ready"], 1)
            t.clear(sp)
            sp.wait_ge(s["x_loaded"], 16)

        @block.tensor
        def _(pe):
            ident8 = chip.const[0:EXPERTS, C_ID:C_ID + EXPERTS]
            pe.wait_ge(s["const_loaded"], 16)
            pe.wait_ge(s["mix_ready"], 1)
            pe.transpose(chip.bank[0][0:ATOMS, 0:EXPERTS], mix, ident8).then_inc(s["mixT_ready"], 1)
            pe.wait_ge(s["importance_loaded"], 16)
            for i in range(SETS):
                last = pe.transpose(chip.bank[1][:, EXPERTS * i:EXPERTS * (i + 1)],
                                    importance[:, i::SETS], ident8)
            last.then_inc(s["imp_ready"], 1)
            pe.wait_ge(s["mixT_copied"], 1)
            pe.wait_ge(s["atoms_loaded"], 16)
            for i in range(SETS):
                last = pe.matmul(chip.bank[2][:, EXPERTS * i:EXPERTS * (i + 1)], atoms[:, i::SETS], mixT,
                                 start=True, stop=True)
            last.then_inc(s["deltas_ready"], 1)
            pe.wait_ge(s["index_ready"], 1)
            for n in range(SETS // 4):
                if n >= 2:
                    pe.wait_ge(s["same_ready"], 4 * (n - 1))
                for i in range(4 * n, 4 * n + 4):
                    last = pe.matmul(chip.bank[3 + n % 2][:, P * (i % 4):P * (i % 4 + 1)],
                                     indexf[:, i:i + 1].to_broadcast([P, P]), chip.ident, start=True, stop=True)
                last.then_inc(s["row_ready"], 1)
            pe.wait_ge(s["same_ready"], SETS)
            pe.wait_ge(s["weighted_ready"], 1)
            for i in range(SETS):
                last = pe.matmul(chip.bank[5][:, EXPERTS * i:EXPERTS * (i + 1)], same[:, i, :], weighted[:, i, :],
                                 start=True, stop=True)
            last.then_inc(s["sums_ready"], 1)

        @block.scalar
        def _(act):
            act.wait_ge(s["mix_max"], 1)
            act.activation(mix, mix, ACT.Exp, bias=mstat[:, 1:2], accum_out=mstat[:, 2:3]).then_inc(s["mix_exp"], 1)
            act.wait_ge(s["imp_ready"], 1)
            act.activation(flat(gate), chip.bank[1][:, 0:SETS * EXPERTS], ACT.Exp, scale=-1.0)\
               .then_inc(s["imp_exp"], 1)

        @block.vector
        def _(dve):
            dve.memset(zero, 0.0).then_inc(s["zeros_ready"], 1)
            dve.memset(chip.x[:, NTILE:, :], 0.0)
            dve.wait_ge(s["mix_loaded"], 16)
            dve.tensor_reduce(mstat[:, 0:1], mix, AX.X, ALU.max)
            dve.drain()
            dve.tensor_scalar(mstat[:, 1:2], mstat[:, 0:1], -1.0, None, ALU.mult).then_inc(s["mix_max"], 1)
            dve.wait_ge(s["mix_exp"], 1)
            dve.reciprocal(mstat[:, 3:4], mstat[:, 2:3])
            dve.drain()
            dve.tensor_scalar(mix, mix, mstat[:, 3:4], None, ALU.mult).then_inc(s["mix_ready"], 1)
            dve.wait_ge(s["index_loaded"], 16)
            dve.tensor_copy(indexf, index)
            dve.tensor_scalar(col, index, DIM - 1, None, ALU.bitwise_and)
            dve.tensor_scalar(row, index, DIM.bit_length() - 1, None, ALU.logical_shift_right)
            dve.drain().then_inc(s["index_ready"], 1)
            dve.tensor_copy(colf, col)
            dve.tensor_copy(rowf, row)
            dve.drain()
            dve.scalar_tensor_tensor(dest, colf, float(DIM), rowf, ALU.mult, ALU.add)
            dve.wait_ge(s["mixT_ready"], 1)
            dve.tensor_copy(mixT, chip.bank[0][0:ATOMS, 0:EXPERTS]).then_inc(s["mixT_copied"], 1)
            dve.wait_ge(s["imp_exp"], 1)
            dve.tensor_scalar(flat(gate), flat(gate), 1.0, None, ALU.add)
            dve.drain()
            dve.reciprocal(flat(gate), flat(gate))
            dve.drain()
            dve.wait_ge(s["deltas_ready"], 1)
            dve.tensor_tensor(flat(weighted), chip.bank[2][:, 0:SETS * EXPERTS], flat(gate), ALU.mult)\
               .then_inc(s["weighted_ready"], 1)
            for i in range(SETS):
                if i % 4 == 0:
                    dve.wait_ge(s["row_ready"], i // 4 + 1)
                dve.tensor_scalar(same[:, i, :], chip.bank[3 + i // 4 % 2][:, P * (i % 4):P * (i % 4 + 1)],
                                  indexf[:, i:i + 1], None, ALU.is_equal).then_inc(s["same_ready"], 1)
            dve.drain()
            dve.tensor_tensor(earlier, same, chip.const[:, C_BEFORE:C_BEFORE + P].unsqueeze(1)
                              .to_broadcast([P, SETS, P]), ALU.mult)
            dve.drain()
            dve.tensor_reduce(before, earlier, AX.X, ALU.add)
            dve.drain()
            dve.tensor_scalar(before, before, 0.0, None, ALU.is_gt)
            dve.wait_ge(s["const_loaded"], 16)
            dve.tensor_scalar(colf, dest, -1.0, chip.const[:, C_SPARE:C_SPARE + 1], ALU.mult, ALU.add)
            dve.drain()
            dve.tensor_tensor(colf, colf, before, ALU.mult)
            dve.drain()
            dve.tensor_tensor(dest, dest, colf, ALU.add)
            dve.drain()
            dve.tensor_copy(t.dest[:, :], dest)
            dve.wait_ge(s["sums_ready"], 1)
            dve.tensor_copy(t.summed[:, :], chip.bank[5][:, 0:SETS * EXPERTS])


class RotaryTables:
    NT = NTILE + TILES

    def __init__(self, nc, ctx, fside_dram):
        self.nc, self.fside_dram = nc, fside_dram
        self.sin, self.cos = (ctx.enter_context(nc.sbuf_tensor(n, [P, self.NT, HW], FP32)) for n in ("rot_sin", "rot_cos"))
        self.cleared, self.loaded, self.reduced, self.taken = (
            ctx.enter_context(nc.semaphore(n)) for n in ("pos_cleared", "pos_loaded", "ang_reduced", "sin_taken"))
        ctx.callback(clear_semaphores, nc, [self.cleared, self.loaded, self.reduced, self.taken])

    def work(self, ctx):
        sb = lambda name, shape: ctx.enter_context(self.nc.sbuf_tensor(name, shape, FP32))
        self.pos = sb("pos", [P, self.NT, 2])
        self.ang, self.turns = (sb(n, [P, self.NT, 8]) for n in ("ang", "turns"))
        self.red = [sb(n, [P, self.NT, 8]) for n in ("red_sin", "red_cos")]

    def load(self, sp):
        sp.wait_ge(self.cleared, 1)
        with self.nc.allow_non_contiguous_dma(reason="two positions a token"):
            sp.dma_start(self.pos[:, 0:NTILE, :], self.fside_dram.rearrange("b (t p) a -> p (b t) a", p=P)).then_inc(self.loaded, 16)

    def sines(self, act):
        for i, table in enumerate((self.sin, self.cos)):
            act.wait_ge(self.reduced, i + 1)
            odd = table[:, :, :].rearrange("p n (f two) -> p n f two", two=2)[:, :, :, 1]
            act.activation(odd, self.red[i][:, :, :], ACT.Sin).then_inc(self.taken, 1)

    def angles(self, dve, chip):
        TWO_PI_HI = 6.28125
        TWO_PI_LO = float(2 * np.pi - TWO_PI_HI)
        pi_floor = float(np.nextafter(np.float32(np.pi), np.float32(0)))
        MAGIC = float(3 << 22)
        pos, ang, turns = self.pos, self.ang, self.turns
        dve.wait_ge(self.loaded, 16)
        freq = chip.const[:, C_FREQ:C_FREQ + 4]
        for axis in range(2):
            dve.tensor_tensor(ang[:, :, 4 * axis:4 * axis + 4],
                              pos[:, :, axis:axis + 1].to_broadcast([P, self.NT, 4]),
                              freq.unsqueeze(1).to_broadcast([P, self.NT, 4]), ALU.mult)
        dve.drain()
        for red, shift in zip(self.red, (0.0, 0.25)):
            dve.tensor_scalar(turns[:, :, :], ang[:, :, :], float(1 / (2 * np.pi)), shift, ALU.mult, ALU.add)
            dve.drain()
            dve.tensor_scalar(turns[:, :, :], turns[:, :, :], MAGIC, MAGIC, ALU.add, ALU.subtract)
            dve.drain()
            dve.scalar_tensor_tensor(red[:, :, :], turns[:, :, :], -TWO_PI_HI, ang[:, :, :], ALU.mult, ALU.add)
            dve.drain()
            dve.scalar_tensor_tensor(red[:, :, :], turns[:, :, :], -TWO_PI_LO, red[:, :, :], ALU.mult, ALU.add)
            dve.drain()
            if shift:
                dve.tensor_scalar(red[:, :, :], red[:, :, :], float(np.pi / 2), None, ALU.add)
                dve.drain()
            dve.tensor_scalar(red[:, :, :], red[:, :, :], -pi_floor, pi_floor, ALU.max, ALU.min)
            dve.drain().then_inc(self.reduced, 1)

    def first_members(self, dve):
        for i, (table, sign) in enumerate(((self.sin, -1.0), (self.cos, 1.0))):
            dve.wait_ge(self.taken, i + 1)
            pairs = table[:, :, :].rearrange("p n (f two) -> p n f two", two=2)
            dve.tensor_scalar(pairs[:, :, :, 0], pairs[:, :, :, 1], sign, None, ALU.mult)


def experts(nc, chip, t, gate_dram, w_dram, rotary):
    DVE_TILES = 8
    UNROLL = 4
    c = ExitStack()
    chip.sequence_buffers(c, "m")
    rotary.work(c)
    weights = c.enter_context(nc.sbuf_tensor("weights_m", [P, 26624], FP32))
    WT = weights[:, 0:DC * DIM].rearrange("p (c r) -> p c r", c=DC)
    at = DC * DIM
    M = weights[:, at:at + DC * EXPERTS * DIM].rearrange("p (c e r) -> p c e r", c=DC, e=EXPERTS)
    at += DC * EXPERTS * DIM
    stage = weights[:, at:at + 2 * EXPERTS * DIM].rearrange("p (s n) -> p s n", s=2)
    total = weights[:, at:at + NTILE * DIM].rearrange("p (t d) -> p t d", t=NTILE)
    carve = Carve(c.enter_context(nc.sbuf_tensor("work_m", [P, 11264], FP32)), 11264)
    xT, xs = [chip.xT, carve(DC, SEQ)], [chip.xs, carve(TILES, DIM)]
    stats = carve(NTILE, 8)
    rstd, newton, variance = (carve(NTILE) for _ in range(3))
    shared = carve(2 * UNROLL * DIM)
    w_rows = shared[:, 0:DC * DIM].rearrange("p (c n) -> p c n", c=DC)
    slot_rows = shared[:, 0:UNROLL * DIM].rearrange("p (k d) -> p k d", k=UNROLL)
    product = shared[:, UNROLL * DIM:].rearrange("p (k d) -> p k d", k=UNROLL)
    fetched = shared.rearrange("p (u t k d) -> p u t k d", u=2, t=TILES, k=2)
    slotT = carve(2, DC, P)
    gate_rows = carve(DIM)[0:EXPERTS]
    gateT = carve(DC, EXPERTS)
    logit, low, key, one, two, sent, place, count = (carve(NTILE, EXPERTS) for _ in range(8))
    before = carve(NTILE + 1, EXPERTS)
    m1, m2, k1, k2, d, g1, g2 = (carve(NTILE) for _ in range(7))
    dest = carve(2, NTILE)
    dest_int = carve(2, NTILE).bitcast(INT32)
    full = carve(EXPERTS).bitcast(INT32)
    slots, end = carve(EXPERTS), carve(EXPERTS)
    ended = carve(SLOTS_OF_TOKENS, EXPERTS)
    slot_expert = carve(SLOTS_OF_TOKENS)
    slot_expert_int = carve(SLOTS_OF_TOKENS).bitcast(INT32)
    tick, ticks = carve(1), carve(2 * TILES)
    rank = chip.const[:, C_RANK:C_RANK + EXPERTS].unsqueeze(1).to_broadcast([P, NTILE, EXPERTS])
    logits_bank = chip.bank[0]
    x_bank = [chip.bank[2:4], chip.bank[4:6]]
    turn_bank, out = chip.bank[4:6], chip.bank[6:8]
    wide = lambda a: a.unsqueeze(2).to_broadcast([P, NTILE, EXPERTS])
    by_tile = lambda cols: cols.rearrange("p (t e) -> p t e", t=NTILE)
    ranks, counts = (by_tile(chip.bank[1][:, i * NTILE * EXPERTS:(i + 1) * NTILE * EXPERTS]) for i in range(2))

    with c:
        s = {n: c.enter_context(nc.semaphore(f"{n}_m")) for n in (
            "w_loaded", "gate_loaded", "chunk_used", "chunk_used2", "wT_ready", "wT_copied", "xs_ready",
            "xT_ready", "xT_copied", "logits_ready", "logits_read", "margin_ready", "exp_ready", "sent_ready",
            "ranks_ready", "dest_ready", "slots_known", "dense_ready", "dense_copied", "slot_turned",
            "slot_copied", "slot_done", "product_copied", "stats_ready", "x_ready")}
        ring = lambda name, n: [c.enter_context(nc.semaphore(f"{name}{i}_m")) for i in range(n)]
        chunk_loaded, slot_loaded = ring("chunk_loaded", 2), ring("slot_loaded", UNROLL)
        stored, back = chip.products_stored, chip.products_back
        returned = c.enter_context(nc.semaphore("returned_m"))
        block = c.enter_context(nc.Block())

        @block.sync
        def _(sp):
            sp.dma_start(gate_rows, gate_dram).then_inc(s["gate_loaded"], 16)
            sp.dma_start(w_rows, w_dram.rearrange("(c p) n -> p c n", p=P)).then_inc(s["w_loaded"], 16)
            for cc in range(DC):
                if cc >= 2:
                    sp.wait_ge(s["chunk_used"], cc - 1)
                    sp.wait_ge(s["chunk_used2"], cc - 1)
                sp.dma_start(stage[:, cc % 2, :], t.table[cc * P * DIM:(cc + 1) * P * DIM, :].rearrange("(p r) e -> p (r e)", p=P))\
                  .then_inc(chunk_loaded[cc % 2], 16)
            rotary.load(sp)
            sp.wait_ge(chip.rows_sent, 16 * 2 * NTILE)
            sp.wait_ge(s["wT_copied"], DC + 1)
            for k in range(UNROLL):
                sp.dma_start(slot_rows[:, k, :], t.rows[k * P:(k + 1) * P, :]).then_inc(slot_loaded[k], 16)
            with sp.Fori(1, SLOTS_OF_TOKENS // UNROLL) as it:
                for k in range(UNROLL):
                    sp.wait_ge(s["slot_turned"], it * UNROLL + k + 1 - UNROLL)
                    sp.dma_start(slot_rows[:, k, :], t.rows[bass.ds(it * (UNROLL * P) + k * P, P), :]).then_inc(slot_loaded[k], 16)
            sp.wait_ge(s["x_ready"], 2)

        @block.tensor
        def _(pe):
            def transpose_pair(pair):
                for u in range(2):
                    pe.wait_ge(s["xs_ready"], 2 * pair + u + 1)
                    for j in range(2):
                        for i in range(4):
                            cc, tile = 2 * j + i // 2, i % 2
                            last = pe.transpose(x_bank[u][j][:, P * i:P * i + P],
                                                xs[u][:, tile, cc * P:(cc + 1) * P], chip.ident)
                        last.then_inc(s["xT_ready"], 1)

            pe.wait_ge(s["w_loaded"], 16)
            for cc in range(DC):
                if cc >= 2:
                    pe.wait_ge(s["wT_copied"], cc - 1)
                for ro in range(DC):
                    last = pe.transpose(turn_bank[cc % 2][:, P * ro:P * (ro + 1)],
                                        w_rows[:, ro, cc * P:(cc + 1) * P], chip.ident)
                last.then_inc(s["wT_ready"], 1)
            pe.wait_ge(s["gate_loaded"], 16)
            for cc in range(DC):
                last = pe.transpose(logits_bank[:, EXPERTS * cc:EXPERTS * (cc + 1)], gate_rows[:, cc * P:(cc + 1) * P],
                                    chip.const[0:EXPERTS, C_ID:C_ID + EXPERTS])
            last.then_inc(s["wT_ready"], 1)
            pe.wait_ge(s["wT_copied"], DC + 1)
            with pe.Fori(0, BATCH // 2) as it:
                transpose_pair(it)
                pe.wait_ge(s["logits_read"], it + 1)
                for u in range(2):
                    pe.wait_ge(s["xT_copied"], 4 * it + 2 * u + 2)
                    for tile in range(TILES):
                        col = EXPERTS * (TILES * u + tile)
                        for cc in range(DC):
                            last = pe.matmul(logits_bank[:, col:col + EXPERTS], xT[u][:, cc, tile * P:(tile + 1) * P],
                                             gateT[:, cc, :], start=(cc == 0), stop=(cc == DC - 1))
                last.then_inc(s["logits_ready"], 1)
            pe.wait_ge(s["sent_ready"], 1)
            pe.matmul(ranks, chip.const[:, C_BEFORE:C_BEFORE + P], sent, start=True, stop=True)
            pe.matmul(counts, chip.const[:, C_HAD:C_HAD + 1].to_broadcast([P, P]), sent, start=True, stop=True)\
              .then_inc(s["ranks_ready"], 1)
            def dense_pair(it):
                for u in range(2):
                    pe.wait_ge(s["xT_copied"], 4 * it + 2 * BATCH + 2 * u + 2)
                    for tile in range(TILES):
                        pe.wait_ge(s["dense_copied"], 4 * it + 2 * u + tile + 1)
                        for cc in range(DC):
                            last = pe.matmul(out[tile][:, :], xT[u][:, cc, tile * P:(tile + 1) * P], WT[:, cc, :],
                                             start=(cc == 0), stop=(cc == DC - 1))
                        last.then_inc(s["dense_ready"], 1)

            with pe.Fori(0, BATCH // 2 - 1) as it:
                transpose_pair(it + BATCH // 2)
                dense_pair(it)
            transpose_pair(BATCH - 1)
            pe.wait_ge(s["dense_copied"], 2 * BATCH - 2)
            pe.wait_ge(s["xT_copied"], 4 * BATCH)

            def turn_slot(it, k):
                pe.wait_ge(slot_loaded[k], 16 * it + 16)
                pe.wait_ge(s["slot_copied"], it * UNROLL + k + 1)
                for cc in range(DC):
                    last = pe.transpose(turn_bank[k % 2][:, P * cc:P * (cc + 1)], slot_rows[:, k, cc * P:(cc + 1) * P], chip.ident)
                last.then_inc(s["slot_turned"], 1)

            def slot_body(it, last_slots):
                for k in range(UNROLL):
                    if k + 1 < UNROLL:
                        turn_slot(it, k + 1)
                    elif not last_slots:
                        turn_slot(it + 1, 0)
                    expert = nc.values_load(slot_expert_int[0:1, bass.ds(it * UNROLL + k, 1)],
                                            engines=[mybir.EngineType.PE], min_val=0, max_val=EXPERTS - 1,
                                            skip_runtime_bounds_check_because="a minimum with the last expert bounds it")
                    pe.wait_ge(s["slot_copied"], it * UNROLL + k + 3)
                    pe.wait_ge(s["product_copied"], it * UNROLL + k + 1)
                    for cc in range(DC):
                        last = pe.matmul(out[k % 2][:, :], slotT[:, k % 2, cc, :], M[:, cc, bass.ds(expert, 1), :],
                                         start=(cc == 0), stop=(cc == DC - 1))
                    last.then_inc(s["slot_done"], 1)

            pe.wait_ge(s["chunk_used"], DC)
            pe.wait_ge(s["chunk_used2"], DC)
            pe.wait_ge(s["slots_known"], 1)
            turn_slot(0, 0)
            with pe.Fori(0, SLOTS_OF_TOKENS // UNROLL - 1) as it:
                slot_body(it, False)
            slot_body(SLOTS_OF_TOKENS // UNROLL - 1, True)
            pe.wait_ge(s["product_copied"], SLOTS_OF_TOKENS + 2)
            dense_pair(BATCH // 2 - 1)

        @block.scalar
        def _(act):
            copy = lambda dst, src: act.activation(dst, src, ACT.Copy)

            def transposed(pair):
                for u in range(2):
                    for j in range(2):
                        act.wait_ge(s["xT_ready"], 4 * pair + 2 * u + j + 1)
                        copy(xT[u][:, 2 * j:2 * j + 2, :].rearrange("p c q -> p (c q)"), x_bank[u][j][:, :])\
                            .then_inc(s["xT_copied"], 1)

            def regroup(cc):
                act.wait_ge(chunk_loaded[cc % 2], 16 * (cc // 2 + 1))
                copy(M[:, cc, :, DIM // 2:], stage[:, cc % 2, :].rearrange("p (r e) -> p e r", e=EXPERTS)[:, :, DIM // 2:])\
                    .then_inc(s["chunk_used"], 1)

            for cc in range(DC):
                act.wait_ge(s["wT_ready"], cc + 1)
                copy(WT[:, cc, :], turn_bank[cc % 2][:, :]).then_inc(s["wT_copied"], 1)
            act.wait_ge(s["wT_ready"], DC + 1)
            copy(gateT.rearrange("p c e -> p (c e)"), logits_bank[:, 0:DC * EXPERTS]).then_inc(s["wT_copied"], 1)
            with act.Fori(0, BATCH // 4) as it:
                transposed(it)
            regroup(0)
            regroup(1)
            with act.Fori(BATCH // 4, BATCH // 2) as it:
                transposed(it)

            def stage_pair(pair):
                for u in range(2):
                    copy(xs[u][:, :, :], chip.x[:, bass.ds((2 * pair + u) * TILES, TILES), :]).then_inc(s["xs_ready"], 1)

            stage_pair(0)
            regroup(2)
            regroup(3)
            act.wait_ge(s["margin_ready"], 1)
            act.activation(d, d, ACT.Exp).then_inc(s["exp_ready"], 1)
            act.wait_ge(s["chunk_used2"], DC)
            act.drain().then_inc(s["dense_copied"], 2)

            def dense_share(pair):
                act.drain()
                for i in range(2 * TILES):
                    act.wait_ge(s["dense_ready"], 2 * TILES * pair + i + 1)
                    act.activation(ticks[:, i:i + 1], chip.const[:, 0:1], ACT.Copy)
                    copy(total[:, bass.ds(2 * TILES * pair + i, 1), :], out[i % TILES][:, :]).then_inc(s["dense_copied"], 1)

            with act.Fori(0, BATCH // 2 - 1) as it:
                transposed(it + BATCH // 2)
                stage_pair(it + 1)
                dense_share(it)
            transposed(BATCH - 1)
            rotary.sines(act)
            act.drain().then_inc(s["slot_copied"], 2)
            with act.Fori(0, SLOTS_OF_TOKENS // UNROLL) as it:
                for k in range(UNROLL):
                    act.wait_ge(s["slot_turned"], it * UNROLL + k + 1)
                    copy(slotT[:, k % 2, :, :].rearrange("p c q -> p (c q)"), turn_bank[k % 2][:, :]).then_inc(s["slot_copied"], 1)
            dense_share(BATCH // 2 - 1)
            act.wait_ge(s["stats_ready"], 1)
            for tile in range(DVE_TILES, NTILE):
                last = act.activation(chip.x[:, tile, :], total[:, tile, :], ACT.Identity,
                                      bias=newton[:, tile:tile + 1], scale=rstd[:, tile:tile + 1])
            last.then_inc(s["x_ready"], 1)

        @block.vector
        def _(dve):
            def stage_pair(pair):
                for u in range(2):
                    dve.tensor_copy(xs[u][:, :, :], chip.x[:, bass.ds((2 * pair + u) * TILES, TILES), :]).then_inc(s["xs_ready"], 1)

            def read_logits(pair):
                dve.tensor_scalar(logit[:, bass.ds(pair * 2 * TILES, 2 * TILES), :],
                                  logits_bank[:, 0:2 * TILES * EXPERTS].rearrange("p (t e) -> p t e", t=2 * TILES),
                                  -50.0, 50.0, ALU.max, ALU.min).then_inc(s["logits_read"], 1)

            stage_pair(0)
            dve.memset(rotary.pos[:, :, :], 0.0).then_inc(rotary.cleared, 1)
            dve.drain().then_inc(s["logits_read"], 1)
            with dve.Fori(1, BATCH // 2) as it:
                dve.wait_ge(s["logits_ready"], it)
                dve.memset(tick, 0.0)
                stage_pair(it)
                read_logits(it - 1)
            dve.wait_ge(s["logits_ready"], BATCH // 2)
            read_logits(BATCH // 2 - 1)
            dve.drain()

            def pick(values, top, rank_top, chosen):
                dve.tensor_reduce(top, values, AX.X, ALU.max)
                dve.drain()
                dve.tensor_tensor(key, values, wide(top), ALU.is_equal)
                dve.drain()
                dve.tensor_tensor(key, key, rank, ALU.mult)
                dve.drain()
                dve.tensor_reduce(rank_top, key, AX.X, ALU.max)
                dve.drain()
                dve.tensor_tensor(chosen, rank, wide(rank_top), ALU.is_equal)
                dve.drain()

            pick(logit, m1, k1, one)
            dve.scalar_tensor_tensor(low, one, -1000.0, logit, ALU.mult, ALU.add)
            dve.drain()
            pick(low, m2, k2, two)
            dve.tensor_tensor(sent, one, two, ALU.add).then_inc(s["sent_ready"], 1)
            dve.tensor_tensor(d, m2, m1, ALU.subtract).then_inc(s["margin_ready"], 1)
            dve.wait_ge(s["ranks_ready"], 1)
            dve.tensor_copy(count, counts)
            dve.memset(before[:, 0, :], 0.0)
            dve.drain()
            for tile in range(NTILE):
                dve.tensor_tensor(before[:, tile + 1, :], before[:, tile, :], count[:, tile, :], ALU.add)
                dve.drain()
            dve.tensor_scalar(full, before[:, NTILE, :], float(P - 1), None, ALU.add)
            dve.drain()
            dve.tensor_scalar(full, full, P.bit_length() - 1, None, ALU.logical_shift_right)
            dve.drain()
            dve.tensor_copy(slots, full)
            dve.drain()
            dve.tensor_copy(end, slots)
            dve.drain()
            for e in range(1, EXPERTS):
                dve.tensor_tensor(end[:, e:e + 1], end[:, e:e + 1], end[:, e - 1:e], ALU.add)
                dve.drain()
            dve.tensor_tensor(slots, end, slots, ALU.subtract)
            dve.drain()
            dve.tensor_scalar(slots, slots, float(P), None, ALU.mult)
            dve.tensor_tensor(place, before[:, 0:NTILE, :], ranks, ALU.add)
            dve.drain()
            dve.tensor_tensor(place, place, slots.unsqueeze(1).to_broadcast([P, NTILE, EXPERTS]), ALU.add)
            dve.drain()
            for i, chosen in enumerate((one, two)):
                dve.tensor_tensor(key, place, chosen, ALU.mult)
                dve.drain()
                dve.tensor_reduce(dest[:, i, :], key, AX.X, ALU.add)
                dve.drain()
            dve.tensor_copy(dest_int, dest).then_inc(s["dest_ready"], 1)
            dve.tensor_tensor(ended, chip.const[:, C_SLOT:C_SLOT + SLOTS_OF_TOKENS].unsqueeze(2)
                              .to_broadcast([P, SLOTS_OF_TOKENS, EXPERTS]),
                              end.unsqueeze(1).to_broadcast([P, SLOTS_OF_TOKENS, EXPERTS]), ALU.is_ge)
            dve.drain()
            dve.tensor_reduce(slot_expert, ended, AX.X, ALU.add)
            dve.drain()
            dve.tensor_scalar(slot_expert, slot_expert, float(EXPERTS - 1), None, ALU.min)
            dve.drain()
            dve.tensor_copy(slot_expert_int, slot_expert)
            dve.drain().then_inc(s["slots_known"], 1)
            dve.wait_ge(s["exp_ready"], 1)
            dve.tensor_scalar(g1, d, 1.0, None, ALU.add)
            dve.drain()
            dve.reciprocal(g1, g1)
            dve.drain()
            dve.tensor_tensor(g2, d, g1, ALU.mult)
            rotary.angles(dve, chip)
            def add_x(it):
                dve.wait_ge(s["dense_copied"], it * TILES + TILES + 2)
                dve.memset(tick, 0.0)
                rows = total[:, bass.ds(it * TILES, TILES), :]
                dve.tensor_tensor(rows, rows, chip.x[:, bass.ds(it * TILES, TILES), :], ALU.add)
                dve.drain()

            with dve.Fori(0, BATCH - 2) as it:
                add_x(it)
            dve.drain().then_inc(s["product_copied"], 2)

            for k in range(UNROLL):
                dve.wait_ge(s["slot_done"], k + 1)
                dve.tensor_copy(product[:, k, :], out[k % 2][:, :]).then_inc(s["product_copied"], 1)
            with dve.Fori(1, SLOTS_OF_TOKENS // UNROLL) as it:
                for k in range(UNROLL):
                    dve.wait_ge(s["slot_done"], it * UNROLL + k + 1)
                    dve.wait_ge(stored[k], 16 * it)
                    dve.tensor_copy(product[:, k, :], out[k % 2][:, :]).then_inc(s["product_copied"], 1)
            rotary.first_members(dve)

            def finish_pair(it):
                for u in range(2):
                    n = 2 * it + u
                    dve.wait_ge(back[u], 64 * it + 64)
                    dve.memset(tick, 0.0)
                    rows = [total[:, bass.ds(n * TILES + tile, 1), :] for tile in range(TILES)]
                    for i, gate in enumerate((g1, g2)):
                        for tile in range(TILES):
                            last = dve.scalar_tensor_tensor(rows[tile], fetched[:, u, tile, i:i + 1, :],
                                                            gate[:, bass.ds(n * TILES + tile, 1)], rows[tile], ALU.mult, ALU.add)
                        if i == 1:
                            last.then_inc(returned, 1)
                        dve.drain()
                    for tile in range(TILES):
                        dve.bn_stats(stats[:, bass.ds(n * TILES + tile, 1), 0:6], rows[tile])

            with dve.Fori(0, BATCH // 2 - 1) as it:
                finish_pair(it)
            for n in (BATCH - 2, BATCH - 1):
                add_x(n)
            finish_pair(BATCH // 2 - 1)
            dve.drain()
            for tile in range(NTILE):
                dve.bn_aggr(stats[:, tile, 6:8], stats[:, tile, 0:6])
            dve.drain()
            rsqrt(dve, rstd, stats[:, :, 7], variance, newton)
            dve.scalar_tensor_tensor(newton, stats[:, :, 6], -1.0, rstd, ALU.mult, ALU.mult).then_inc(s["stats_ready"], 1)
            for tile in range(DVE_TILES):
                last = dve.tensor_scalar(chip.x[:, tile, :], total[:, tile, :],
                                         stats[:, tile, 6:7], rstd[:, tile:tile + 1], ALU.subtract, ALU.mult)
            last.then_inc(s["x_ready"], 1)

        @block.gpsimd
        def _(pool):
            for cc in range(DC):
                pool.wait_ge(chunk_loaded[cc % 2], 16 * (cc // 2 + 1))
                pool.tensor_copy(M[:, cc, :, 0:DIM // 2], stage[:, cc % 2, :].rearrange("p (r e) -> p e r", e=EXPERTS)[:, :, 0:DIM // 2])\
                    .then_inc(s["chunk_used2"], 1)
            pool.wait_ge(s["dest_ready"], 1)
            place_of = lambda tile, i: bass.IndirectOffsetOnAxis(ap=dest_int[:, i, tile:tile + 1].bitcast(mybir.dt.uint32), axis=0)
            for tile in range(NTILE):
                for i in range(2):
                    pool.indirect_dma_start(out=t.rows, out_offset=place_of(tile, i), in_=chip.x[:, tile, :], in_offset=None)\
                        .then_inc(chip.rows_sent, 16)
            with pool.Fori(0, SLOTS_OF_TOKENS // UNROLL) as it:
                for k in range(UNROLL):
                    pool.wait_ge(s["product_copied"], it * UNROLL + k + 3)
                    pool.dma_start(t.products[bass.ds(it * (UNROLL * P) + k * P, P), :], product[:, k, :]).then_inc(stored[k], 16)
            for k in range(UNROLL):
                pool.wait_ge(stored[k], 16 * (SLOTS_OF_TOKENS // UNROLL))
            for n in range(BATCH):
                if n >= 2:
                    pool.wait_ge(returned, n - 1)
                for tile in range(TILES):
                    for i in range(2):
                        pool.indirect_dma_start(out=fetched[:, n % 2, tile, i, :], out_offset=None, in_=t.products,
                                                in_offset=place_of(TILES * n + tile, i)).then_inc(back[n % 2], 16)

NH, VW = 32, 32


class Uses:

    def __init__(self, first, each):
        assert len(first) % 2 == 0 and len(each) % 2 == 0
        self.first, self.each = first, each
        self.name = {n: j for j, (n, _) in enumerate(each)}
        self.name_first = {n: j for j, (n, _) in enumerate(first)}

    def count(self, uses, engine):
        return sum(e == engine for _, e in uses)

    def place(self, name, batch):
        if batch is None:
            j = self.name_first[name]
            e = self.first[j][1]
            return j % 2, j + 1, e, self.count(self.first[:j + 1], e)
        j = self.name[name]
        e = self.each[j][1]
        return (j % 2, len(self.first) + batch * len(self.each) + j + 1, e,
                self.count(self.first, e) + batch * self.count(self.each, e) + self.count(self.each[:j + 1], e))

    def before(self, name, batch):
        if batch is None:
            j = self.name_first[name]
            return None if j < 2 else (self.first[j - 2][1], self.count(self.first[:j - 1], self.first[j - 2][1]))
        j = self.name[name]
        if j >= 2:
            e = self.each[j - 2][1]
            return e, (self.count(self.first, e) + batch * self.count(self.each, e)
                       + self.count(self.each[:j - 1], e))
        e = self.each[j - 2][1]
        later = self.count(self.each[len(self.each) + j - 1:], e)
        return e, self.count(self.first, e) + batch * self.count(self.each, e) - later


def attention_narrow(nc, chip, wq_dram, wk_dram, wv_dram, wo_dram, ctx_dram=None, bias_dram=None,
                     rotary=None):
    cross = ctx_dram is not None
    tag = "y" if cross else "c"
    KC = CC if cross else DC
    KVH = NH if cross else 8
    KW = KVH * HW
    KB = NH // 2 if cross else KVH
    SCALE = 0.25
    PTS = 2

    c = ExitStack()
    chip.sequence_buffers(c, tag)
    sb = lambda name, shape, dt=FP32: c.enter_context(nc.sbuf_tensor(f"{name}_{tag}", shape, dt))
    wq, wo = sb("wq", [P, DC, DIM]), sb("wo", [P, DC, DIM])
    wk, wv = sb("wk", [P, KC, KW]), sb("wv", [P, KC, KW])
    qT, kT = sb("qT", [P, 2, NH // 2, SEQ], FP32R), sb("kT", [P, 2, KB, SEQ], FP32R)
    v = sb("v", [P, 2, TILES, KVH, VW])
    parts = sb("parts", [P, 2, NH, 4 * HW])
    rot, turn = sb("rot", [P, DIM]), sb("turn", [P, DIM])
    mx, neg_hl = sb("mx", [P, TILES, NH]), sb("neg_hl", [P, TILES, 2, 2, NH])
    negT = sb("negT", [P, 2, SEQ], FP32R)
    select = sb("select", [P, NH], FP32R)
    probsT = sb("probsT", [P, PTS, 2 * SEQ])
    heads = sb("heads", [P, NH // 4, SEQ])
    rden = sb("rden", [P, NH // 2])
    heads_n = sb("heads_n", [P, TILES, DIM])
    scratch, tick = sb("scratch", [P, P]), sb("tick", [P, 1])
    if cross:
        ctx_sb, ctxT = sb("ctx", [P, TILES, CTX_DIM]), sb("ctxT", [P, CC, SEQ])
        bout = sb("bout", [P, DIM])
        headsT = heads[:, 0:DC, :]
        cos_now, sin_now = sb("cos_now", [P, TILES, HW]), sb("sin_now", [P, TILES, HW])
    else:
        ident16, hide16 = sb("ident16", [P, P], BF16), sb("hide16", [P, P], BF16)
    kv_src = ctxT if cross else chip.xT

    prep, score, scoreT, hbank = chip.bank[0:2], chip.bank[2:4], chip.bank[4:6], chip.bank[6:8]

    KU = KB // 4
    QU = NH // 2 // 4
    A_USES = ([("xT0", "act"), ("xT1", "act")] + ([("ctxT", "act")] if cross else [])
              + [("k0", "dve"), ("k1", "dve"), ("v0", "act"), ("v1", "act")]
              + [(f"kT0{n}", "act") for n in range(KU)] + [("q0", "dve")]
              + [(f"kT1{n}", "act") for n in range(KU)] + [("q1", "dve")]
              + [(f"qT{t}{n}", "act") for t in range(TILES) for n in range(QU)])
    FIN = ([(f"h{n}", "dve") for n in range(4)] + ([("hT0", "act"), ("hT1", "act")] if cross else [])
           + [("out0", "dve"), ("neg", "dve"), ("out1", "dve")])
    pad = lambda u: ([("spare", "act")] if len(u) % 2 else [])
    first = A_USES + [("neg", "dve")]
    first = pad(first) + first
    each = A_USES + FIN
    each = pad(each) + each
    uses = Uses(first, each)

    with c:
        s = {n: c.enter_context(nc.semaphore(f"{n}_{tag}")) for n in (
            "wq_loaded", "wk_loaded", "wv_loaded", "wo_loaded", "bias_loaded", "consts_ready", "xs_ready",
            "ctx_loaded", "ctx_used", "prep_ready", "prep_act", "prep_dve", "split",
            "scores_ready", "scores_read", "neg_ready", "scoresT_ready", "exp_ready", "values_ready",
            "heads_ready", "heads_copied", "x_ready", "out_read", "rot_ready")}
        block = c.enter_context(nc.Block())

        def nxt(batch):
            return 0 if batch is None else batch + 1

        @block.sync
        def _(sp):
            sp.dma_start(wk[:, :, :], wk_dram.rearrange("(c p) n -> p c n", p=P)).then_inc(s["wk_loaded"], 16)
            sp.dma_start(wq[:, :, :], wq_dram.rearrange("(c p) n -> p c n", p=P)).then_inc(s["wq_loaded"], 16)
            sp.dma_start(wv[:, :, :], wv_dram.rearrange("(c p) n -> p c n", p=P)).then_inc(s["wv_loaded"], 16)
            if cross:
                sp.dma_start(ctx_sb[:, :, :], ctx_dram[0, :, :].rearrange("(t p) d -> p t d", p=P))\
                  .then_inc(s["ctx_loaded"], 16)
            sp.dma_start(wo[:, :, :], wo_dram.rearrange("(c p) n -> p c n", p=P)).then_inc(s["wo_loaded"], 16)
            if cross:
                sp.dma_start(bout[:, :], bias_dram.partition_broadcast(P)).then_inc(s["bias_loaded"], 16)
                with sp.Fori(1, BATCH) as it:
                    sp.wait_ge(s["ctx_used"], it)
                    sp.dma_start(ctx_sb[:, :, :], ctx_dram[bass.ds(it, 1), :, :].rearrange("b (t p) d -> p (b t) d", p=P))\
                      .then_inc(s["ctx_loaded"], 16)
                sp.wait_ge(s["ctx_used"], BATCH)
                sp.dma_start(ctx_sb[:, :, :], ctx_dram[0, :, :].rearrange("(t p) d -> p t d", p=P))\
                  .then_inc(s["ctx_loaded"], 16)
            sp.wait_ge(s["x_ready"], BATCH)

        AFTER = [n for n, _ in A_USES if n not in ("xT0", "xT1", "ctxT")]
        S_AT = 18

        def at_step(h):
            if h == 0:
                return (["spare"] if pad(A_USES + FIN) else []) + ["xT0", "xT1"] + (["ctxT"] if cross else [])
            n = len(AFTER)
            return AFTER[(h - 1) * n // (S_AT - 1):h * n // (S_AT - 1)] if h < S_AT else []

        def score_step(h):
            return [] if h < S_AT else [2 * (h - S_AT), 2 * (h - S_AT) + 1]

        @block.tensor
        def _(pe):
            def claim(name, batch):
                free = uses.before(name, batch)
                if free:
                    pe.wait_ge(s[f"prep_{free[0]}"], free[1])
                return prep[uses.place(name, batch)[0]]

            def read(name, batch):
                _, _, engine, n = uses.place(name, batch)
                pe.wait_ge(s[f"prep_{engine}"], n)

            def prepare(name, batch, par):
                n = nxt(batch)
                b = claim(name, batch)
                if name == "spare":
                    last = pe.transpose(b[:, 0:P], chip.ident, chip.ident)
                elif name in ("xT0", "xT1"):
                    if name == "xT0":
                        pe.wait_ge(s["xs_ready"], n + 1)
                    j = int(name[2])
                    for i in range(4):
                        cc, t = 2 * j + i // 2, i % 2
                        last = pe.transpose(b[:, P * i:P * i + P], chip.xs[:, t, cc * P:(cc + 1) * P], chip.ident)
                elif name == "ctxT":
                    pe.wait_ge(s["ctx_loaded"], 16 * (n + 1))
                    for i in range(4):
                        cc, t = i // 2, i % 2
                        last = pe.transpose(b[:, P * i:P * i + P], ctx_sb[:, t, cc * P:(cc + 1) * P], chip.ident)
                    pe.drain().then_inc(s["ctx_used"], 1)
                elif name[0] in "qkv" and name[1] != "T":
                    t = int(name[1])
                    if name == "k0":
                        read("xT1", batch)
                        if cross:
                            read("ctxT", batch)
                        if batch is None:
                            pe.wait_ge(s["wk_loaded"], 16)
                            pe.wait_ge(s["wv_loaded"], 16)
                            pe.wait_ge(s["wq_loaded"], 16)
                    w, src, chunks = {"q": (wq, chip.xT, DC), "k": (wk, kv_src, KC), "v": (wv, kv_src, KC)}[name[0]]
                    width = DIM if name[0] == "q" else KW
                    for cc in range(chunks):
                        last = pe.matmul(b[:, 0:width], src[:, cc, t * P:(t + 1) * P], w[:, cc, :],
                                         start=(cc == 0), stop=(cc == chunks - 1))
                elif name[0:2] in ("qT", "kT"):
                    k = name[0] == "k"
                    t, n4 = int(name[2]), int(name[3])
                    pe.wait_ge(s["split"], 4 * n + (0 if k else 2) + t + 1)
                    flat_parts = parts[:, t, :, :].rearrange("p h w -> p (h w)")
                    for i in range(4):
                        blk = 4 * n4 + i
                        last = pe.transpose(b[:, P * i:P * (i + 1)], flat_parts[:, P * blk:P * (blk + 1)], chip.ident)
                elif name == "neg":
                    pe.wait_ge(s["neg_ready"], n + 1)
                    for t in range(TILES):
                        last = pe.transpose(b[:, t * P:(t + 1) * P],
                                            neg_hl[:, t, :, :, :].rearrange("p a b h -> p (a b h)"), chip.ident)
                last.then_inc(s["prep_ready"], 1)

            def first_scores(h, batch, par):
                n = nxt(batch)
                if h == 0:
                    read(f"qT1{QU - 1}", batch)
                if h >= 2:
                    pe.wait_ge(s["scores_read"], n * NH + h - 1)
                r = 64 * (h % 2)
                kb = h // 2 if cross else h // 4
                for t in range(TILES):
                    last = pe.matmul(score[h % 2][:, t * SEQ:(t + 1) * SEQ], qT[r:r + 64, par, h // 2, t * P:(t + 1) * P],
                                     kT[r:r + 64, par, kb, :], start=True, stop=True)
                last.then_inc(s["scores_ready"], 1)

            def second_scores(h, batch, par):
                if h == 0:
                    pe.wait_ge(s["prep_dve"], uses.count(uses.first, "dve") + batch * uses.count(uses.each, "dve") - 1)
                if h >= 2:
                    pe.wait_ge(s["exp_ready"], batch * NH + h - 1)
                r = 64 * (h % 2)
                kb = h // 2 if cross else h // 4
                b = scoreT[h % 2]
                for k in range(TILES):
                    dst = b[:, k * SEQ:(k + 1) * SEQ]
                    pe.matmul(dst, kT[r:r + 64, par, kb, k * P:(k + 1) * P], qT[r:r + 64, par, h // 2, :],
                              start=True, stop=False, skip_group_check=True)
                    last = pe.matmul(dst, select[r:r + 64, h:h + 1].to_broadcast([64, P]), negT[r:r + 64, par, :],
                                     start=False, stop=cross, skip_group_check=True)
                    if not cross:
                        last = pe.matmul(b[:, k * SEQ + k * P:k * SEQ + (k + 1) * P], ident16[:, :], hide16[:, :],
                                         start=False, stop=True, skip_group_check=True)
                last.then_inc(s["scoresT_ready"], 1)

            def values(h, batch, par):
                pe.wait_ge(s["exp_ready"], batch * NH + h + 1)
                if h % 8 == 0 and h >= 16:
                    pe.wait_ge(s["heads_copied"], batch * 4 + h // 8 - 1)
                r = VW * (h % 4)
                b = hbank[h // 8 % 2]
                col = h // 4 % 2 * SEQ
                kh = h if cross else h // 4
                for k in range(TILES):
                    q0 = 0 if cross else k * P
                    last = pe.matmul(b[r:r + VW, col + q0:col + SEQ], v[:, par, k, kh, :],
                                     probsT[:, h % PTS, k * SEQ + q0:(k + 1) * SEQ],
                                     start=(k == 0), stop=(k == TILES - 1), skip_group_check=True)
                last.then_inc(s["values_ready"], 1)
                if h % 8 == 7:
                    pe.drain().then_inc(s["heads_ready"], 1)

            def finish(name, batch):
                if name == "h0":
                    pe.wait_ge(s["heads_copied"], batch * 4 + 4)
                b = claim(name, batch)
                n = int(name[-1])
                if name[:-1] == "h":
                    t = n // 2
                    for i in range(4):
                        last = pe.transpose(b[:, P * i:P * (i + 1)], heads[:, 4 * (n % 2) + i, t * P:(t + 1) * P], chip.ident)
                elif name[:-1] == "hT":
                    read("h3", batch)
                    for i in range(4):
                        cc, t = 2 * n + i // 2, i % 2
                        last = pe.transpose(b[:, P * i:P * (i + 1)], heads_n[:, t, cc * P:(cc + 1) * P], chip.ident)
                else:
                    read("hT1" if cross else "h3", batch)
                    for i in range(DC):
                        if cross:
                            a = headsT[:, i, n * P:(n + 1) * P]
                        else:
                            a = heads_n[:, i % 2, 2 * n * P + i // 2:2 * (n + 1) * P:2]
                        last = pe.matmul(b[:, :], a, wo[:, i, :], start=(i == 0), stop=(i == DC - 1))
                last.then_inc(s["prep_ready"], 1)

            pe.wait_ge(s["consts_ready"], 1)
            for name, _ in uses.first[:-1]:
                prepare(name, None, 0)
            for h in range(NH):
                first_scores(h, None, 0)
            prepare("neg", None, 0)
            read("neg", None)
            pe.wait_ge(s["wo_loaded"], 16)
            with pe.Fori(0, BATCH // 2) as pair:
                for par in range(2):
                    batch = pair * 2 + par
                    for h in range(NH):
                        second_scores(h, batch, par)
                        for name in at_step(h):
                            prepare(name, batch, 1 - par)
                        for hh in score_step(h):
                            first_scores(hh, batch, 1 - par)
                        if h >= 1:
                            values(h - 1, batch, par)
                    values(NH - 1, batch, par)
                    left = range(2 * (NH - S_AT), NH)
                    finish("h0", batch)
                    finish("h1", batch)
                    first_scores(left[0], batch, 1 - par)
                    finish("h2", batch)
                    finish("h3", batch)
                    for hh in left[1:3]:
                        first_scores(hh, batch, 1 - par)
                    if cross:
                        finish("hT0", batch)
                        finish("hT1", batch)
                    for hh in left[3:]:
                        first_scores(hh, batch, 1 - par)
                    finish("out0", batch)
                    prepare("neg", batch, 1 - par)
                    finish("out1", batch)

        @block.scalar
        def _(act):
            copy = lambda dst, src: act.activation(dst, src, ACT.Copy)
            flat = lambda a: a.rearrange("p a b -> p (a b)")

            def take(name, batch):
                bank, ready, _, _ = uses.place(name, batch)
                act.wait_ge(s["prep_ready"], ready)
                return prep[bank]

            def prepare(name, batch, par):
                n = nxt(batch)
                b = take(name, batch)
                if name == "spare":
                    last = copy(scratch[:, 0:P], b[:, 0:P])
                elif name in ("xT0", "xT1"):
                    j = int(name[2])
                    last = copy(flat(chip.xT[:, 2 * j:2 * j + 2, :]), b[:, :])
                elif name == "ctxT":
                    last = copy(flat(ctxT[:, :, :]), b[:, :])
                elif name in ("v0", "v1"):
                    last = copy(v[:, par, int(name[1]), :, 0:HW], b[:, 0:KW].rearrange("p (h w) -> p h w", w=HW))
                else:
                    t, n = int(name[2]), int(name[3])
                    dst = (kT if name[0] == "k" else qT)[:, par, 4 * n:4 * n + 4, t * P:(t + 1) * P]
                    last = copy(dst, b[:, :].rearrange("p (g q) -> p g q", g=4))
                last.then_inc(s["prep_act"], 1)

            def is_act(name):
                return dict(uses.each + uses.first)[name] == "act"

            copy(chip.xs[:, :, :], chip.x[:, 0:TILES, :]).then_inc(s["xs_ready"], 1)
            act.wait_ge(s["consts_ready"], 1)
            for name, e in uses.first:
                if e == "act":
                    prepare(name, None, 0)
            with act.Fori(0, BATCH // 2) as pair:
                for par in range(2):
                    batch = pair * 2 + par

                    def stage_next():
                        copy(chip.xs[:, :, :], chip.x[:, bass.ds(batch * TILES + TILES, TILES), :])\
                            .then_inc(s["xs_ready"], 1)

                    if not cross:
                        stage_next()
                    for h in range(NH):
                        act.wait_ge(s["scoresT_ready"], batch * NH + h + 1)
                        if h >= PTS:
                            act.wait_ge(s["values_ready"], batch * NH + h - PTS + 1)
                        act.activation(probsT[:, h % PTS, :], scoreT[h % 2][:, :], ACT.Exp, scale=SCALE)\
                           .then_inc(s["exp_ready"], 1)
                        if cross and h == 0:
                            stage_next()
                        for name in at_step(h):
                            if is_act(name):
                                prepare(name, batch, 1 - par)
                        if h % 8 == 1 and h > 1:
                            g = h // 8 - 1
                            act.wait_ge(s["heads_ready"], batch * 4 + g + 1)
                            copy(flat(heads[:, 2 * g:2 * g + 2, :]), hbank[g % 2][:, :]).then_inc(s["heads_copied"], 1)
                    act.wait_ge(s["heads_ready"], batch * 4 + 4)
                    copy(flat(heads[:, 6:8, :]), hbank[1][:, :]).then_inc(s["heads_copied"], 1)
                    if cross:
                        for n in range(2):
                            b = take(f"hT{n}", batch)
                            copy(flat(headsT[:, 2 * n:2 * n + 2, :]), b[:, :]).then_inc(s["prep_act"], 1)

        @block.vector
        def _(dve):
            def take(name, batch):
                bank, ready, _, _ = uses.place(name, batch)
                dve.wait_ge(s["prep_ready"], ready)
                return prep[bank]

            def rotate(name, batch, par):
                t = int(name[1])
                q = name[0] == "q"
                if q:
                    dve.wait_ge(s["prep_ready"], uses.place(f"kT{t}{KU - 1}", batch)[1])
                heads_ = NH if q else KVH
                width = heads_ * HW
                b = take(name, batch)[:, 0:width].rearrange("p (h w) -> p h w", w=HW)
                if cross:
                    cos, sin = cos_now[:, t, :], sin_now[:, t, :]
                else:
                    cos = chip.const[:, C_COS + HW * t:C_COS + HW * (t + 1)]
                    sin = chip.const[:, C_SIN + HW * t:C_SIN + HW * (t + 1)]
                wide = lambda a, n: a.unsqueeze(1).to_broadcast([P, heads_, n])
                r = rot[:, 0:width].rearrange("p (h w) -> p h w", w=HW)
                u = turn[:, 0:width].rearrange("p (h w) -> p h w", w=HW)
                dve.tensor_tensor(r, b, wide(cos, HW), ALU.mult)
                for i in range(2):
                    mine, other = ((slice(i, HW, 2), slice(1 - i, HW, 2)) if cross else
                                   (slice(8 * i, 8 * i + 8), slice(8 - 8 * i, 16 - 8 * i)))
                    last = dve.tensor_tensor(u[:, :, mine], b[:, :, other], wide(sin[:, mine], 8), ALU.mult)
                last.then_inc(s["prep_dve"], 1)
                dve.drain()
                dve.tensor_tensor(r, r, u, ALU.add)
                dve.drain()
                flat_parts = parts[:, t, :, :].rearrange("p h w -> p (h w)")
                if q:
                    d = parts[:, t, :, :].rearrange("p h (r l w) -> p l h r w", r=2, l=2)
                    hi, lo = [d[:, 0]], [d[:, 1]]
                elif cross:
                    d = parts[:, t, :, :].rearrange("p h (l r w) -> p l h r w", r=2, l=2)
                    hi, lo = [d[:, 0]], [d[:, 1]]
                else:
                    d = flat_parts[:, 0:KVH * P].rearrange("p (h c l r w) -> p l c h r w", c=2, r=2, l=2, w=HW)
                    hi, lo = [d[:, 0, 0], d[:, 0, 1]], [d[:, 1, 0], d[:, 1, 1]]
                twice = lambda a: a.unsqueeze(2).to_broadcast([P, heads_, 2, HW])
                for o in hi:
                    dve.tensor_copy(o.bitcast(FP32R), twice(r))
                dve.drain()
                for o in lo:
                    last = dve.tensor_tensor(o, twice(r), hi[0], ALU.subtract)
                last.then_inc(s["split"], 1)
                dve.drain()

            def prepare(name, batch, par):
                n = nxt(batch)
                if name == "k0" and cross:
                    first_tile = (batch + 1) * TILES if batch is not None else 0
                    dve.tensor_copy(cos_now[:, :, :], rotary.cos[:, bass.ds(first_tile, TILES), :])
                    dve.tensor_copy(sin_now[:, :, :], rotary.sin[:, bass.ds(first_tile, TILES), :])
                    dve.drain()
                if name[0] in "qk":
                    rotate(name, batch, par)
                else:
                    b = take(name, batch)
                    dve.tensor_copy(negT[:, par, :], b[:, 0:SEQ]).then_inc(s["prep_dve"], 1)

            def maxima(h, batch):
                n = nxt(batch)
                dve.wait_ge(s["scores_ready"], n * NH + h + 1)
                b = score[h % 2]
                if cross:
                    dve.tensor_reduce(mx[:, :, h], b[:, :].rearrange("p (t k) -> p t k", t=TILES), AX.X, ALU.max)\
                       .then_inc(s["scores_read"], 1)
                else:
                    dve.memset(tick[:, :], 0.0)
                    for t in range(TILES):
                        nk = (t + 1) * P
                        at_ = C_OWN if t == 0 else C_CAUSAL
                        dve.tensor_tensor_reduce(out=scratch2[t][:, 0:nk], in0=b[:, t * SEQ:t * SEQ + nk],
                                                 in1=chip.const[:, at_:at_ + nk], scale=1.0, scalar=FLOOR,
                                                 op0=ALU.add, op1=ALU.max, accum_out=mx[:, t, h:h + 1])
                    dve.drain().then_inc(s["scores_read"], 1)

            def negate():
                dve.drain()
                hi, lo = neg_hl[:, :, :, 0, :], neg_hl[:, :, :, 1, :]
                twice = mx[:, :, :].unsqueeze(2).to_broadcast([P, TILES, 2, NH])
                dve.tensor_scalar(mx[:, :, :], mx[:, :, :], -1.0, None, ALU.mult)
                dve.drain()
                dve.tensor_copy(hi.bitcast(FP32R), twice)
                dve.drain()
                dve.tensor_tensor(lo, twice, hi, ALU.subtract)
                dve.drain().then_inc(s["neg_ready"], 1)

            def is_dve(name):
                return dict(uses.each + uses.first)[name] == "dve"

            scratch2 = [rot, turn]
            dve.memset(v[:, :, :, :, :].rearrange("p a t h w -> p (a t h) w")[:, :, HW:HW + 1], 1.0)
            dve.memset(v[:, :, :, :, :].rearrange("p a t h w -> p (a t h) w")[:, :, HW + 1:], 0.0)
            for r in (0, 64):
                for i in (0, NH):
                    dve.tensor_copy(select[r + i:r + i + NH, :], chip.const[r + i:r + i + NH, C_ID + r + i:C_ID + r + i + NH])
            if not cross:
                dve.tensor_copy(ident16[:, :], chip.ident)
                dve.tensor_copy(hide16[:, :], chip.const[:, C_OWN_T:C_OWN_T + P])
            dve.drain().then_inc(s["consts_ready"], 1)
            for name, e in uses.first[:-1]:
                if e == "dve":
                    prepare(name, None, 0)
            for h in range(NH):
                maxima(h, None)
            negate()
            prepare("neg", None, 0)
            if cross:
                dve.wait_ge(s["bias_loaded"], 16)
            with dve.Fori(0, BATCH // 2) as pair:
                for par in range(2):
                    batch = pair * 2 + par
                    for h in range(NH):
                        for name in at_step(h):
                            if is_dve(name):
                                prepare(name, batch, 1 - par)
                        for hh in score_step(h):
                            maxima(hh, batch)
                    left = range(2 * (NH - S_AT), NH)

                    def normalise(n):
                        b = take(f"h{n}", batch)[:, :].rearrange("p (h w) -> p h w", w=VW)
                        dve.reciprocal(rden[:, :], b[:, :, HW])
                        dve.drain()
                        t = n // 2
                        dst = heads_n[:, t, 256 * (n % 2):256 * (n % 2) + 256].rearrange("p (h w) -> p h w", w=HW)
                        dve.tensor_tensor(dst, b[:, :, 0:HW], rden[:, :].unsqueeze(2).to_broadcast([P, NH // 2, HW]),
                                          ALU.mult).then_inc(s["prep_dve"], 1)
                        dve.drain()

                    normalise(0)
                    normalise(1)
                    maxima(left[0], batch)
                    normalise(2)
                    normalise(3)
                    for hh in left[1:]:
                        maxima(hh, batch)
                    negate()
                    for t in range(TILES):
                        b = take(f"out{t}", batch)
                        dve.tensor_tensor(chip.res[:, t, :], b[:, :], chip.x[:, bass.ds(batch * TILES + t, 1), :],
                                          ALU.add).then_inc(s["prep_dve"], 1)
                        if t == 0:
                            prepare("neg", batch, 1 - par)
                    dve.drain()
                    if cross:
                        dve.tensor_tensor(chip.res[:, :, :], chip.res[:, :, :],
                                          bout[:, :].unsqueeze(1).to_broadcast([P, TILES, DIM]), ALU.add)
                        dve.drain()
                    ln_rows(dve, chip, batch, s)

INTER = 2048
MC = INTER // P
BLOCK = 2
NBLOCK = MC // BLOCK
GROUP = 512
NGROUP = NTILE * P // GROUP
GT = GROUP // P


def hadamard_inputs(nc, chip, y_hi, y_lo, down, sign_up_dram, down_dram, scale_down_dram):
    with ExitStack() as c:
        sb = lambda name, shape: c.enter_context(nc.sbuf_tensor(name, shape, FP32))
        rows = sb("down_rows", [P, DC, INTER])
        sign, scale = sb("sign_up", [P, DC]), sb("scale_down", [P, DC])
        half, folded = sb("half_turned", [P, DC, SEQ]), sb("folded", [P, DC, SEQ])
        chip.sequence_buffers(c, "h")
        xs, xT = chip.xs, chip.xT
        s = {n: c.enter_context(nc.semaphore(f"{n}_h")) for n in (
            "small_loaded", "scaled", "ready", "copied", "folded", "xs_ready", "hi_ready", "lo_ready",
            "xT_ready", "xT_copied", "down_ready", "down_copied", "h_ready", "h_copied", "pair_read", "y_ready")}
        rows_loaded = [c.enter_context(nc.semaphore(f"rows_loaded{o}_h")) for o in range(DC)]
        turn, had, xbank, ybank = chip.bank[0:2], chip.bank[2:4], chip.bank[4:6], chip.bank[6:8]
        h128 = chip.const[:, C_HAD:C_HAD + P]
        block = c.enter_context(nc.Block())

        @block.sync
        def _(sp):
            with nc.allow_non_contiguous_dma(reason="512 signs and scales onto the partitions"):
                sp.dma_start(sign[:, :], sign_up_dram.rearrange("(c p) -> p c", p=P)).then_inc(s["small_loaded"], 16)
                sp.dma_start(scale[:, :], scale_down_dram.rearrange("(c p) -> p c", p=P)).then_inc(s["small_loaded"], 16)
            for o in range(DC):
                sp.dma_start(rows[:, o, :], down_dram[o * P:(o + 1) * P, :]).then_inc(rows_loaded[o], 16)

        @block.tensor
        def _(pe):
            for b in range(BATCH + 1):
                chunks = (2 * b, 2 * b + 1) if b < BATCH else ()
                if b < BATCH:
                    pe.wait_ge(s["xs_ready"], b + 1)
                    for j in range(2):
                        if b >= 1:
                            pe.wait_ge(s["xT_copied"], 2 * b - 1 + j)
                        for i in range(4):
                            cc, t = 2 * j + i // 2, i % 2
                            last = pe.transpose(xbank[j][:, P * i:P * i + P], xs[:, t, cc * P:(cc + 1) * P], chip.ident)
                        last.then_inc(s["xT_ready"], 1)
                if b == 0:
                    pe.wait_ge(s["scaled"], DC)
                for m in chunks:
                    if m >= 2:
                        pe.wait_ge(s["down_copied"], m - 1)
                    for o in range(DC):
                        last = pe.transpose(turn[m % 2][:, P * o:P * (o + 1)], rows[:, o, m * P:(m + 1) * P], chip.ident)
                    last.then_inc(s["down_ready"], 1)
                if b >= 1:
                    pe.wait_ge(s["folded"], b)
                    for j in range(2):
                        if b >= 2:
                            pe.wait_ge(s["lo_ready"], 2 * b - 3 + j)
                        for i in range(2):
                            last = pe.matmul(ybank[j][:, i * SEQ:(i + 1) * SEQ], h128, folded[:, 2 * j + i, :],
                                             start=True, stop=True)
                        last.then_inc(s["y_ready"], 1)
                if b >= 1 and chunks:
                    pe.wait_ge(s["pair_read"], b)
                for m in chunks:
                    pe.wait_ge(s["down_copied"], m + 1)
                    pe.matmul(had[m % 2][:, :], h128, down[:, m, :], start=True, stop=True).then_inc(s["h_ready"], 1)

        @block.scalar
        def _(act):
            copy = lambda dst, src, **k: act.activation(dst, src, ACT.Copy, **k)
            copy(xs[:, :, :], chip.x[:, 0:TILES, :]).then_inc(s["xs_ready"], 1)
            act.wait_ge(s["small_loaded"], 32)
            for b in range(BATCH + 1):
                if b < BATCH:
                    if b >= 1:
                        act.wait_ge(s["folded"], b)
                    for j in range(2):
                        act.wait_ge(s["xT_ready"], 2 * b + j + 1)
                        for i in range(2):
                            cc = 2 * j + i
                            last = copy(half[:, cc, :], xbank[j][:, i * SEQ:(i + 1) * SEQ], scale=sign[:, cc:cc + 1])
                        last.then_inc(s["xT_copied"], 1)
                if b + 1 < BATCH:
                    copy(xs[:, :, :], chip.x[:, (b + 1) * TILES:(b + 2) * TILES, :]).then_inc(s["xs_ready"], 1)
                if b == 0:
                    for o in range(DC):
                        act.wait_ge(rows_loaded[o], 16)
                        copy(rows[:, o, :], rows[:, o, :], scale=scale[:, o:o + 1]).then_inc(s["scaled"], 1)
                for m in (2 * b, 2 * b + 1) if b < BATCH else ():
                    act.wait_ge(s["down_ready"], m + 1)
                    copy(down[:, m, :], turn[m % 2][:, :]).then_inc(s["down_copied"], 1)
                if b >= 1:
                    for j in range(2):
                        act.wait_ge(s["y_ready"], 2 * b + j - 1)
                        copy(y_hi[:, 2 * j:2 * j + 2, (b - 1) * SEQ:b * SEQ],
                             ybank[j][:, :].rearrange("p (c q) -> p c q", c=2), scale=float(DIM ** -0.5))\
                            .then_inc(s["hi_ready"], 1)
                if b < BATCH:
                    act.wait_ge(s["h_ready"], 2 * b + 1)
                    copy(down[:, 2 * b, :], had[0][:, :]).then_inc(s["h_copied"], 1)

        @block.vector
        def _(dve):
            def fold(dst, src, two):
                src, dst = src.rearrange(two, two=2), dst.rearrange(two, two=2)
                dve.tensor_tensor(dst[:, 0], src[:, 0], src[:, 1], ALU.add)
                return dve.tensor_tensor(dst[:, 1], src[:, 0], src[:, 1], ALU.subtract)

            by_chunk = down[:, :, :].rearrange("p m (o q) -> p m o q", q=P)
            by_row = rows[:, :, :].rearrange("p o (m q) -> p m o q", q=P)

            def butterfly(dst, src, first, w):
                lo, hi = src[:, first:first + w], src[:, first + w:first + 2 * w]
                dve.tensor_tensor(dst[:, first:first + w], lo, hi, ALU.add)
                dve.tensor_tensor(dst[:, first + w:first + 2 * w], lo, hi, ALU.subtract)
                dve.drain()

            for b in range(BATCH + 1):
                if b < BATCH:
                    dve.wait_ge(s["xT_copied"], 2 * b + 2)
                    fold(xT[:, :, :], half[:, :, :], "p (a two) q -> p two a q")
                    dve.drain()
                    if b >= 1:
                        dve.wait_ge(s["y_ready"], 2 * b)
                    fold(folded[:, :, :], xT[:, :, :], "p (two a) q -> p two a q")
                    dve.drain().then_inc(s["folded"], 1)
                if b >= 1:
                    for j in range(2):
                        dve.wait_ge(s["hi_ready"], 2 * b + j - 1)
                        dve.scalar_tensor_tensor(
                            y_lo[:, 2 * j:2 * j + 2, (b - 1) * SEQ:b * SEQ],
                            ybank[j][:, :].rearrange("p (c q) -> p c q", c=2), float(DIM ** -0.5),
                            y_hi[:, 2 * j:2 * j + 2, (b - 1) * SEQ:b * SEQ].bitcast(FP32), ALU.mult, ALU.subtract)\
                            .then_inc(s["lo_ready"], 1)
                if b < BATCH:
                    m = 2 * b
                    dve.wait_ge(s["h_ready"], m + 2)
                    dve.wait_ge(s["h_copied"], b + 1)
                    h1 = had[1][:, :].rearrange("p (o q) -> p o q", q=P)
                    dve.tensor_tensor(by_chunk[:, m + 1], by_chunk[:, m], h1, ALU.subtract)
                    dve.tensor_tensor(by_chunk[:, m], by_chunk[:, m], h1, ALU.add)
                    dve.drain().then_inc(s["pair_read"], 1)
                    if m % 4 == 2:
                        butterfly(by_row, by_chunk, m - 2, 2)
                    if m % 8 == 6:
                        butterfly(by_chunk, by_row, m - 6, 4)


def hadamard_ffn(nc, chip, sign_up_dram, sign_down_dram, scale_up_dram, scale_down_dram,
                 up_dram, gate_dram, down_dram):
    with ExitStack() as c:
        sb = lambda name, shape, dt=FP32: c.enter_context(nc.sbuf_tensor(name, shape, dt))
        y_hi, y_lo = sb("y_hi", [P, DC, NTILE * P], FP32R), sb("y_lo", [P, DC, NTILE * P], FP32R)
        down = sb("down", [P, MC, DIM])
        hadamard_inputs(nc, chip, y_hi, y_lo, down, sign_up_dram, down_dram, scale_down_dram)

        rows = sb("ug_rows", [P, BLOCK, 2, DIM])
        w_hi, w_lo = (sb(n, [P, 2, DC, 2 * BLOCK, P], FP32R) for n in ("ug_hi", "ug_lo"))
        d_hi, d_lo = (sb(n, [P, BLOCK, DIM], FP32R) for n in ("down_hi", "down_lo"))
        scale_ug, sign_down = sb("scale_ug", [P, 2, MC]), sb("sign_down", [P, MC])
        scale_now, sign_now = sb("scale_now", [P, 2, BLOCK]), sb("sign_now", [P, BLOCK])
        silu, h = sb("silu", [P, GROUP]), sb("h", [P, GROUP])
        h_hi, h_lo = (sb(n, [P, 2, BLOCK, GROUP], FP32R) for n in ("h_hi", "h_lo"))
        s = {n: c.enter_context(nc.semaphore(f"{n}_f")) for n in (
            "small_loaded", "rows_loaded", "rows_used", "scales_ready", "turned", "hi_ready", "lo_ready",
            "gate_ready", "up_ready", "silu_ready", "h_ready", "h_hi_ready", "h_lo_ready", "d_hi_ready",
            "d_lo_ready", "down_ready", "added")}
        turn, gate, up, dbank = chip.bank[0:2], chip.bank[2:4], chip.bank[4:6], chip.bank[6:8]
        block = c.enter_context(nc.Block())
        NA = NGROUP * BLOCK
        ND = NGROUP * GT

        @block.sync
        def _(sp):
            with nc.allow_non_contiguous_dma(reason="scales and signs onto the partitions"):
                sp.dma_start(scale_ug[:, :, :], scale_up_dram.rearrange("(k c p) -> p k c", p=P, k=2))\
                  .then_inc(s["small_loaded"], 16)
                sp.dma_start(sign_down[:, :], sign_down_dram.rearrange("(c p) -> p c", p=P)).then_inc(s["small_loaded"], 16)

            def load(blk):
                for kind, w in enumerate((gate_dram, up_dram)):
                    src = w[bass.ds(blk * (BLOCK * P), BLOCK * P), :].rearrange("(c p) n -> p c n", p=P)
                    sp.dma_start(rows[:, :, kind, :], src).then_inc(s["rows_loaded"], 16)

            load(0)
            with sp.Fori(1, NBLOCK) as blk:
                sp.wait_ge(s["rows_loaded"], 32 * blk)
                sp.wait_ge(s["rows_used"], blk)
                load(blk)
            sp.wait_ge(s["rows_loaded"], 32 * NBLOCK)
            sp.wait_ge(s["rows_used"], NBLOCK)
            load(0)
            sp.wait_ge(s["rows_loaded"], 32 * (NBLOCK + 1))

        @block.tensor
        def _(pe):
            def turn_weights(blk, par, n):
                if n == 0:
                    pe.wait_ge(s["rows_loaded"], 32 * blk + 32)
                if not (isinstance(blk, int) and n < 2):
                    pe.wait_ge(s["lo_ready"], 2 * BLOCK * blk + n - 1)
                for cc in range(DC):
                    last = pe.transpose(turn[n % 2][:, P * cc:P * (cc + 1)],
                                        rows[:, n // 2, n % 2, cc * P:(cc + 1) * P], chip.ident)
                last.then_inc(s["turned"], 1)
                if n == 2 * BLOCK - 1:
                    pe.drain().then_inc(s["rows_used"], 1)

            def gate_up(blk, par, g):
                for m in range(BLOCK):
                    a = g * BLOCK + m
                    for kind, banks, read in ((0, gate, "silu_ready"), (1, up, "h_ready")):
                        if a >= 2:
                            pe.wait_ge(s[read], blk * NA + a - 1)
                        n = 0
                        for w, y in ((w_hi, y_hi), (w_hi, y_lo), (w_lo, y_hi)):
                            for cc in range(DC):
                                last = pe.matmul(banks[m][:, :], w[:, par, cc, 2 * m + kind, :],
                                                 y[:, cc, g * GROUP:(g + 1) * GROUP], start=(n == 0), stop=(n == 11))
                                n += 1
                        last.then_inc(s["up_ready" if kind else "gate_ready"], 1)

            def down_product(blk, par, g):
                pe.wait_ge(s["h_lo_ready"], blk * NA + (g + 1) * BLOCK)
                for t in range(GT):
                    d = g * GT + t
                    pe.wait_ge(s["added"], blk * ND + d + 1)
                    n = 0
                    for hh, dd in ((h_hi, d_hi), (h_hi, d_lo), (h_lo, d_hi)):
                        for m in range(BLOCK):
                            last = pe.matmul(dbank[d % 2][:, :], hh[:, g % 2, m, t * P:(t + 1) * P], dd[:, m, :],
                                             start=(n == 0), stop=(n == 5))
                            n += 1
                    last.then_inc(s["down_ready"], 1)

            for n in range(2 * BLOCK):
                turn_weights(0, 0, n)
            with pe.Fori(0, NBLOCK // 2) as i:
                for par in range(2):
                    blk = 2 * i + par
                    for g in range(NGROUP):
                        turn_weights(blk + 1, 1 - par, g)
                        if g == 0:
                            pe.wait_ge(s["lo_ready"], 2 * BLOCK * blk + 2 * BLOCK)
                        gate_up(blk, par, g)
                        if g == 1:
                            pe.wait_ge(s["d_lo_ready"], blk + 1)
                        if g >= 1:
                            down_product(blk, par, g - 1)
                    down_product(blk, par, NGROUP - 1)

        @block.scalar
        def _(act):
            def split_weights(blk, par, n):
                act.wait_ge(s["turned"], 2 * BLOCK * blk + n + 1)
                act.activation(w_hi[:, par, :, n, :], turn[n % 2][:, :].rearrange("p (c n) -> p c n", c=DC), ACT.Copy)\
                   .then_inc(s["hi_ready"], 1)

            for n in range(2 * BLOCK):
                split_weights(0, 0, n)
            with act.Fori(0, NBLOCK // 2) as i:
                for par in range(2):
                    blk = 2 * i + par
                    for g in range(NGROUP):
                        split_weights(blk + 1, 1 - par, g)
                        if g == 0:
                            act.wait_ge(s["scales_ready"], blk + 1)
                        for m in range(BLOCK):
                            a = g * BLOCK + m
                            act.wait_ge(s["gate_ready"], blk * NA + a + 1)
                            act.activation(silu[:, :], gate[m][:, :], ACT.Silu, scale=scale_now[:, 1, m:m + 1])\
                               .then_inc(s["silu_ready"], 1)
                            act.wait_ge(s["h_ready"], blk * NA + a + 1)
                            act.activation(h_hi[:, g % 2, m, :], h[:, :], ACT.Copy).then_inc(s["h_hi_ready"], 1)

        @block.vector
        def _(dve):
            def split_weights(blk, par, n):
                dve.wait_ge(s["hi_ready"], 2 * BLOCK * blk + n + 1)
                dve.tensor_tensor(w_lo[:, par, :, n, :], turn[n % 2][:, :].rearrange("p (c n) -> p c n", c=DC),
                                  w_hi[:, par, :, n, :].bitcast(FP32), ALU.subtract).then_inc(s["lo_ready"], 1)

            def add_down(blk, g):
                for t in range(GT):
                    d = g * GT + t
                    dve.wait_ge(s["down_ready"], blk * ND + d + 1)
                    dve.tensor_tensor(chip.x[:, d, :], chip.x[:, d, :], dbank[d % 2][:, :], ALU.add)\
                       .then_inc(s["added"], 1)

            dve.drain().then_inc(s["added"], 2)
            dve.wait_ge(s["small_loaded"], 32)
            dve.tensor_scalar(sign_down[:, :], sign_down[:, :], float(INTER ** -0.5), None, ALU.mult)
            dve.drain()
            for n in range(2 * BLOCK):
                split_weights(0, 0, n)

            def pair_of_blocks(i, upper):
                for par in range(2):
                    blk = 2 * i + par
                    dve.tensor_copy(scale_now[:, :, :], scale_ug[:, :, bass.ds(blk * BLOCK, BLOCK)])
                    dve.tensor_copy(sign_now[:, :], sign_down[:, bass.ds(blk * BLOCK, BLOCK)])
                    dve.drain().then_inc(s["scales_ready"], 1)
                    for m in range(BLOCK):
                        rows_m = h[:, :].unsqueeze(1)
                        low = blk * BLOCK + m - (MC // 2 if upper else 0)
                        dve.tensor_tensor(rows_m, down[:, bass.ds(low, 1), :], down[:, bass.ds(low + MC // 2, 1), :],
                                          ALU.subtract if upper else ALU.add)
                        dve.drain()
                        dve.tensor_scalar(d_hi[:, m:m + 1, :], rows_m, sign_now[:, m:m + 1], None, ALU.mult)
                        dve.drain()
                        dve.scalar_tensor_tensor(d_lo[:, m:m + 1, :], rows_m, sign_now[:, m:m + 1],
                                                 d_hi[:, m:m + 1, :].bitcast(FP32), ALU.mult, ALU.subtract)
                        dve.drain()
                    dve.drain().then_inc(s["d_lo_ready"], 1)
                    for g in range(NGROUP):
                        split_weights(blk + 1, 1 - par, g)
                        for m in range(BLOCK):
                            a = g * BLOCK + m
                            dve.wait_ge(s["silu_ready"], blk * NA + a + 1)
                            dve.wait_ge(s["up_ready"], blk * NA + a + 1)
                            dve.scalar_tensor_tensor(h[:, :], up[m][:, :], scale_now[:, 0, m:m + 1], silu[:, :],
                                                     ALU.mult, ALU.mult).then_inc(s["h_ready"], 1)
                            dve.wait_ge(s["h_hi_ready"], blk * NA + a + 1)
                            dve.tensor_tensor(h_lo[:, g % 2, m, :], h[:, :], h_hi[:, g % 2, m, :].bitcast(FP32),
                                              ALU.subtract).then_inc(s["h_lo_ready"], 1)
                            dve.drain()
                        if g >= 1:
                            add_down(blk, g - 1)
                    add_down(blk, NGROUP - 1)

            for upper in (False, True):
                with dve.Fori(NBLOCK // 4 * upper, NBLOCK // 4 * (1 + upper)) as i:
                    pair_of_blocks(i, upper)


def last_norm(nc, chip, out_dram):
    NT = 4
    with ExitStack() as c:
        sb = lambda name, shape: c.enter_context(nc.sbuf_tensor(name, shape, FP32))
        stat, agg = sb("last_stat", [P, NTILE, 6]), sb("last_agg", [P, NTILE, 2])
        var, rstd, newton = sb("last_var", [P, NTILE]), sb("last_rstd", [P, NTILE]), sb("last_newton", [P, NTILE])
        done, stored = c.enter_context(nc.semaphore("rows_done")), c.enter_context(nc.semaphore("rows_stored"))
        block = c.enter_context(nc.Block())

        @block.sync
        def _(sp):
            out = out_dram.rearrange("b (t p) d -> p (b t) d", p=P)
            for i in range(NTILE // NT):
                sp.wait_ge(done, i + 1)
                sp.dma_start(out[:, i * NT:(i + 1) * NT, :], chip.x[:, i * NT:(i + 1) * NT, :]).then_inc(stored, 16)
            sp.wait_ge(stored, 16 * (NTILE // NT))

        @block.vector
        def _(dve):
            for i in range(NTILE // NT):
                r = slice(i * NT, (i + 1) * NT)
                for t in range(i * NT, (i + 1) * NT):
                    dve.bn_stats(stat[:, t, :], chip.x[:, t, :])
                dve.drain()
                for t in range(i * NT, (i + 1) * NT):
                    dve.bn_aggr(agg[:, t, :], stat[:, t, :])
                dve.drain()
                rsqrt(dve, rstd[:, r], agg[:, r, 1], var[:, r], newton[:, r])
                for t in range(i * NT, (i + 1) * NT):
                    last = dve.tensor_scalar(chip.x[:, t, :], chip.x[:, t, :], agg[:, t, 0:1], rstd[:, t:t + 1],
                                             ALU.subtract, ALU.mult)
                last.then_inc(done, 1)

def decoder(nc, x, ctx_1024, fside, mask, const, a0_wq, a0_wk, a0_wv, a0_wo, x0_wq, x0_wk, x0_wv, x0_wo,
            gate_w, ffn_w, atoms, mix, importance, mask_idx, a1_wq, a1_wk, a1_wv, a1_wo,
            x1_wq, x1_wkv, x1_wout, x1_bout, su_ug, su_dp, ws_ug, ws_dp, w_up, w_gate, w_down, out):
    with ExitStack() as ctx:
        chip = Chip(nc, ctx)
        with ExitStack() as c:
            table = ExpertTable(nc, chip, c)
            weights = WideWeights(nc, c, "s", 4, DC)
            start(nc, chip, x, const, table, atoms, mix, importance, mask_idx,
                  lambda sp: weights.load(sp, a0_wq, a0_wk, a0_wv))
            attention_wide(nc, chip, weights, 4, 1 / 128, a0_wo, table=table)
        with ExitStack() as c:
            weights = WideWeights(nc, c, "x", 8, CC)
            attention_wide(nc, chip, weights, 8, float(np.float32(1) / np.sqrt(np.float32(128))),
                           x0_wo, (x0_wq, x0_wk, x0_wv), ctx_1024, mask)
        with ExitStack() as c:
            rotary = RotaryTables(nc, c, fside)
            experts(nc, chip, table, gate_w, ffn_w, rotary)
            attention_narrow(nc, chip, a1_wq, a1_wk, a1_wv, a1_wo)
            attention_narrow(nc, chip, x1_wq, x1_wkv[:, 0:DIM], x1_wkv[:, DIM:], x1_wout, ctx_1024, x1_bout, rotary)
        hadamard_ffn(nc, chip, su_ug, su_dp, ws_ug, ws_dp, w_up, w_gate, w_down)
        last_norm(nc, chip, out)


_INS = ['x', 'ctx_1024', 'fside_BxSx2_0', 'mask_BxS2_bf1', 'const', 'L0_attn_Wq', 'L0_attn_Wk', 'L0_attn_Wv', 'L0_attn_Wo',
        'L0_xattn_Wq', 'L0_xattn_Wk', 'L0_xattn_Wv', 'L0_xattn_Wo', 'L0_ffn_gate_w', 'L0_ffn_W', 'L0_ffn_atoms',
        'L0_ffn_expert_atom_weights', 'L0_ffn_importance', 'L0_ffn_mask_idx', 'L1_attn_Wq', 'L1_attn_Wk', 'L1_attn_Wv',
        'L1_attn_Wo', 'L1_xattn_Wq', 'L1_xattn_Wkv', 'L1_xattn_Wout', 'L1_xattn_bout', 'L1_ffn_SU_ug', 'L1_ffn_SU_dp',
        'L1_ffn_Wscale_ug', 'L1_ffn_Wscale_dp', 'L1_ffn_W_up', 'L1_ffn_W_gate', 'L1_ffn_W_down']


def kernel(**inputs):
    import concourse.bacc as _bacc
    from concourse.bass_utils import run_bass_kernel_spmd as _run

    nc = _bacc.Bacc("TRN2", target_bir_lowering=False, num_devices=1)
    arrays, args = {}, []
    for name in _INS:
        a = constants() if name == 'const' else np.ascontiguousarray(inputs[name])
        arrays[f"in_{name}"] = a
        args.append(nc.dram_tensor(f"in_{name}", a.shape, mybir.dt.from_np(a.dtype), kind="ExternalInput").ap())
    args.append(nc.dram_tensor("out_0", (BATCH, SEQ, DIM), FP32, kind="ExternalOutput").ap())
    decoder(nc, *args)
    r = _run(nc, [arrays], core_ids=[0])
    return r.results[0]["out_0"]
```
